# Optimizing a Trainium2 kernel written in Bass

```python
import numpy as np
import jax
import jax.numpy as jnp

def _softmax(x, axis=-1):
    return jax.nn.softmax(x, axis=axis)

def _gelu(x):
    return jax.nn.gelu(x, approximate=True)

def _silu(x):
    return jax.nn.silu(x)

def _sigmoid(x):
    return jax.nn.sigmoid(x)

def _layernorm(x, axis=-1, eps=1e-05):
    m = jnp.mean(x, axis=axis, keepdims=True)
    v = jnp.var(x, axis=axis, keepdims=True)
    return (x - m) / jnp.sqrt(v + eps)

def _scatter_add(tgt, idx, src, axis=0):
    return tgt.at[idx].add(src)

def _segment_sum(src, seg, n):
    return jax.ops.segment_sum(src, seg, n)
kernel_name = 'mk_xattn_ffn_d2_seqx_r4_4df9c2'

def setup_inputs(seed: int=0):
    np.random.seed(seed)
    _w = jnp.asarray

    def _rec_inputs():
        import jax
        import jax.numpy as jnp
        _rk = jax.random.key(seed)
        x = 0.0002279 + 0.9999 * jax.random.normal(jax.random.fold_in(_rk, 1), (4, 1024, 256), jnp.float32)
        _lenS = 1024 - jax.random.randint(jax.random.fold_in(_rk, 7), (4,), 0, max(1, 1024 // 4) + 1, jnp.int32)
        _lenS2 = 154 - jax.random.randint(jax.random.fold_in(_rk, 8), (4,), 0, max(1, 154 // 4) + 1, jnp.int32)
        _ctx_1024P = jax.random.normal(jax.random.fold_in(_rk, 11), (4, 16, 256), jnp.float32)
        _ctx_1024c = jax.random.dirichlet(jax.random.fold_in(_rk, 511), 0.3 * jnp.ones((16,), jnp.float32), (4, 154))
        _ctx_1024t = jnp.einsum('bsk,bkd->bsd', _ctx_1024c, _ctx_1024P)
        _ctx_1024t = _ctx_1024t * jax.lax.rsqrt(jnp.mean(jnp.square(_ctx_1024t)) + 1e-12) * 0.953939
        ctx_1024 = -0.000125008 + 0.999885 * (_ctx_1024t + 0.3 * jax.random.normal(jax.random.fold_in(_rk, 611), (4, 154, 256), jnp.float32))
        _validS = jnp.arange(1024)[None, :] < _lenS[:, None]
        _validS2 = jnp.arange(154)[None, :] < _lenS2[:, None]
        _causal = jnp.tril(jnp.ones((1024, 1024), dtype=bool))
        mask_BxS2_bk0 = jnp.logical_not(jnp.broadcast_to(_validS2[:, :], (4, 154)))
        return (x, ctx_1024, mask_BxS2_bk0)
    x, ctx_1024, mask_BxS2_bk0 = _rec_inputs()

    def _L0_xattn_setup():
        import jax, jax.numpy as jnp
        import numpy as np
        DIM = 256
        HEADS = 8
        DIM_HEAD = 64
        INNER = HEADS * DIM_HEAD
        EPS = 1e-05

        def layernorm(x, w, b):
            mu = jnp.mean(x, axis=-1, keepdims=True)
            var = jnp.var(x, axis=-1, keepdims=True)
            return (x - mu) * jax.lax.rsqrt(var + EPS) * w + b
        key = jax.random.key(seed)
        ks = jax.random.split(key, 7)
        b, n_media, n_lat = (16, 512, 64)
        x = jax.random.normal(ks[0], (b, n_media, DIM), dtype=jnp.float32)
        latents = jax.random.normal(ks[1], (b, n_lat, DIM), dtype=jnp.float32)
        ln_m_w = jnp.ones((DIM,), jnp.float32)
        ln_m_b = jnp.zeros((DIM,), jnp.float32)
        ln_l_w = jnp.ones((DIM,), jnp.float32)
        ln_l_b = jnp.zeros((DIM,), jnp.float32)
        Wq = jax.random.normal(ks[2], (DIM, INNER), dtype=jnp.float32) * DIM ** (-0.5)
        Wkv = jax.random.normal(ks[3], (DIM, 2 * INNER), dtype=jnp.float32) * DIM ** (-0.5)
        Wout = jax.random.normal(ks[4], (INNER, DIM), dtype=jnp.float32) * INNER ** (-0.5)
        return {'x': x, 'latents': latents, 'ln_m_w': ln_m_w, 'ln_m_b': ln_m_b, 'ln_l_w': ln_l_w, 'ln_l_b': ln_l_b, 'Wq': Wq, 'Wkv': Wkv, 'Wout': Wout}
    _L0_xattn_all = _L0_xattn_setup()
    _L0_xattn_in = {k: v for k, v in _L0_xattn_all.items() if k in ('ln_m_w', 'ln_m_b', 'ln_l_w', 'ln_l_b', 'Wq', 'Wkv', 'Wout')}
    del _L0_xattn_all

    def _L0_ffn_setup():
        import math
        import jax, jax.numpy as jnp
        import numpy as np
        B, T, D, H, E, K, S = (4, 1024, 256, 512, 16, 2, 2)
        ROUTE_SCALE = 1.0

        def _swiglu(x, w1, w3, w2):
            return jax.nn.silu(x @ w1) * (x @ w3) @ w2
        key = jax.random.key(seed)
        ks = jax.random.split(key, 9)
        s = 0.02
        return {'x': jax.random.normal(ks[0], (B, T, D), jnp.float32), 'gate_w': jax.random.normal(ks[1], (D, E), jnp.float32) * s, 'gate_b': jnp.zeros((E,), jnp.float32), 'ew1': jax.random.normal(ks[2], (E, D, H), jnp.float32) * s, 'ew3': jax.random.normal(ks[3], (E, D, H), jnp.float32) * s, 'ew2': jax.random.normal(ks[4], (E, H, D), jnp.float32) * s, 'sw1': jax.random.normal(ks[5], (S, D, H), jnp.float32) * s, 'sw3': jax.random.normal(ks[6], (S, D, H), jnp.float32) * s, 'sw2': jax.random.normal(ks[7], (S, H, D), jnp.float32) * s}
    _L0_ffn_all = _L0_ffn_setup()
    _L0_ffn_in = {k: v for k, v in _L0_ffn_all.items() if k in ('gate_w', 'gate_b', 'ew1', 'ew3', 'ew2', 'sw1', 'sw3', 'sw2')}
    del _L0_ffn_all

    def _L1_xattn_setup():
        import jax, jax.numpy as jnp
        import numpy as np
        DIM = 256
        HEADS = 16
        HEAD_DIM = DIM // HEADS
        B, N, S = (4, 1024, 128)
        key = jax.random.key(seed)
        ks = jax.random.split(key, 9)
        scale = DIM ** (-0.5)
        return {'x': jax.random.normal(ks[0], (B, N, DIM), dtype=jnp.float32), 'context': jax.random.normal(ks[1], (B, S, DIM), dtype=jnp.float32), 'context_mask': jax.random.uniform(ks[2], (B, S)) < 0.2, 'q_w': jax.random.normal(ks[3], (DIM, DIM), dtype=jnp.float32) * scale, 'q_b': jnp.zeros((DIM,), dtype=jnp.float32), 'kv_w': jax.random.normal(ks[4], (DIM, 2 * DIM), dtype=jnp.float32) * scale, 'kv_b': jnp.zeros((2 * DIM,), dtype=jnp.float32), 'proj_w': jax.random.normal(ks[5], (DIM, DIM), dtype=jnp.float32) * scale, 'proj_b': jnp.zeros((DIM,), dtype=jnp.float32)}
    _L1_xattn_all = _L1_xattn_setup()
    _L1_xattn_in = {k: v for k, v in _L1_xattn_all.items() if k in ('q_w', 'q_b', 'kv_w', 'kv_b', 'proj_w', 'proj_b')}
    del _L1_xattn_all

    def _L1_ffn_setup():
        import jax, jax.numpy as jnp
        import numpy as np
        key = jax.random.key(seed)
        k0, k1, k2, k3 = jax.random.split(key, 4)
        B, S, D, F, E = (8, 512, 256, 512, 8)
        x = jax.random.normal(k0, (B, S, D), dtype=jnp.float32)
        Wg = jax.random.normal(k1, (D, E), dtype=jnp.float32) * 0.02
        W1 = jax.random.normal(k2, (E, D, F), dtype=jnp.float32) * 0.02
        W2 = jax.random.normal(k3, (E, F, D), dtype=jnp.float32) * 0.02
        return {'x': x, 'Wg': Wg, 'W1': W1, 'W2': W2}
    _L1_ffn_all = _L1_ffn_setup()
    _L1_ffn_in = {k: v for k, v in _L1_ffn_all.items() if k in ('Wg', 'W1', 'W2')}
    del _L1_ffn_all
    return {'x': x, 'ctx_1024': ctx_1024, 'mask_BxS2_bk0': mask_BxS2_bk0, 'L0_xattn_ln_m_w': _L0_xattn_in['ln_m_w'], 'L0_xattn_ln_m_b': _L0_xattn_in['ln_m_b'], 'L0_xattn_ln_l_w': _L0_xattn_in['ln_l_w'], 'L0_xattn_ln_l_b': _L0_xattn_in['ln_l_b'], 'L0_xattn_Wq': _L0_xattn_in['Wq'], 'L0_xattn_Wkv': _L0_xattn_in['Wkv'], 'L0_xattn_Wout': _L0_xattn_in['Wout'], 'L0_ffn_gate_w': _L0_ffn_in['gate_w'], 'L0_ffn_gate_b': _L0_ffn_in['gate_b'], 'L0_ffn_ew1': _L0_ffn_in['ew1'], 'L0_ffn_ew3': _L0_ffn_in['ew3'], 'L0_ffn_ew2': _L0_ffn_in['ew2'], 'L0_ffn_sw1': _L0_ffn_in['sw1'], 'L0_ffn_sw3': _L0_ffn_in['sw3'], 'L0_ffn_sw2': _L0_ffn_in['sw2'], 'L1_xattn_q_w': _L1_xattn_in['q_w'], 'L1_xattn_q_b': _L1_xattn_in['q_b'], 'L1_xattn_kv_w': _L1_xattn_in['kv_w'], 'L1_xattn_kv_b': _L1_xattn_in['kv_b'], 'L1_xattn_proj_w': _L1_xattn_in['proj_w'], 'L1_xattn_proj_b': _L1_xattn_in['proj_b'], 'L1_ffn_Wg': _L1_ffn_in['Wg'], 'L1_ffn_W1': _L1_ffn_in['W1'], 'L1_ffn_W2': _L1_ffn_in['W2']}

def reference(x, ctx_1024, mask_BxS2_bk0, L0_xattn_ln_m_w, L0_xattn_ln_m_b, L0_xattn_ln_l_w, L0_xattn_ln_l_b, L0_xattn_Wq, L0_xattn_Wkv, L0_xattn_Wout, L0_ffn_gate_w, L0_ffn_gate_b, L0_ffn_ew1, L0_ffn_ew3, L0_ffn_ew2, L0_ffn_sw1, L0_ffn_sw3, L0_ffn_sw2, L1_xattn_q_w, L1_xattn_q_b, L1_xattn_kv_w, L1_xattn_kv_b, L1_xattn_proj_w, L1_xattn_proj_b, L1_ffn_Wg, L1_ffn_W1, L1_ffn_W2):
    import jax
    import jax.numpy as jnp

    def _L0_xattn_ref(x, latents, ln_m_w, ln_m_b, ln_l_w, ln_l_b, Wq, Wkv, Wout):
        import jax, jax.numpy as jnp
        import numpy as np
        DIM = 256
        HEADS = 8
        DIM_HEAD = 64
        INNER = HEADS * DIM_HEAD
        EPS = 1e-05

        def layernorm(x, w, b):
            mu = jnp.mean(x, axis=-1, keepdims=True)
            var = jnp.var(x, axis=-1, keepdims=True)
            return (x - mu) * jax.lax.rsqrt(var + EPS) * w + b
        scale = DIM_HEAD ** (-0.5)
        xn = layernorm(x, ln_m_w, ln_m_b)
        ln = layernorm(latents, ln_l_w, ln_l_b)
        b = xn.shape[0]
        q = ln @ Wq
        kv_input = jnp.concatenate([xn, ln], axis=-2)
        kv = kv_input @ Wkv
        k, v = jnp.split(kv, 2, axis=-1)

        def to_heads(t):
            return t.reshape(b, t.shape[1], HEADS, DIM_HEAD).transpose(0, 2, 1, 3)
        q, k, v = (to_heads(q) * scale, to_heads(k), to_heads(v))
        sim = jnp.einsum('bhid,bhjd->bhij', q, k)
        attn = jax.nn.softmax(sim, axis=-1)
        out = jnp.einsum('bhij,bhjd->bhid', attn, v)
        out = out.transpose(0, 2, 1, 3).reshape(b, out.shape[2], INNER)
        return out @ Wout

    def _L0_ffn_ref(x, gate_w, gate_b, ew1, ew3, ew2, sw1, sw3, sw2):
        import math
        import jax, jax.numpy as jnp
        import numpy as np
        B, T, D, H, E, K, S = (4, 1024, 256, 512, 16, 2, 2)
        ROUTE_SCALE = 1.0

        def _swiglu(x, w1, w3, w2):
            return jax.nn.silu(x @ w1) * (x @ w3) @ w2
        Bx, Tx, Dx = x.shape
        flat = x.reshape(-1, Dx)
        N = flat.shape[0]
        n_experts = gate_w.shape[1]
        logits = flat @ gate_w
        scores = jax.nn.softmax(logits.astype(jnp.float32), -1) + gate_b
        _, topi = jax.lax.top_k(scores, K)
        weights = jnp.take_along_axis(logits, topi, axis=-1) * ROUTE_SCALE
        weights = weights.astype(flat.dtype)
        capacity = math.ceil(N * K / n_experts * 1.25)

        def per_expert(gid, w1, w3, w2):
            match = topi == gid
            assigned = match.any(-1)
            w_tok = jnp.sum(jnp.where(match, weights, 0.0), -1)
            wm = jnp.where(assigned, w_tok, -jnp.inf)
            vals, idx = jax.lax.top_k(wm, capacity)
            valid = assigned[idx]
            xs = flat[idx]
            y = _swiglu(xs, w1, w3, w2) * jnp.where(valid, vals, 0.0)[:, None]
            return (idx, y)
        idxs, ys = jax.vmap(per_expert)(jnp.arange(n_experts), ew1, ew3, ew2)
        out = jnp.zeros_like(flat).at[idxs.reshape(-1)].add(ys.reshape(-1, Dx))
        shared = jax.vmap(lambda w1, w3, w2: _swiglu(flat, w1, w3, w2))(sw1, sw3, sw2)
        out = out + shared.mean(0)
        return out.reshape(Bx, Tx, Dx)

    def _L1_xattn_ref(x, context, context_mask, q_w, q_b, kv_w, kv_b, proj_w, proj_b):
        import jax, jax.numpy as jnp
        import numpy as np
        DIM = 256
        HEADS = 16
        HEAD_DIM = DIM // HEADS
        B, N, S = (4, 1024, 128)
        b, n, c = x.shape
        s = context.shape[1]
        h, d = (HEADS, HEAD_DIM)
        scale = d ** (-0.5)
        q = (x @ q_w + q_b).reshape(b, n, h, d)
        kv = (context @ kv_w + kv_b).reshape(b, s, 2, h, d)
        k = kv[:, :, 0]
        v = kv[:, :, 1]
        attn = jnp.einsum('bnhd,bshd->bhns', q, k) * scale
        attn = jnp.where(context_mask[:, None, None, :], -jnp.inf, attn)
        attn = jax.nn.softmax(attn, axis=-1)
        out = jnp.einsum('bhns,bshd->bnhd', attn, v).reshape(b, n, c)
        return out @ proj_w + proj_b

    def _L1_ffn_ref(x, Wg, W1, W2):
        import jax, jax.numpy as jnp
        import numpy as np
        B, S, D = x.shape
        E = Wg.shape[1]
        T = B * S
        cap = max(1, T // E)
        xt = x.reshape(T, D)
        logits = xt @ Wg
        probs = jax.nn.softmax(logits, axis=-1)
        pT = probs.T
        _, top_idx = jax.lax.top_k(pT, cap)
        sel = jnp.zeros((E, T), dtype=bool).at[jnp.arange(E)[:, None], top_idx].set(True)
        masked = jnp.where(sel, pT, -jnp.inf)
        assigned = sel.any(axis=0)
        tok2exp = jnp.where(assigned, jnp.argmax(masked, axis=0), jnp.argmax(pT, axis=0))
        weights = jnp.take_along_axis(probs, tok2exp[:, None], axis=1)[:, 0]
        out = jnp.zeros_like(xt)
        for e in range(E):
            gate = jnp.where(tok2exp == e, weights, 0.0)
            h = jax.nn.gelu(xt @ W1[e], approximate=False) @ W2[e]
            out = out + gate[:, None] * h
        return out.reshape(B, S, D)
    x = x + _L0_xattn_ref(ctx_1024, _layernorm(x, axis=-1), L0_xattn_ln_m_w, L0_xattn_ln_m_b, L0_xattn_ln_l_w, L0_xattn_ln_l_b, L0_xattn_Wq, L0_xattn_Wkv, L0_xattn_Wout)
    x = x + _L0_ffn_ref(_layernorm(x, axis=-1), L0_ffn_gate_w, L0_ffn_gate_b, L0_ffn_ew1, L0_ffn_ew3, L0_ffn_ew2, L0_ffn_sw1, L0_ffn_sw3, L0_ffn_sw2)
    x = x + _L1_xattn_ref(_layernorm(x, axis=-1), ctx_1024, mask_BxS2_bk0, L1_xattn_q_w, L1_xattn_q_b, L1_xattn_kv_w, L1_xattn_kv_b, L1_xattn_proj_w, L1_xattn_proj_b)
    x = x + _L1_ffn_ref(_layernorm(x, axis=-1), L1_ffn_Wg, L1_ffn_W1, L1_ffn_W2)
    return x

_drawn_inputs = setup_inputs


def setup_inputs(seed=0):
    import zlib

    import numpy as np

    out = dict(_drawn_inputs(seed))
    spreads = {'L0_xattn_ln_m_w': (1.0, 0.6),
     'L0_xattn_ln_m_b': (0.0, 0.595),
     'L0_xattn_ln_l_w': (1.0, 0.2),
     'L0_xattn_ln_l_b': (0.0, 0.1),
     'L0_ffn_gate_b': (0.0, 0.586),
     'L1_xattn_q_b': (0.0, 2.0),
     'L1_xattn_kv_b': (0.0, 0.8),
     'L1_xattn_proj_b': (0.0, 0.8)}
    factors = {'L0_ffn_gate_w': 7.036,
     'L0_ffn_ew1': 6.571,
     'L0_ffn_ew3': 6.497,
     'L0_ffn_ew2': 6.484,
     'L0_ffn_sw1': 3.83,
     'L0_ffn_sw3': 3.797,
     'L0_ffn_sw2': 3.797,
     'L1_ffn_Wg': 4.62,
     'L1_ffn_W1': 4.414,
     'L1_ffn_W2': 4.356,
     'L1_xattn_q_w': 5.42}
    for name, (base, spread) in spreads.items():
        noise = np.random.default_rng([zlib.crc32(name.encode()), seed]).standard_normal(out[name].shape)
        drawn = base * np.exp(spread * noise) if base else spread * noise
        out[name] = jnp.asarray(drawn.astype(out[name].dtype))
    for name, factor in factors.items():
        out[name] = (out[name] * factor).astype(out[name].dtype)
    return out
```

```python
from contextlib import ExitStack

import numpy as np

import concourse.bass as bass
from concourse import mybir

F32 = mybir.dt.float32
F32R = mybir.dt.float32r
I32 = mybir.dt.int32
U32 = mybir.dt.uint32
ALU = mybir.AluOpType
ACT = mybir.ActivationFunctionType
AX = mybir.AxisListType

P = 128
B, N, S, D = 4, 1024, 154, 256
TOK = B * N
TT = TOK // P
TB = N // P
KD = D // P
S1 = S - P
EPS = 1e-5

KEYS = N + S
PAIRS = 4
DH = 64
KC = -(-KEYS // P)
KREST = KEYS - (KC - 1) * P


class Steps:

    def __init__(self, eng, sem, it=0, per=0, base=0):
        self.eng, self.sem, self.it, self.per, self.base, self.n = eng, sem, it, per, base, 0

    def done(self, instruction):
        instruction.then_inc(self.sem, 1)
        self.n += 1

    def wait(self):
        self.eng.wait_ge(self.sem, self.it * self.per + (self.base + self.n))

    def then(self, instruction):
        self.done(instruction)
        self.wait()


def due(count):
    return not isinstance(count, int) or count > 0


def spans(n, width=512):
    return [(a, min(width, n - a)) for a in range(0, n, width)]


def inverse_root(act, dve, steps, root_done, ve, root, y, tmp, count):
    if act is not None:
        act.activation(root, ve, ACT.Sqrt).then_inc(root_done, 1)
        return
    dve.wait_ge(root_done, count)
    steps.then(dve.reciprocal(y, root))
    steps.then(dve.tensor_tensor(tmp, y, y, ALU.mult))
    steps.then(dve.tensor_tensor(tmp, tmp, ve, ALU.mult))
    steps.then(dve.tensor_scalar(tmp, tmp, -0.5, 1.5, ALU.mult, ALU.add))
    steps.then(dve.tensor_tensor(y, y, tmp, ALU.mult))


def embed(nc, io, x_sb, ident, kvT):
    with ExitStack() as ctx:
        sb = lambda n, s, d=F32: ctx.enter_context(nc.sbuf_tensor(n, s, d))
        sem = lambda n: ctx.enter_context(nc.semaphore(n))
        ctx0 = sb("ctx_rows0", [P, B, D])
        ctx1 = sb("ctx_rows1", [S1, B, D])
        NS = TT + 2 * B
        stats = sb("ln0_stats", [P, NS, 6])
        mv = sb("ln0_mean_var", [P, NS, 2])
        ve = sb("ln0_var_eps", [P, NS])
        root = sb("ln0_root", [P, NS])
        inv = sb("ln0_inv", [P, NS])
        tmp = sb("ln0_tmp", [P, NS])
        ve2 = sb("ln0_var_eps2", [P, TT])
        root2 = sb("ln0_root2", [P, TT])
        inv2 = sb("ln0_inv2", [P, TT])
        tmp2 = sb("ln0_tmp2", [P, TT])
        lw = sb("ln_l_affine", [P, 2, KD])
        mw = sb("ln_m_affine", [P, 2, KD])
        xn = sb("ln0_rows", [P, 2, 4, D])
        cn = sb("ln0_ctx_rows", [P, 2, D])
        pt = [ctx.enter_context(nc.psum_tensor(f"ln0_T{i}", [P, 512], F32)) for i in range(6)]
        x_loaded = [sem(f"x_loaded{b}") for b in range(B)]
        c_loaded = sem("ctx_loaded")
        w_loaded = sem("ln_affine_loaded")
        identity_made = sem("identity_made")
        dve_step = sem("ln0_dve_step")
        var_ready = sem("ln0_var_ready")
        root_done = sem("ln0_root_done")
        rows_ready = sem("ln0_rows_ready")
        turned = sem("ln0_turned")
        copied = sem("ln0_copied")

        with nc.Block() as block:
            @block.sync
            def _(sp):
                x_t = io["x"].rearrange("b (t p) d -> b p t d", p=P)
                for b in range(B):
                    sp.dma_start(x_sb[:, b * TB:(b + 1) * TB, :], x_t[b]).then_inc(x_loaded[b], 16)

            @block.gpsimd
            def _(pool):
                pool.memset(ident[:, :], 0.0).then_inc(identity_made, 1)
                pool.wait_ge(identity_made, 1)
                pool.affine_select(out=ident[:, :], in_=ident[:, :], compare_op=ALU.not_equal, fill=1.0,
                                   base=0, pattern=[[-1, P]], channel_multiplier=1).then_inc(identity_made, 1)

            @block.scalar
            def _(act):
                act.dma_start(ctx0[:, :, :], io["ctx_1024"][:, 0:P, :].rearrange("b p d -> p b d")).then_inc(c_loaded, 16)
                act.dma_start(ctx1[:, :, :], io["ctx_1024"][:, P:S, :].rearrange("b p d -> p b d")).then_inc(c_loaded, 16)
                for t, names in ((lw, ("L0_xattn_ln_l_w", "L0_xattn_ln_l_b")), (mw, ("L0_xattn_ln_m_w", "L0_xattn_ln_m_b"))):
                    for j, name in enumerate(names):
                        act.dma_start(t[:, j, :], io[name].rearrange("(k p) -> p k", p=P), allow_slow_non_contiguous=True).then_inc(w_loaded, 16)
                act.wait_ge(var_ready, 1)
                inverse_root(act, None, None, root_done, ve[:, :], root[:, :], None, None, 0)
                act.wait_ge(var_ready, 2)
                inverse_root(act, None, None, root_done, ve2[:, :], root2[:, :], None, None, 0)
                act.wait_ge(w_loaded, 64)
                with act.Fori(0, B) as b:
                    for u in range(3):
                        act.wait_ge(turned, b * 3 + (u + 1))
                        for k in range(KD):
                            w = lw if u < 2 else mw
                            cols, n = (u * 512, 512) if u < 2 else (N, S)
                            out = kvT[:, k, bass.ds(b * KEYS + cols, n)]
                            ins = act.activation(out, pt[2 * u + k][:, 0:n], ACT.Identity,
                                                 bias=w[:, 1, k:k + 1], scale=w[:, 0, k:k + 1])
                        ins.then_inc(copied, 1)

            @block.vector
            def _(dve):
                step = Steps(dve, dve_step)
                step.then(dve.memset(mv[:, :, :], 1.0))
                for b in range(B):
                    dve.wait_ge(x_loaded[b], 16)
                    for j in range(TB):
                        t = b * TB + j
                        step.done(dve.bn_stats(stats[:, t, :], x_sb[:, t, :]))
                dve.wait_ge(c_loaded, 32)
                for b in range(B):
                    step.done(dve.bn_stats(stats[:, TT + b, :], ctx0[:, b, :]))
                    step.done(dve.bn_stats(stats[0:S1, TT + B + b, :], ctx1[:, b, :]))
                step.wait()
                for t in range(NS):
                    r = P if t < TT + B else S1
                    step.done(dve.bn_aggr(mv[0:r, t, :], stats[0:r, t, :]))
                step.wait()
                dve.tensor_scalar(ve[:, :], mv[:, :, 1], EPS, None, ALU.add).then_inc(var_ready, 1)
                inverse_root(None, dve, step, root_done, ve[:, :], root[:, :], inv[:, :], tmp[:, :], 1)
                lat = slice(0, TT)
                step.then(dve.tensor_tensor(tmp[:, lat], inv[:, lat], inv[:, lat], ALU.mult))
                step.then(dve.tensor_tensor(tmp[:, lat], tmp[:, lat], mv[:, lat, 1], ALU.mult))
                dve.tensor_scalar(ve2[:, :], tmp[:, lat], EPS, None, ALU.add).then_inc(var_ready, 1)
                dve.wait_ge(var_ready, 2)
                inverse_root(None, dve, step, root_done, ve2[:, :], root2[:, :], inv2[:, :], tmp2[:, :], 2)
                step.then(dve.tensor_tensor(inv[:, lat], inv[:, lat], inv2[:, :], ALU.mult))
                def batch(b):
                    for u in range(2):
                        if due(b * 3):
                            dve.wait_ge(turned, b * 3)
                        for j in range(4):
                            t = b * TB + (u * 4 + j)
                            ins = dve.tensor_scalar(xn[:, u, j, :], x_sb[:, bass.ds(t, 1), :].rearrange("p a d -> p (a d)"),
                                                    mv[:, bass.ds(t, 1), 0], inv[:, bass.ds(t, 1)], ALU.subtract, ALU.mult)
                        ins.then_inc(rows_ready, 1)
                    t0, t1 = b + TT, b + (TT + B)
                    dve.tensor_scalar(cn[:, 0, :], ctx0[:, bass.ds(b, 1), :].rearrange("p a d -> p (a d)"),
                                      mv[:, bass.ds(t0, 1), 0], inv[:, bass.ds(t0, 1)], ALU.subtract, ALU.mult)
                    dve.tensor_scalar(cn[0:S1, 1, :], ctx1[:, bass.ds(b, 1), :].rearrange("p a d -> p (a d)"),
                                      mv[0:S1, bass.ds(t1, 1), 0], inv[0:S1, bass.ds(t1, 1)],
                                      ALU.subtract, ALU.mult).then_inc(rows_ready, 1)

                batch(0)
                with dve.Fori(1, B) as b:
                    batch(b)

            @block.tensor
            def _(pe):
                def batch(b):
                    for u in range(3):
                        pe.wait_ge(rows_ready, b * 3 + (u + 1))
                        if due(b * 3):
                            pe.wait_ge(copied, b * 3)
                        for k in range(KD):
                            cols = slice(k * P, (k + 1) * P)
                            if u < 2:
                                for j in range(4):
                                    ins = pe.transpose(pt[2 * u + k][:, j * P:(j + 1) * P], xn[:, u, j, cols], ident[:, :])
                            else:
                                pe.transpose(pt[4 + k][:, 0:P], cn[:, 0, cols], ident[:, :])
                                ins = pe.transpose(pt[4 + k][:, P:S], cn[0:S1, 1, cols], ident[0:S1, 0:S1])
                        ins.then_inc(turned, 1)

                pe.wait_ge(identity_made, 2)
                batch(0)
                with pe.Fori(1, B) as b:
                    batch(b)


def latent_attention(nc, io, x_sb, ident, kvT):
    ROUNDS = B * PAIRS
    G, GQ = 4, 256
    SC = KEYS
    with ExitStack() as ctx:
        sb = lambda n, s, d=F32: ctx.enter_context(nc.sbuf_tensor(n, s, d))
        sem = lambda n: ctx.enter_context(nc.semaphore(n))
        w_pair = sb("w_pair", [P, 3, KD, P])
        w_out = sb("w_out", [P, PAIRS, D])
        q2 = sb("q_halves", [P, 2, N], F32R)
        k_hi = sb("k_high", [P, 2, SC], F32R)
        k_lo = sb("k_low", [P, 2, SC], F32R)
        vT = sb("vT", [P, SC])
        v = sb("v_pair", [P, KC, P])
        probs = sb("probs", [P, 8, SC])
        sums = sb("prob_sums", [P, 8])
        neg_max = sb("neg_max", [P, 8])
        recip = sb("prob_recip", [P, 8])
        pT = sb("probsT", [P, 2, 512])
        oT = sb("outT", [P, GQ])
        tile = [ctx.enter_context(nc.psum_tensor(f"tile{j}", [P, 1536], F32)) for j in range(2)]
        turn = ctx.enter_context(nc.psum_tensor("turn", [P, 512], F32))
        outp = ctx.enter_context(nc.psum_tensor("out_acc", [P, 512], F32))

        wout_loaded = sem("wout_loaded")
        w_loaded = sem("w_pair_loaded")
        q_made = sem("q_made")
        k_made = sem("k_made")
        v_made = sem("v_made")
        v_turned = sem("v_turned")
        q_hi_done = sem("q_hi_done")
        q_lo_done = sem("q_lo_done")
        k_hi_done = sem("k_hi_done")
        k_lo_done = sem("k_lo_done")
        vT_done = sem("vT_done")
        v_done = sem("v_done")
        scores = sem("scores_made")
        maxed = sem("max_done")
        exped = sem("exp_done")
        recips = sem("recip_done")
        scaled = sem("probs_scaled")
        p_turned = sem("probs_turned")
        pT_even = sem("pT_even_done")
        pT_odd = sem("pT_odd_done")
        o_made = sem("out_made")
        o_done = sem("out_done")
        y_made = sem("y_made")
        y_added = sem("y_added")
        CE, CO = KC - KC // 2, KC // 2

        def chunk(c):
            return P if c < KC - 1 else KREST

        with nc.Block() as block:
            @block.sync
            def _(sp):
                sp.dma_start(w_out[:, :, :], io["L0_xattn_Wout"].rearrange("(q p) n -> p q n", p=P)).then_inc(wout_loaded, 16)
                wq = io["L0_xattn_Wq"].rearrange("(k p) n -> p k n", p=P)
                wkv = io["L0_xattn_Wkv"].rearrange("(k p) n -> p k n", p=P)
                def load(i):
                    if due(i):
                        sp.wait_ge(v_made, i)
                    c = (i % PAIRS) * P
                    sp.dma_start(w_pair[:, 0], wq[:, :, bass.ds(c, P)]).then_inc(w_loaded, 16)
                    sp.dma_start(w_pair[:, 1], wkv[:, :, bass.ds(c, P)]).then_inc(w_loaded, 16)
                    sp.dma_start(w_pair[:, 2], wkv[:, :, bass.ds(c + PAIRS * P, P)]).then_inc(w_loaded, 16)

                load(0)
                with sp.Fori(1, ROUNDS) as i:
                    load(i)

            @block.tensor
            def _(pe):
                def project(j, which):
                    dst = tile[(0, 1, 0)[which]]
                    if which == 0:
                        pe.wait_ge(w_loaded, j * 48 + 48)
                    for a, n in spans(N if which == 0 else SC):
                        for k in range(KD):
                            ins = pe.matmul(dst[:, a:a + n], w_pair[:, which, k, :], kvT[:, k, bass.ds((j // PAIRS) * KEYS + a, n)],
                                            start=k == 0, stop=k == KD - 1)
                    ins.then_inc((q_made, k_made, v_made)[which], 1)

                def turn_v(j):
                    pe.wait_ge(vT_done, j + 1)
                    pe.wait_ge(k_lo_done, j * 2 + 2)
                    pe.wait_ge(k_hi_done, j * 2 + 2)
                    for c in range(KC):
                        ins = pe.transpose(tile[1][0:chunk(c), c * P:(c + 1) * P], vT[:, c * P:c * P + chunk(c)], ident[:, :])
                    ins.then_inc(v_turned, 1)

                def score(i, s):
                    g, h, t = s // 4, s // 2 % 2, s % 2
                    if s == 0:
                        pe.wait_ge(vT_done, i + 1)
                        pe.wait_ge(q_hi_done, i * 2 + 2)
                        pe.wait_ge(q_lo_done, i * 2 + 2)
                        pe.wait_ge(k_hi_done, i * 2 + 2)
                        pe.wait_ge(k_lo_done, i * 2 + 2)
                    elif s == 1:
                        pe.wait_ge(v_done, i + 1)
                    else:
                        pe.wait_ge(exped, i * 16 + (s - 1))
                    q = q2[:, h, g * GQ + t * P:g * GQ + (t + 1) * P]
                    for a, n in spans(SC):
                        pe.matmul(tile[s % 2][:, a:a + n], q, k_hi[:, h, a:a + n], start=True, stop=False)
                        ins = pe.matmul(tile[s % 2][:, a:a + n], q, k_lo[:, h, a:a + n], start=False, stop=True)
                    ins.then_inc(scores, 1)

                def turn_probs(i, g, c):
                    if c == 0:
                        pe.wait_ge(scaled, i * 16 + 4 * (g + 1))
                        if due(i * G + g):
                            pe.wait_ge(y_added, i * G + g)
                    elif c % 2:
                        pe.wait_ge(pT_even, i * G * CE + g * CE + c // 2 + 1)
                    else:
                        pe.wait_ge(pT_odd, i * G * CO + g * CO + c // 2)
                    for j in range(4):
                        ins = pe.transpose(turn[0:chunk(c), j * P:(j + 1) * P],
                                           probs[:, 4 * (g % 2) + j, c * P:c * P + chunk(c)], ident[:, :])
                    ins.then_inc(p_turned, 1)

                def weigh(i, g, c):
                    if c == 0:
                        if due(i * G + g):
                            pe.wait_ge(o_done, i * G + g)
                    if c % 2:
                        pe.wait_ge(pT_odd, i * G * CO + g * CO + c // 2 + 1)
                    else:
                        pe.wait_ge(pT_even, i * G * CE + g * CE + c // 2 + 1)
                    for h in range(2):
                        ins = pe.matmul(outp[h * DH:(h + 1) * DH, 0:GQ], v[0:chunk(c), c, h * DH:(h + 1) * DH],
                                        pT[0:chunk(c), c % 2, h * GQ:(h + 1) * GQ], start=c == 0, stop=c == KC - 1)
                    if c == KC - 1:
                        ins.then_inc(o_made, 1)

                def to_width(i, g):
                    pe.wait_ge(o_done, i * G + g + 1)
                    pe.wait_ge(pT_odd, i * G * CO + (g + 1) * CO)
                    for t in range(2):
                        ins = pe.matmul(turn[:, t * D:(t + 1) * D], oT[:, t * P:(t + 1) * P],
                                        w_out[:, bass.ds(i % PAIRS, 1), :].rearrange("p a n -> p (a n)"), start=True, stop=True)
                    ins.then_inc(y_made, 1)

                def round_(i, last):
                    for s in range(4):
                        score(i, s)
                    for g in range(G):
                        extra = {1: 0, 2: 1, 4: 2, 6: 3}
                        for c in range(KC):
                            turn_probs(i, g, c)
                            if c:
                                weigh(i, g, c - 1)
                            if g < G - 1 and c in (0, 1, 3, 5):
                                score(i, 4 * (g + 1) + (0, 1, 3, 5).index(c))
                            if g == G - 1 and not last and c in (0, 2, 5):
                                if c == 0:
                                    pe.wait_ge(exped, i * 16 + 15)
                                elif c == 2:
                                    pe.wait_ge(exped, i * 16 + 16)
                                else:
                                    pe.wait_ge(q_lo_done, i * 2 + 4)
                                    pe.wait_ge(q_hi_done, i * 2 + 4)
                                project(i + 1, (0, 2, 5).index(c))
                        weigh(i, g, KC - 1)
                        if g == G - 1 and not last:
                            turn_v(i + 1)
                        to_width(i, g)

                project(0, 0)
                project(0, 1)
                pe.wait_ge(q_lo_done, 2)
                pe.wait_ge(q_hi_done, 2)
                project(0, 2)
                turn_v(0)
                pe.wait_ge(wout_loaded, 16)
                round_(0, False)
                with pe.Fori(1, ROUNDS - 1) as i:
                    round_(i, False)
                round_(ROUNDS - 1, True)

            @block.scalar
            def _(act):
                def q_high(j):
                    act.wait_ge(q_made, j + 1)
                    for h in range(2):
                        r = slice(h * DH, (h + 1) * DH)
                        act.activation(q2[r, h, :], tile[0][r, 0:N], ACT.Copy, scale=DH ** -0.5).then_inc(q_hi_done, 1)

                def k_high(j):
                    act.wait_ge(k_made, j + 1)
                    for h in range(2):
                        for r in range(2):
                            ins = act.activation(k_hi[r * DH:(r + 1) * DH, h, :], tile[1][h * DH:(h + 1) * DH, 0:SC], ACT.Copy)
                        ins.then_inc(k_hi_done, 1)

                def copy_vT(j):
                    act.wait_ge(v_made, j + 1)
                    act.activation(vT[:, :], tile[0][:, 0:SC], ACT.Copy).then_inc(vT_done, 1)

                def copy_v(j):
                    act.wait_ge(v_turned, j + 1)
                    act.activation(v[:, 0:KC - 1, :], tile[1][:, 0:(KC - 1) * P].rearrange("p (c n) -> p c n", n=P), ACT.Copy)
                    act.activation(v[0:KREST, KC - 1, :], tile[1][0:KREST, (KC - 1) * P:KC * P], ACT.Copy).then_inc(v_done, 1)

                def exp(i, s):
                    act.wait_ge(maxed, i * 16 + (s + 1))
                    act.activation(probs[:, s % 8, :], tile[s % 2][:, 0:SC], ACT.Exp, bias=neg_max[:, s % 8:s % 8 + 1],
                                   accum_out=sums[:, s % 8:s % 8 + 1]).then_inc(exped, 1)

                def copy_pT(i, g, c):
                    act.wait_ge(p_turned, i * G * KC + (g * KC + c + 1))
                    act.activation(pT[0:chunk(c), c % 2, :], turn[0:chunk(c), :], ACT.Copy).then_inc(pT_even, 1)

                def copy_out(i, g):
                    act.wait_ge(o_made, i * G + (g + 1))
                    act.activation(oT[:, :], outp[:, 0:GQ], ACT.Copy).then_inc(o_done, 1)

                def round_(i, last):
                    for s in range(4):
                        exp(i, s)
                    for g in range(G):
                        for n, c in enumerate(range(0, KC, 2)):
                            copy_pT(i, g, c)
                            if g < G - 1 and n < 4:
                                exp(i, 4 * (g + 1) + n)
                            if g == G - 1 and not last and n in (0, 1, 3):
                                (q_high, k_high, None, copy_vT)[n](i + 1)
                        copy_out(i, g)
                        if g == G - 1 and not last:
                            copy_v(i + 1)

                q_high(0)
                k_high(0)
                copy_vT(0)
                copy_v(0)
                round_(0, False)
                with act.Fori(1, ROUNDS - 1) as i:
                    round_(i, False)
                round_(ROUNDS - 1, True)

            @block.vector
            def _(dve):
                def q_low(j):
                    for h in range(2):
                        dve.wait_ge(q_hi_done, j * 2 + (h + 1))
                        r, o = slice(h * DH, (h + 1) * DH), slice((1 - h) * DH, (2 - h) * DH)
                        dve.scalar_tensor_tensor(out=q2[o, h, :], in0=tile[0][r, 0:N], scalar=DH ** -0.5,
                                                 in1=q2[r, h, :].bitcast(F32), op0=ALU.mult,
                                                 op1=ALU.subtract).then_inc(q_lo_done, 1)

                def k_low(j):
                    for h in range(2):
                        dve.wait_ge(k_hi_done, j * 2 + (h + 1))
                        r = slice(h * DH, (h + 1) * DH)
                        for o in range(2):
                            ins = dve.tensor_tensor(k_lo[o * DH:(o + 1) * DH, h, :], tile[1][r, 0:SC],
                                                    k_hi[r, h, :].bitcast(F32), ALU.subtract)
                        ins.then_inc(k_lo_done, 1)

                def top(i, s):
                    dve.wait_ge(scores, i * 16 + (s + 1))
                    dve.tensor_reduce(neg_max[:, s % 8:s % 8 + 1], tile[s % 2][:, 0:SC], AX.X, ALU.max,
                                      negate=True).then_inc(maxed, 1)

                def invert(i, s):
                    dve.wait_ge(exped, i * 16 + (s + 1))
                    dve.reciprocal(recip[:, s % 8:s % 8 + 1], sums[:, s % 8:s % 8 + 1]).then_inc(recips, 1)

                def scale(i, s):
                    dve.wait_ge(recips, i * 16 + (s + 1))
                    dve.tensor_scalar(probs[:, s % 8, :], probs[:, s % 8, :], recip[:, s % 8:s % 8 + 1], None,
                                      ALU.mult).then_inc(scaled, 1)

                def copy_pT(i, g, c):
                    dve.wait_ge(p_turned, i * G * KC + (g * KC + c + 1))
                    dve.tensor_copy(pT[0:chunk(c), c % 2, :], turn[0:chunk(c), :]).then_inc(pT_odd, 1)

                def add(i, g):
                    dve.wait_ge(y_made, i * G + (g + 1))
                    dst = x_sb[:, bass.ds((i // PAIRS) * TB + 2 * g, 2), :]
                    dve.tensor_tensor(dst, dst, turn[:, :].rearrange("p (t d) -> p t d", d=D), ALU.add).then_inc(y_added, 1)

                def round_(i, last):
                    top(i, 0)
                    for s in range(1, 4):
                        top(i, s)
                        invert(i, s - 1)
                        if s > 1:
                            scale(i, s - 2)
                    scale(i, 2)
                    invert(i, 3)
                    scale(i, 3)
                    for g in range(G):
                        s = 4 * (g + 1)
                        for n, c in enumerate(range(1, KC, 2)):
                            if g < G - 1:
                                if n < 4:
                                    top(i, s + n)
                                if 1 <= n <= 4:
                                    invert(i, s + n - 1)
                                if n == 4:
                                    scale(i, s + 3)
                            elif not last and n == 0:
                                q_low(i + 1)
                            elif not last and n == 2:
                                k_low(i + 1)
                            copy_pT(i, g, c)
                            if g < G - 1 and 1 <= n < 4:
                                scale(i, s + n - 1)
                        if due(i * G + g):
                            dve.wait_ge(y_added, i * G + g)
                        add(i, g)

                q_low(0)
                k_low(0)
                round_(0, False)
                with dve.Fori(1, ROUNDS - 1) as i:
                    round_(i, False)
                round_(ROUNDS - 1, True)


E0, H0, CAP0 = 16, 512, 640
SLOTS0 = E0 * CAP0
NEG = -3.0e38
HC = H0 // P
NT0 = CAP0 // P


def normalise(nc, x_sb, ident, xh, xl, rows, gate, E, logits, tag=""):
    GT = 4
    NG = TT // GT
    places = xh.shape[2] // (GT * P)
    with ExitStack() as ctx:
        sb = lambda n, s, d=F32: ctx.enter_context(nc.sbuf_tensor(tag + n, s, d))
        sem = lambda n: ctx.enter_context(nc.semaphore(tag + n))
        stats = sb("ln_stats", [P, TT, 6])
        mv = sb("ln_mean_var", [P, TT, 2])
        ve, root, inv, tmp = (sb(f"ln_{n}", [P, TT]) for n in ("ve", "root", "inv", "tmp"))
        xn = sb("ln_rows", [P, 2, GT, D])
        pt = [ctx.enter_context(nc.psum_tensor(f"{tag}ln_T{i}", [P, 512], F32)) for i in range(4)]
        pl = [ctx.enter_context(nc.psum_tensor(f"{tag}ln_L{i}", [P, 512], F32)) for i in range(2)]
        dve_step, var_ready, root_done = sem("ln_dve_step"), sem("ln_var_ready"), sem("ln_root_done")
        rows_ready = sem("ln_rows_ready")
        turned = sem("ln_turned")
        hi_done = sem("ln_hi_done")
        lo_done = sem("ln_lo_done")
        stored = sem("ln_rows_stored")
        gate_loaded, gate_hi, gate_lo = sem("gate_loaded"), sem("gate_hi"), sem("gate_lo")
        multiplied = sem("logits_multiplied")
        summed = sem("logits_summed")
        if gate is not None:
            g32 = sb("gate32", [P, KD, E])
            g2 = sb("gate_halves", [P, KD, 2, E], F32R)

        with nc.Block() as block:
            @block.sync
            def _(sp):
                if gate is not None:
                    sp.dma_start(g32[:, :, :], gate.rearrange("(k p) e -> p k e", p=P)).then_inc(gate_loaded, 16)
                if rows is not None:
                    r = rows.rearrange("(g t p) d -> g p t d", p=P, t=GT)
                    for g in range(NG):
                        sp.wait_ge(rows_ready, g + 1)
                        if g:
                            sp.wait_ge(stored, 16 * g)
                        sp.dma_start(r[g], xn[:, g % 2]).then_inc(stored, 16)
                    sp.wait_ge(stored, 16 * NG)

            @block.vector
            def _(dve):
                step = Steps(dve, dve_step)
                for t in range(TT):
                    step.done(dve.bn_stats(stats[:, t, :], x_sb[:, t, :]))
                step.wait()
                for t in range(TT):
                    step.done(dve.bn_aggr(mv[:, t, :], stats[:, t, :]))
                step.wait()
                dve.tensor_scalar(ve[:, :], mv[:, :, 1], EPS, None, ALU.add).then_inc(var_ready, 1)
                inverse_root(None, dve, step, root_done, ve[:, :], root[:, :], inv[:, :], tmp[:, :], 1)
                if gate is not None:
                    dve.wait_ge(gate_loaded, 16)
                    dve.wait_ge(gate_hi, 1)
                    dve.tensor_tensor(g2[:, :, 1, :], g32[:, :, :], g2[:, :, 0, :].bitcast(F32), ALU.subtract).then_inc(gate_lo, 1)
                for g in range(NG + 2):
                    if g < NG:
                        if g >= 2:
                            dve.wait_ge(turned, g - 1)
                            if rows is not None:
                                dve.wait_ge(stored, 16 * (g - 1))
                        for j in range(GT):
                            t = g * GT + j
                            ins = dve.tensor_scalar(xn[:, g % 2, j, :], x_sb[:, t, :], mv[:, t, 0:1], inv[:, t:t + 1],
                                                    ALU.subtract, ALU.mult)
                        ins.then_inc(rows_ready, 1)
                    if 1 <= g <= NG:
                        dve.wait_ge(hi_done, g)
                        for k in range(KD):
                            c = slice((g - 1) % places * 512, ((g - 1) % places + 1) * 512)
                            ins = dve.tensor_tensor(xl[:, k, c], pt[(g - 1) % 2 * 2 + k][:, :], xh[:, k, c].bitcast(F32), ALU.subtract)
                        ins.then_inc(lo_done, 1)
                    if gate is not None and g >= 2:
                        dve.wait_ge(multiplied, g - 1)
                        dve.tensor_reduce(logits[:, (g - 2) * GT:(g - 1) * GT, :],
                                          pl[g % 2][:, 0:GT * 2 * E].rearrange("p (t h e) -> p t e h", t=GT, h=2),
                                          AX.X, ALU.add).then_inc(summed, 1)

            @block.scalar
            def _(act):
                if gate is not None:
                    act.wait_ge(gate_loaded, 16)
                    act.activation(g2[:, :, 0, :], g32[:, :, :], ACT.Copy).then_inc(gate_hi, 1)
                act.wait_ge(var_ready, 1)
                inverse_root(act, None, None, root_done, ve[:, :], root[:, :], None, None, 0)
                for g in range(NG):
                    act.wait_ge(turned, g + 1)
                    for k in range(KD):
                        ins = act.activation(xh[:, k, g % places * 512:(g % places + 1) * 512], pt[g % 2 * 2 + k][:, :], ACT.Copy)
                    ins.then_inc(hi_done, 1)

            @block.tensor
            def _(pe):
                def multiply(g):
                    pe.wait_ge(lo_done, g + 1)
                    pe.wait_ge(hi_done, g + 1)
                    if g == 0:
                        pe.wait_ge(gate_lo, 1)
                        pe.wait_ge(gate_hi, 1)
                    if g >= 2:
                        pe.wait_ge(summed, g - 1)
                    for j in range(GT):
                        c = slice((g % places * GT + j) * P, (g % places * GT + j + 1) * P)
                        n = 0
                        for half in (xh, xl):
                            for k in range(KD):
                                ins = pe.matmul(pl[g % 2][:, j * 2 * E:(j + 1) * 2 * E], half[:, k, c],
                                                g2[:, k, :, :].rearrange("p h e -> p (h e)"), start=n == 0, stop=n == 3)
                                n += 1
                    ins.then_inc(multiplied, 1)

                for g in range(NG):
                    pe.wait_ge(rows_ready, g + 1)
                    if g >= 2:
                        pe.wait_ge(hi_done, g - 1)
                        pe.wait_ge(lo_done, g - 1)
                    for k in range(KD):
                        for j in range(GT):
                            ins = pe.transpose(pt[g % 2 * 2 + k][:, j * P:(j + 1) * P], xn[:, g % 2, j, k * P:(k + 1) * P], ident[:, :])
                    ins.then_inc(turned, 1)
                    if gate is not None and g:
                        multiply(g - 1)
                if gate is not None:
                    multiply(NG - 1)


def choose(nc, cst, key, E, cap, chosen, rank, tag="", weights=None):
    W = E * TT
    with ExitStack() as ctx:
        sb = lambda n, s, d=F32: ctx.enter_context(nc.sbuf_tensor(tag + n, s, d))
        sem = lambda n: ctx.enter_context(nc.semaphore(tag + n))
        thr = sb("threshold", [P, E], I32)
        cand = sb("candidate", [P, E], I32)
        change = sb("kept_bit", [P, E], I32)
        part = sb("count_part", [P, E])
        above = sb("count_above", [P, E])
        hit = sb("at_least", [P, E, TT])
        a = sb("prefix_sum", [P, E, TT])
        tot = [ctx.enter_context(nc.psum_tensor(f"{tag}total{j}", [P, 512], F32)) for j in range(2)]
        within = ctx.enter_context(nc.psum_tensor(tag + "within", [P, 512], F32))
        tiles = ctx.enter_context(nc.psum_tensor(tag + "tile_totals", [P, 512], F32))
        dve_step = sem("choose_step")
        counted = sem("choose_counted")
        totalled = sem("choose_totalled")
        bc = lambda t: t.rearrange("p (e t) -> p e t", t=1).broadcast_to([P, E, TT])
        flat = lambda t: t.rearrange("p e t -> p (e t)")

        with nc.Block() as block:
            if weights is not None:
                @block.sync
                def _(sp):
                    weights.load(sp)

                @block.scalar
                def _(act):
                    weights.high(act)

                @block.gpsimd
                def _(pool):
                    weights.low(pool)

            @block.vector
            def _(dve):
                step = Steps(dve, dve_step)
                step.then(dve.memset(thr[:, :], -1))
                PER = 5
                with dve.Fori(0, 32) as i:
                    s = Steps(dve, dve_step, i, PER, 1)
                    dve.wait_ge(dve_step, i * PER + 1)
                    s.then(dve.tensor_tensor(cand[:, :], thr[:, :], cst["bits"][:, bass.ds(i, 1)].broadcast_to([P, E]), ALU.bitwise_xor))
                    s.then(dve.tensor_tensor(hit[:, :, :], key[:, :, :], bc(cand[:, :].bitcast(F32)), ALU.is_ge))
                    s.then(dve.tensor_reduce(part[:, :], hit[:, :, :], AX.X, ALU.add))
                    dve.wait_ge(totalled, i + 1)
                    s.then(dve.scalar_tensor_tensor(out=change[:, :], in0=tot[0][:, 0:E], scalar=cap - 0.5,
                                                    in1=cst["bits"][:, bass.ds(i, 1)].broadcast_to([P, E]), op0=ALU.is_ge, op1=ALU.mult))
                    s.then(dve.tensor_tensor(thr[:, :], thr[:, :], change[:, :], ALU.bitwise_xor))
                    assert s.n == PER
                step = Steps(dve, dve_step, base=1 + 32 * PER)
                thr_f = bc(thr[:, :].bitcast(F32))
                step.then(dve.tensor_tensor(chosen[:, :, :], key[:, :, :], thr_f, ALU.is_gt))
                step.then(dve.tensor_reduce(part[:, :], chosen[:, :, :], AX.X, ALU.add))
                step.then(dve.tensor_tensor(hit[:, :, :], key[:, :, :], thr_f, ALU.is_equal))
                step.then(dve.tensor_scalar(rank[:, :, :], key[:, :, :], NEG, None, ALU.is_gt))
                step.then(dve.tensor_tensor(hit[:, :, :], hit[:, :, :], rank[:, :, :], ALU.mult))
                dve.tensor_copy(rank[:, :, :], hit[:, :, :]).then_inc(counted, 1)

                def prefix(n):
                    dve.wait_ge(totalled, 32 + n)
                    step.then(dve.tensor_copy(a[:, :, :], tiles[:, 0:W].rearrange("p (e t) -> p e t", t=TT)))
                    step.then(dve.tensor_tensor_scan(flat(rank[:, :, :]), cst["keep"][:, 0:W], flat(a[:, :, :]), 0.0, ALU.mult, ALU.add))
                    step.then(dve.tensor_tensor(rank[:, :, :], rank[:, :, :], a[:, :, :], ALU.subtract))
                    step.then(dve.tensor_tensor(rank[:, :, :], rank[:, :, :], within[:, 0:W].rearrange("p (e t) -> p e t", t=TT), ALU.add))

                prefix(1)
                step.then(dve.tensor_scalar(above[:, :], tot[1][:, 0:E], -1.0, float(cap), ALU.mult, ALU.add))
                step.then(dve.tensor_tensor(rank[:, :, :], rank[:, :, :], bc(above[:, :]), ALU.is_lt))
                step.then(dve.tensor_tensor(rank[:, :, :], rank[:, :, :], hit[:, :, :], ALU.mult))
                dve.tensor_tensor(chosen[:, :, :], chosen[:, :, :], rank[:, :, :], ALU.add).then_inc(counted, 1)
                prefix(2)

            @block.tensor
            def _(pe):
                with pe.Fori(0, 32) as i:
                    pe.wait_ge(dve_step, i * 5 + 4)
                    pe.matmul(tot[0][:, 0:E], cst["ones"][:, :], part[:, :], start=True, stop=True).then_inc(totalled, 1)
                pe.wait_ge(counted, 1)
                pe.matmul(tot[1][:, 0:E], cst["ones"][:, :], part[:, :], start=True, stop=True)
                pe.matmul(within[:, 0:W], cst["before"][:, :], flat(rank[:, :, :]), start=True, stop=True)
                pe.matmul(tiles[:, 0:W], cst["ones"][:, :], flat(rank[:, :, :]), start=True, stop=True).then_inc(totalled, 1)
                pe.wait_ge(counted, 2)
                pe.matmul(within[:, 0:W], cst["before"][:, :], flat(chosen[:, :, :]), start=True, stop=True)
                pe.matmul(tiles[:, 0:W], cst["ones"][:, :], flat(chosen[:, :, :]), start=True, stop=True).then_inc(totalled, 1)


def constants(nc, ctx):
    sb = lambda n, s, d=F32: ctx.enter_context(nc.sbuf_tensor(n, s, d))
    cst = {"ones": sb("ones", [P, P]), "before": sb("before", [P, P]), "bits": sb("bits", [P, 32], I32),
           "keep": sb("keep", [P, 512]), "keep_e": sb("keep_e", [P, 512]), "token": sb("token", [P, TT], I32),
           "zero": sb("zero_ids", [P, 80], I32),
           "keep_8": sb("keep_8", [P, 256]), "tile_no": sb("tile_no", [P, 64])}
    made = ctx.enter_context(nc.semaphore("constants_made"))
    with nc.Block() as block:
        @block.gpsimd
        def _(pool):
            for name in ("ones", "before", "keep", "keep_e", "keep_8"):
                pool.memset(cst[name][:, :], 1.0).then_inc(made, 1)
            pool.wait_ge(made, 5)
            pool.affine_select(out=cst["before"][:, :], in_=cst["before"][:, :], compare_op=ALU.is_gt, fill=0.0, base=0,
                               pattern=[[1, P]], channel_multiplier=-1)
            pool.memset(cst["keep"][:, :].rearrange("p (e t) -> p e t", t=TT)[:, :, 0:1], 0.0)
            pool.memset(cst["keep_e"][:, :].rearrange("p (t e) -> p t e", e=E0)[:, :, 0:1], 0.0)
            for i in range(32):
                pool.memset(cst["bits"][:, i:i + 1], -1 if i == 0 else 1 << (31 - i))
            pool.memset(cst["keep_8"][:, :].rearrange("p (t e) -> p t e", e=8)[:, :, 0:1], 0.0)
            pool.iota(cst["tile_no"][:, :], pattern=[[1, 64]], base=0, channel_multiplier=0, allow_small_or_imprecise_dtypes=True)
            pool.memset(cst["zero"][:, :], 0)
            pool.iota(cst["token"][:, :], pattern=[[P, TT]], base=0, channel_multiplier=1).then_inc(made, 1)
            pool.wait_ge(made, 6)
    return cst


def slot_arrays(nc, ctx, J, tag=""):
    sb = lambda n, d: ctx.enter_context(nc.sbuf_tensor(tag + n, [P, J, TT], d))
    return {"scatter": sb("slot_or_beyond", I32), "slot": sb("slot_or_zero", I32), "weight": sb("slot_weight", F32)}


def route0(nc, io, cst, logits, r):
    with ExitStack() as c1:
        sb = lambda n, s, d=F32: c1.enter_context(nc.sbuf_tensor(n, s, d))
        sem = lambda n: c1.enter_context(nc.semaphore(n))
        first = sb("first_expert", [P, TT, E0])
        second = sb("second_expert", [P, TT, E0])
        key = sb("router_key", [P, E0, TT])
        chosen = sb("chosen", [P, E0, TT])
        rank = sb("slot_rank", [P, E0, TT])
        with ExitStack() as c2:
            sb2 = lambda n, s, d=F32: c2.enter_context(nc.sbuf_tensor(n, s, d))
            sc = sb2("scores", [P, TT, E0])
            eq = sb2("score_is_max", [P, TT, E0])
            pre = sb2("score_prefix", [P, TT, E0])
            m = sb2("score_max", [P, TT])
            gb = sb2("gate_b_sb", [P, E0])
            step_s, exped, loaded = sem("route_step"), sem("route_exp"), sem("gate_b_loaded")
            over_e = lambda t: t.rearrange("p (t e) -> p t e", e=1).broadcast_to([P, TT, E0])
            flat = lambda t: t.rearrange("p t e -> p (t e)")
            with nc.Block() as block:
                @block.sync
                def _(sp):
                    sp.dma_start(gb[:, :], io["L0_ffn_gate_b"].rearrange("(o e) -> o e", o=1).broadcast_to([P, E0])).then_inc(loaded, 16)

                @block.vector
                def _(dve):
                    step = Steps(dve, step_s)
                    step.then(dve.tensor_reduce(m[:, :], logits[:, :, :], AX.X, ALU.max))
                    step.then(dve.tensor_tensor(sc[:, :, :], logits[:, :, :], over_e(m[:, :]), ALU.subtract))
                    dve.wait_ge(exped, 1)
                    step.then(dve.tensor_reduce(m[:, :], sc[:, :, :], AX.X, ALU.add))
                    step.then(dve.reciprocal(m[:, :], m[:, :]))
                    step.then(dve.tensor_tensor(sc[:, :, :], sc[:, :, :], over_e(m[:, :]), ALU.mult))
                    dve.wait_ge(loaded, 16)
                    step.then(dve.tensor_tensor(sc[:, :, :], sc[:, :, :],
                                                gb[:, :].rearrange("p (t e) -> p t e", t=1).broadcast_to([P, TT, E0]), ALU.add))
                    for pick in (first, second):
                        step.then(dve.tensor_reduce(m[:, :], sc[:, :, :], AX.X, ALU.max))
                        step.then(dve.tensor_tensor(eq[:, :, :], sc[:, :, :], over_e(m[:, :]), ALU.is_equal))
                        step.then(dve.tensor_tensor_scan(flat(pre[:, :, :]), cst["keep_e"][:, :], flat(eq[:, :, :]), 0.0, ALU.mult, ALU.add))
                        step.then(dve.tensor_scalar(pre[:, :, :], pre[:, :, :], 1.0, None, ALU.is_equal))
                        step.then(dve.tensor_tensor(pick[:, :, :], pre[:, :, :], eq[:, :, :], ALU.mult))
                        if pick is first:
                            step.then(dve.tensor_scalar(eq[:, :, :], first[:, :, :], NEG, None, ALU.mult))
                            step.then(dve.tensor_tensor(sc[:, :, :], sc[:, :, :], eq[:, :, :], ALU.add))
                    step.then(dve.tensor_tensor(eq[:, :, :], first[:, :, :], second[:, :, :], ALU.add))
                    step.then(dve.tensor_tensor(sc[:, :, :], eq[:, :, :], logits[:, :, :], ALU.mult))
                    step.then(dve.tensor_scalar(eq[:, :, :], eq[:, :, :], 1.0, -NEG, ALU.subtract, ALU.mult))
                    step.then(dve.tensor_tensor(key[:, :, :].rearrange("p e t -> p t e"), sc[:, :, :], eq[:, :, :], ALU.add))

                @block.scalar
                def _(act):
                    act.wait_ge(step_s, 2)
                    act.activation(sc[:, :, :], sc[:, :, :], ACT.Exp).then_inc(exped, 1)

        choose(nc, cst, key, E0, CAP0, chosen, rank)
        with ExitStack() as c2:
            sb2 = lambda n, s, d=F32: c2.enter_context(nc.sbuf_tensor(n, s, d))
            t1 = sb2("pick_chosen", [P, TT, E0])
            t2 = sb2("pick_value", [P, TT, E0])
            kept = sb2("kept", [P, 2, TT])
            slot = sb2("slot_f32", [P, 2, TT])
            step_s = sem("slots_step")
            te = lambda t: t[:, :, :].rearrange("p e t -> p t e")
            with nc.Block() as block:
                @block.vector
                def _(dve):
                    step = Steps(dve, step_s)
                    for e in range(E0):
                        ins = dve.tensor_scalar(rank[:, e, :], rank[:, e, :], float(e * CAP0), None, ALU.add)
                        step.done(ins)
                    step.wait()
                    for j, pick in enumerate((first, second)):
                        step.then(dve.tensor_tensor(t1[:, :, :], pick[:, :, :], te(chosen), ALU.mult))
                        step.then(dve.tensor_reduce(kept[:, j, :], t1[:, :, :], AX.X, ALU.add))
                        step.then(dve.tensor_tensor(t2[:, :, :], t1[:, :, :], logits[:, :, :], ALU.mult))
                        step.then(dve.tensor_reduce(r["weight"][:, j, :], t2[:, :, :], AX.X, ALU.add))
                        step.then(dve.tensor_tensor(t2[:, :, :], t1[:, :, :], te(rank), ALU.mult))
                        step.then(dve.tensor_reduce(slot[:, j, :], t2[:, :, :], AX.X, ALU.add))
                    step.then(dve.tensor_copy(r["slot"][:, :, :], slot[:, :, :]))
                    step.then(dve.tensor_scalar(kept[:, :, :], kept[:, :, :], -1.0, -2.0 * SLOTS0, ALU.add, ALU.mult))
                    step.then(dve.tensor_tensor(kept[:, :, :], kept[:, :, :], slot[:, :, :], ALU.add))
                    step.then(dve.tensor_copy(r["scatter"][:, :, :], kept[:, :, :]))


def matmul3(pe, out, w_hi, w_lo, x_hi, x_lo, first, last):
    pe.matmul(out, w_hi, x_hi, start=first, stop=False)
    pe.matmul(out, w_hi, x_lo, start=False, stop=False)
    return pe.matmul(out, w_lo, x_hi, start=False, stop=last)


def expert_weights(io, names, e):
    return [io[n][e].rearrange("(c p) h -> p c h", p=P) for n in names]


def shared_experts(nc, io, cst, x_sb, xh, xl, table, ids, scatter, sw):
    NB = TOK // 512
    NE = 2
    with ExitStack() as ctx:
        sb = lambda n, s, d=F32: ctx.enter_context(nc.sbuf_tensor(n, s, d))
        sem = lambda n: ctx.enter_context(nc.semaphore(n))
        stage = sb("sh_stage", [P, 2, 1024])
        wh = sb("sh_w_hi", [P, NE, 3, 1024], F32R)
        wl = sb("sh_w_lo", [P, NE, 3, 1024], F32R)
        sg = sb("sh_gated", [P, HC, 512])
        gh = sb("sh_g_hi", [P, HC, 512], F32R)
        gl = sb("sh_g_lo", [P, HC, 512], F32R)
        hb = [ctx.enter_context(nc.psum_tensor(f"sh_h{i}", [P, 2, 512], F32)) for i in range(2)]
        yb = [ctx.enter_context(nc.psum_tensor(f"sh_y{i}", [P, 512], F32)) for i in range(4)]
        loaded = [sem(f"sh_loaded{i}") for i in range(2)]
        w_hi, w_lo = sem("sh_w_hi_done"), sem("sh_w_lo_done")
        h_made = sem("sh_h_made")
        silu = sem("sh_silu")
        gated = sem("sh_gated_done")
        g_hi, g_lo = sem("sh_g_hi_done"), sem("sh_g_lo_done")
        y_made = sem("sh_y_made")
        y_added = sem("sh_y_added")
        zeroed, scattered, read = sw[0:3]

        with nc.Block() as block:
            @block.sync
            def _(sp):
                for e in range(NE):
                    for j, src in enumerate(expert_weights(io, ("L0_ffn_sw1", "L0_ffn_sw3", "L0_ffn_sw2"), e)):
                        n = e * 3 + j
                        if n >= 2:
                            sp.wait_ge(w_lo, n - 1)
                        sp.dma_start(stage[:, n % 2, :].rearrange("p (c h) -> p c h", h=src.shape[2]), src).then_inc(loaded[n % 2], 16)

            @block.gpsimd
            def _(pool):
                pool.dma_start(table.rearrange("(p c) o -> p (c o)", p=P), cst["zero"][:, 0:SLOTS0 // P]).then_inc(zeroed, 16)
                pool.wait_ge(zeroed, 16)
                for t in range(TT):
                    for j in range(2):
                        pool.indirect_dma_start(out=table, out_offset=bass.IndirectOffsetOnAxis(ap=scatter[:, j, t:t + 1].bitcast(U32), axis=0),
                                                in_=cst["token"][:, t:t + 1], in_offset=None, bounds_check=SLOTS0 - 1,
                                                oob_is_err=False).then_inc(scattered, 16)
                pool.wait_ge(scattered, 16 * 2 * TT)
                pool.dma_start(ids[:, :, :], table.rearrange("(e p j) o -> p e (j o)", p=P, j=NT0)).then_inc(read, 16)
                pool.wait_ge(read, 16)

            @block.scalar
            def _(act):
                for n in range(NE * 3):
                    act.wait_ge(loaded[n % 2], 16 * (n // 2 + 1))
                    act.activation(wh[:, n // 3, n % 3, :], stage[:, n % 2, :], ACT.Copy).then_inc(w_hi, 1)

                def g_high(u, m):
                    act.wait_ge(gated, u + 1)
                    act.activation(gh[:, m, :], sg[:, m, :], ACT.Copy).then_inc(g_hi, 1)

                def block_(q, first):
                    for m in range(HC):
                        u = q * HC + m
                        act.wait_ge(h_made, u + 1)
                        if not first:
                            act.wait_ge(g_lo, u - 3)
                        act.activation(sg[:, m, :], hb[m % 2][:, 0, :], ACT.Silu).then_inc(silu, 1)
                        if m or not first:
                            g_high(u - 1, (m - 1) % HC)

                block_(0, True)
                with act.Fori(1, NE * NB) as q:
                    block_(q, False)
                g_high(NE * NB * HC - 1, HC - 1)

            @block.vector
            def _(dve):
                for n in range(NE * 3):
                    dve.wait_ge(w_hi, n + 1)
                    dve.tensor_tensor(wl[:, n // 3, n % 3, :], stage[:, n % 2, :], wh[:, n // 3, n % 3, :].bitcast(F32),
                                      ALU.subtract).then_inc(w_lo, 1)

                def g_low(u, m):
                    dve.wait_ge(g_hi, u + 1)
                    dve.tensor_tensor(gl[:, m, :], sg[:, m, :], gh[:, m, :].bitcast(F32), ALU.subtract).then_inc(g_lo, 1)

                def add(q):
                    dve.wait_ge(y_made, q + 1)
                    for j in range(4):
                        dst = x_sb[:, bass.ds((q % NB) * 4 + j, 1), :].rearrange("p a d -> p (a d)")
                        ins = dve.scalar_tensor_tensor(out=dst, in0=yb[j][:, 0:D], scalar=1.0 / NE, in1=dst, op0=ALU.mult, op1=ALU.add)
                    ins.then_inc(y_added, 1)

                def block_(q, first):
                    for m in range(HC):
                        u = q * HC + m
                        if m == 1 and not first:
                            add(q - 1)
                        dve.wait_ge(silu, u + 1)
                        dve.tensor_tensor(sg[:, m, :], sg[:, m, :], hb[m % 2][:, 1, :], ALU.mult).then_inc(gated, 1)
                        if m or not first:
                            g_low(u - 1, (m - 1) % HC)

                block_(0, True)
                with dve.Fori(1, NE * NB) as q:
                    block_(q, False)
                g_low(NE * NB * HC - 1, HC - 1)
                add(NE * NB - 1)

            @block.tensor
            def _(pe):
                def hidden(e, q, m, wait=True):
                    u = q * HC + m
                    if wait:
                        pe.wait_ge(gated, u - 1)
                    x = bass.ds((q % NB) * 512, 512)
                    for w in range(2):
                        for k in range(KD):
                            c = slice(k * H0 + m * P, k * H0 + (m + 1) * P)
                            ins = matmul3(pe, hb[m % 2][:, w, :], wh[:, e, w, c], wl[:, e, w, c], xh[:, k, x], xl[:, k, x],
                                          k == 0, k == KD - 1)
                    ins.then_inc(h_made, 1)

                def back(e, q, m):
                    u = q * HC + m
                    pe.wait_ge(g_hi, u + 1)
                    pe.wait_ge(g_lo, u + 1)
                    if m == 0:
                        pe.wait_ge(y_added, q)
                    w = slice(m * D, (m + 1) * D)
                    for j in range(4):
                        c = slice(j * P, (j + 1) * P)
                        pe.matmul(yb[j][:, 0:D], gh[:, m, c], wh[:, e, 2, w], start=m == 0, stop=False)
                        pe.matmul(yb[j][:, 0:D], gh[:, m, c], wl[:, e, 2, w], start=False, stop=False)
                        ins = pe.matmul(yb[j][:, 0:D], gl[:, m, c], wh[:, e, 2, w], start=False, stop=m == HC - 1)
                    if m == HC - 1:
                        ins.then_inc(y_made, 1)

                def block_(e, q, then):
                    for m in range(HC):
                        if m < HC - 1:
                            hidden(e, q, m + 1, wait=m > 0 or not isinstance(q, int) or q > 0)
                        elif then is not None:
                            hidden(then, q + 1, 0)
                        back(e, q, m)

                pe.wait_ge(w_hi, NE * 3)
                pe.wait_ge(w_lo, NE * 3)
                hidden(0, 0, 0, wait=False)
                block_(0, 0, 0)
                with pe.Fori(1, NB - 1) as q:
                    block_(0, q, 0)
                block_(0, NB - 1, 1)
                with pe.Fori(NB, 2 * NB - 1) as q:
                    block_(1, q, 1)
                block_(1, 2 * NB - 1, None)


def routed_experts(nc, io, ident, xn_rows, ids, y_rows, sw):
    BL = [(0, 2), (2, 3)]
    U = 2 * HC
    TG = [(0, 2), (2, 2), (4, 1)]
    names = ("L0_ffn_ew1", "L0_ffn_ew3", "L0_ffn_ew2")
    with ExitStack() as ctx:
        sb = lambda n, s, d=F32: ctx.enter_context(nc.sbuf_tensor(n, s, d))
        sem = lambda n: ctx.enter_context(nc.semaphore(n))
        stage = sb("ex_stage", [P, 3, 1024])
        wh = sb("ex_w_hi", [P, 2, 3, 1024], F32R)
        wl = sb("ex_w_lo", [P, 2, 3, 1024], F32R)
        xr = sb("ex_rows", [P, 2, NT0, D])
        xh = sb("ex_x_hi", [P, 2, KD, CAP0], F32R)
        xl = sb("ex_x_lo", [P, 2, KD, CAP0], F32R)
        sg = sb("ex_gated", [P, HC, 384])
        gh = sb("ex_g_hi", [P, HC, 384], F32R)
        gl = sb("ex_g_lo", [P, HC, 384], F32R)
        ys = sb("ex_y", [P, 2, NT0, D])
        hb = [ctx.enter_context(nc.psum_tensor(f"ex_h{i}", [P, 2, 512], F32)) for i in range(2)]
        yb = [ctx.enter_context(nc.psum_tensor(f"ex_yb{i}", [P, 512], F32)) for i in range(3)]
        tb = ctx.enter_context(nc.psum_tensor("ex_tb", [P, 512], F32))
        loaded = [sem(f"ex_loaded{j}") for j in range(3)]
        w_hi, w_lo = sem("ex_w_hi_done"), sem("ex_w_lo_done")
        gathered = sw[3:5]
        turned = sem("ex_turned")
        x_hi, x_lo = sem("ex_x_hi_done"), sem("ex_x_lo_done")
        h_made, silu, gated = sem("ex_h_made"), sem("ex_silu"), sem("ex_gated_done")
        g_hi, g_lo = sem("ex_g_hi_done"), sem("ex_g_lo_done")
        y_made, y_copied = sem("ex_y_made"), sem("ex_y_copied")
        stored = sw[5:7]

        def width(v):
            return BL[v // HC][1] * P

        with nc.Block() as block:
            @block.sync
            def _(sp):
                def load(e, first):
                    for j, src in enumerate(expert_weights(io, names, 0)):
                        if not first:
                            sp.wait_ge(w_lo, (e - 1) * 3 + (j + 1))
                        full = io[names[j]].rearrange("e (c p) h -> p e c h", p=P)
                        s = full[:, 0] if first else full[:, bass.ds(e, 1)].rearrange("p a c h -> p (a c) h")
                        sp.dma_start(stage[:, j, :].rearrange("p (c h) -> p c h", h=src.shape[2]), s).then_inc(loaded[j], 16)

                load(0, True)
                with sp.Fori(1, E0) as e:
                    load(e, False)

            @block.gpsimd
            def _(pool):
                def gather(e):
                    for j in range(NT0):
                        pool.indirect_dma_start(out=xr[:, e % 2, j, :], out_offset=None, in_=xn_rows,
                                                in_offset=bass.IndirectOffsetOnAxis(ap=ids[:, e, j:j + 1].bitcast(U32), axis=0)
                                                ).then_inc(gathered[e % 2], 16)

                y_t = y_rows.rearrange("(e p j) d -> e p j d", p=P, j=NT0)
                gather(0)
                gather(1)
                pool.wait_ge(turned, 3)
                gather(2)
                for e in range(E0):
                    if e + 3 < E0:
                        pool.wait_ge(turned, 3 * (e + 2))
                        gather(e + 3)
                    pool.wait_ge(y_copied, 2 * (e + 1))
                    pool.dma_start(y_t[e], ys[:, e % 2]).then_inc(stored[e % 2], 16)
                for j in range(2):
                    pool.wait_ge(stored[j], 16 * (E0 // 2))

            def tile_view(t, par, g):
                a, n = TG[g]
                return t[:, par, :, a * P:(a + n) * P]

            def turned_view(g):
                n = TG[g][1] * P
                return tb[:, 0:KD * n].rearrange("p (k c) -> p k c", k=KD)

            @block.scalar
            def _(act):
                def w_high(e, par, j):
                    act.wait_ge(loaded[j], e * 16 + 16)
                    act.activation(wh[:, par, j, :], stage[:, j, :], ACT.Copy).then_inc(w_hi, 1)

                def x_high(e, par, g):
                    act.wait_ge(turned, e * 3 + (g + 1))
                    act.activation(tile_view(xh, par, g), turned_view(g), ACT.Copy).then_inc(x_hi, 1)

                def g_high(u, v):
                    act.wait_ge(gated, u + 1)
                    act.activation(gh[:, v % HC, 0:width(v)], sg[:, v % HC, 0:width(v)], ACT.Copy).then_inc(g_hi, 1)

                def copy_y(e, par, b):
                    act.wait_ge(y_made, e * 2 + (b + 1))
                    if b == 0:
                        act.wait_ge(stored[par], (e // 2) * 16)
                    for j in range(BL[b][1]):
                        ins = act.activation(ys[:, par, BL[b][0] + j, :], yb[j][:, 0:D], ACT.Copy)
                    ins.then_inc(y_copied, 1)

                def expert(e, par, first, last):
                    for v in range(U):
                        u = e * U + v
                        if v == 1 and not first:
                            copy_y(e - 1, 1 - par, 1)
                        if v == HC + 1:
                            copy_y(e, par, 0)
                        act.wait_ge(h_made, u + 1)
                        if not (first and v < HC):
                            act.wait_ge(g_lo, u - 3)
                        act.activation(sg[:, v % HC, 0:width(v)], hb[v % 2][:, 0, 0:width(v)], ACT.Silu).then_inc(silu, 1)
                        if v or not first:
                            g_high(u - 1, (v - 1) % U)
                        if not last and v in (1, 3, 5):
                            w_high(e + 1, 1 - par, v // 2)
                        if not last and v in (2, 4, 6):
                            x_high(e + 1, 1 - par, v // 2 - 1)

                for g in range(3):
                    w_high(0, 0, g)
                for g in range(3):
                    x_high(0, 0, g)
                expert(0, 0, True, False)
                expert(1, 1, False, False)
                with act.Fori(1, E0 // 2 - 1) as i:
                    for par in range(2):
                        expert(i * 2 + par, par, False, False)
                expert(E0 - 2, 0, False, False)
                expert(E0 - 1, 1, False, True)
                g_high(E0 * U - 1, U - 1)
                copy_y(E0 - 1, 1, 1)

            @block.vector
            def _(dve):
                def w_low(e, par, j):
                    dve.wait_ge(w_hi, e * 3 + (j + 1))
                    dve.tensor_tensor(wl[:, par, j, :], stage[:, j, :], wh[:, par, j, :].bitcast(F32), ALU.subtract).then_inc(w_lo, 1)

                def x_low(e, par, g):
                    dve.wait_ge(x_hi, e * 3 + (g + 1))
                    dve.tensor_tensor(tile_view(xl, par, g), turned_view(g), tile_view(xh, par, g).bitcast(F32),
                                      ALU.subtract).then_inc(x_lo, 1)

                def g_low(u, v):
                    dve.wait_ge(g_hi, u + 1)
                    w = slice(0, width(v))
                    dve.tensor_tensor(gl[:, v % HC, w], sg[:, v % HC, w], gh[:, v % HC, w].bitcast(F32), ALU.subtract).then_inc(g_lo, 1)

                def expert(e, par, first, last):
                    for v in range(U):
                        u = e * U + v
                        w = slice(0, width(v))
                        dve.wait_ge(silu, u + 1)
                        dve.tensor_tensor(sg[:, v % HC, w], sg[:, v % HC, w], hb[v % 2][:, 1, w], ALU.mult).then_inc(gated, 1)
                        if v or not first:
                            g_low(u - 1, (v - 1) % U)
                        if not last and v in (1, 3, 5):
                            w_low(e + 1, 1 - par, v // 2)
                        if not last and v in (2, 4, 6):
                            x_low(e + 1, 1 - par, v // 2 - 1)

                for g in range(3):
                    w_low(0, 0, g)
                for g in range(3):
                    x_low(0, 0, g)
                expert(0, 0, True, False)
                expert(1, 1, False, False)
                with dve.Fori(1, E0 // 2 - 1) as i:
                    for par in range(2):
                        expert(i * 2 + par, par, False, False)
                expert(E0 - 2, 0, False, False)
                expert(E0 - 1, 1, False, True)
                g_low(E0 * U - 1, U - 1)

            @block.tensor
            def _(pe):
                def turn(e, par, g, first=False):
                    if g == 0:
                        pe.wait_ge(gathered[par], (e // 2) * (16 * NT0) + 16 * NT0)
                    if not (first and g == 0):
                        pe.wait_ge(x_lo, e * 3 + g)
                        pe.wait_ge(x_hi, e * 3 + g)
                    a, n = TG[g]
                    for k in range(KD):
                        for j in range(n):
                            ins = pe.transpose(tb[:, (k * n + j) * P:(k * n + j + 1) * P], xr[:, par, a + j, k * P:(k + 1) * P], ident[:, :])
                    ins.then_inc(turned, 1)

                def hidden(e, par, v, wait=True):
                    u = e * U + v
                    if v == 0:
                        for s in (w_hi, w_lo, x_hi, x_lo):
                            pe.wait_ge(s, e * 3 + 3)
                    if wait:
                        pe.wait_ge(gated, u - 1)
                    a, n = BL[v // HC]
                    x = slice(a * P, (a + n) * P)
                    m = v % HC
                    for w in range(2):
                        for k in range(KD):
                            c = slice(k * H0 + m * P, k * H0 + (m + 1) * P)
                            ins = matmul3(pe, hb[v % 2][:, w, 0:n * P], wh[:, par, w, c], wl[:, par, w, c],
                                          xh[:, par, k, x], xl[:, par, k, x], k == 0, k == KD - 1)
                    ins.then_inc(h_made, 1)

                def back(e, par, v):
                    u = e * U + v
                    pe.wait_ge(g_hi, u + 1)
                    pe.wait_ge(g_lo, u + 1)
                    m = v % HC
                    if m == 0:
                        pe.wait_ge(y_copied, e * 2 + v // HC)
                    w = slice(m * D, (m + 1) * D)
                    for j in range(BL[v // HC][1]):
                        c = slice(j * P, (j + 1) * P)
                        pe.matmul(yb[j][:, 0:D], gh[:, m, c], wh[:, par, 2, w], start=m == 0, stop=False)
                        pe.matmul(yb[j][:, 0:D], gh[:, m, c], wl[:, par, 2, w], start=False, stop=False)
                        ins = pe.matmul(yb[j][:, 0:D], gl[:, m, c], wh[:, par, 2, w], start=False, stop=m == HC - 1)
                    if m == HC - 1:
                        ins.then_inc(y_made, 1)

                def expert(e, par, first, last):
                    for v in range(U):
                        if v < U - 1:
                            hidden(e, par, v + 1, wait=not (first and v == 0))
                        elif not last:
                            hidden(e + 1, 1 - par, 0)
                        if not last and v in (1, 3, 5):
                            turn(e + 1, 1 - par, v // 2)
                        back(e, par, v)

                for g in range(3):
                    turn(0, 0, g, True)
                hidden(0, 0, 0, wait=False)
                expert(0, 0, True, False)
                expert(1, 1, False, False)
                with pe.Fori(1, E0 // 2 - 1) as i:
                    for par in range(2):
                        expert(i * 2 + par, par, False, False)
                expert(E0 - 2, 0, False, False)
                expert(E0 - 1, 1, False, True)


def combine(nc, x_sb, y_rows, slot, weight, J, tag, sw):
    R = 8
    with ExitStack() as ctx:
        g = ctx.enter_context(nc.sbuf_tensor(f"{tag}_rows", [P, R, D], F32))
        arrived = sw[7:7 + R]
        added = ctx.enter_context(nc.semaphore(f"{tag}_added"))
        with nc.Block() as block:
            @block.gpsimd
            def _(pool):
                for n in range(TT * J):
                    if n >= R:
                        pool.wait_ge(added, n - R + 1)
                    pool.indirect_dma_start(out=g[:, n % R, :], out_offset=None, in_=y_rows,
                                            in_offset=bass.IndirectOffsetOnAxis(ap=slot[:, n % J, n // J:n // J + 1].bitcast(U32), axis=0)
                                            ).then_inc(arrived[n % R], 16)

            @block.vector
            def _(dve):
                for n in range(TT * J):
                    t, j = n // J, n % J
                    dve.wait_ge(arrived[n % R], 16 * (n // R + 1))
                    if j:
                        dve.wait_ge(added, n)
                    dve.scalar_tensor_tensor(out=x_sb[:, t, :], in0=g[:, n % R, :], scalar=weight[:, j, t:t + 1],
                                             in1=x_sb[:, t, :], op0=ALU.mult, op1=ALU.add).then_inc(added, 1)


HD1, GRP = 16, 4
BIG = 1.0e30


def context_keys(nc, io, ident, ks, vm, vt):
    with ExitStack() as ctx:
        sb = lambda n, s, d=F32: ctx.enter_context(nc.sbuf_tensor(n, s, d))
        sem = lambda n: ctx.enter_context(nc.semaphore(n))
        c0 = sb("c1_rows0", [P, B, D])
        c1 = sb("c1_rows1", [S1, B, D])
        cT = sb("c1_T", [P, KD, B * S])
        w = sb("kv_w_sb", [P, KD, 2 * D])
        kb = sb("k_bias", [P, KD])
        vb = sb("v_bias", [P, D])
        kf = sb("k_full", [P, KD, B * S])
        kh = sb("k_hi", [P, KD, B * S], F32R)
        kl = sb("k_lo", [P, KD, B * S], F32R)
        m8 = sb("mask_u8", [97, B * S], mybir.dt.uint8)
        pt = [ctx.enter_context(nc.psum_tensor(f"c1_p{i}", [P, 512], F32)) for i in range(8)]
        loaded, step_s = sem("c1_loaded"), sem("c1_step")
        turned, copied = sem("c1_turned"), sem("c1_copied")
        k_made, k_done, kh_done, kl_done = sem("c1_k_made"), sem("c1_k_done"), sem("c1_kh_done"), sem("c1_kl_done")
        v_made, v_done, placed, zeroed = sem("c1_v_made"), sem("c1_v_done"), sem("c1_placed"), sem("c1_zeroed")
        with nc.Block() as block:
            @block.sync
            def _(sp):
                sp.dma_start(c0[:, :, :], io["ctx_1024"][:, 0:P, :].rearrange("b p d -> p b d")).then_inc(loaded, 16)
                sp.dma_start(c1[:, :, :], io["ctx_1024"][:, P:S, :].rearrange("b p d -> p b d")).then_inc(loaded, 16)
                sp.dma_start(w[:, :, :], io["L1_xattn_kv_w"].rearrange("(k p) n -> p k n", p=P)).then_inc(loaded, 16)
                sp.dma_start(kb[:, :], io["L1_xattn_kv_b"][0:D].rearrange("(k p) -> p k", p=P), allow_slow_non_contiguous=True).then_inc(loaded, 16)
                sp.dma_start(vb[:, :], io["L1_xattn_kv_b"][D:2 * D].rearrange("(o e) -> o e", o=1).broadcast_to([P, D])).then_inc(loaded, 16)
                sp.dma_start(m8[96:97, :], io["mask_BxS2_bk0"].rearrange("(o b) s -> o (b s)", o=1)).then_inc(loaded, 16)
                sp.wait_ge(kl_done, KD)
                sp.wait_ge(kh_done, KD)
                sp.wait_ge(zeroed, 2)
                for c in range(KD):
                    for q in range(4):
                        for h in range(2):
                            src = slice(q * 32 + h * HD1, q * 32 + (h + 1) * HD1)
                            for j, half in enumerate((kh, kh, kl)):
                                dst = slice(j * 32 + h * HD1, j * 32 + (h + 1) * HD1)
                                sp.dma_start(ks[dst, :, c * 4 + q, h, :].bitcast(F32), half[src, c, :].bitcast(F32).rearrange("p (b s) -> p b s", b=B)).then_inc(placed, 16)
                sp.wait_ge(placed, 16 * KD * 4 * 2 * 3)

            @block.gpsimd
            def _(pool):
                pool.memset(ks[:, :, :, :, :].bitcast(F32), 0.0).then_inc(zeroed, 1)
                pool.wait_ge(zeroed, 1)
                pool.memset(vt[:, :, :, :], 0.0)
                pool.memset(vm[:, :, :, :], 0.0).then_inc(zeroed, 1)

            @block.scalar
            def _(act):
                for b in range(B):
                    act.wait_ge(turned, b + 1)
                    for k in range(KD):
                        ins = act.activation(cT[:, k, b * S:(b + 1) * S], pt[(b % 2) * 2 + k][:, 0:S], ACT.Copy)
                    ins.then_inc(copied, 1)
                for c in range(KD):
                    act.wait_ge(k_made, c + 1)
                    act.wait_ge(loaded, 96)
                    for j in range(2):
                        n = slice(j * 2 * S, (j + 1) * 2 * S)
                        ins = act.activation(kf[:, c, n], pt[4 + c * 2 + j][:, 0:2 * S], ACT.Identity, bias=kb[:, c:c + 1])
                    ins.then_inc(k_done, 1)
                    act.wait_ge(k_done, c + 1)
                    act.activation(kh[:, c, :], kf[:, c, :], ACT.Copy).then_inc(kh_done, 1)

            @block.vector
            def _(dve):
                dve.wait_ge(zeroed, 2)
                dve.wait_ge(loaded, 96)
                for b in range(B):
                    dve.tensor_scalar(ks[96:97, b, :, :, :].rearrange("p q h s -> p (q h) s"),
                                      m8[96:97, b * S:(b + 1) * S].rearrange("p (o s) -> p o s", o=1).broadcast_to([1, 16, S]),
                                      -BIG, None, ALU.mult)
                for c in range(KD):
                    dve.wait_ge(kh_done, c + 1)
                    dve.tensor_tensor(kl[:, c, :], kf[:, c, :], kh[:, c, :].bitcast(F32), ALU.subtract).then_inc(kl_done, 1)
                for b in range(B):
                    dve.wait_ge(v_made, b + 1)
                    split = dict(c=2, u=2, h=4)
                    for u in range(2):
                        ins = dve.tensor_tensor(vm[:, b].rearrange("p (c u h) d -> p u c h d", **split)[:, u, :, :, u * HD1:(u + 1) * HD1],
                                                pt[b % 2][:, 0:D].rearrange("p (c u h d) -> p u c h d", **split)[:, u],
                                                vb[:, :].rearrange("p (c u h d) -> p u c h d", **split)[:, u], ALU.add)
                    for hh in range(4):
                        r = slice(32 * hh, 32 * hh + S1)
                        for u in range(2):
                            ins = dve.tensor_tensor(vt[r, b].rearrange("p (c u) w -> p u c w", u=2)[:, u, :, 32 * hh + u * HD1:32 * hh + (u + 1) * HD1],
                                                    pt[2 + b % 2][r, 0:D].rearrange("p (c u h d) -> p u h c d", **split)[:, u, hh],
                                                    vb[r, :].rearrange("p (c u h d) -> p u h c d", **split)[:, u, hh], ALU.add)
                    ins.then_inc(v_done, 1)

            @block.tensor
            def _(pe):
                pe.wait_ge(loaded, 96)
                for b in range(B):
                    if b >= 2:
                        pe.wait_ge(copied, b - 1)
                    for k in range(KD):
                        cols = slice(k * P, (k + 1) * P)
                        pe.transpose(pt[(b % 2) * 2 + k][:, 0:P], c0[:, b, cols], ident[:, :])
                        ins = pe.transpose(pt[(b % 2) * 2 + k][:, P:S], c1[:, b, cols], ident[0:S1, 0:S1])
                    ins.then_inc(turned, 1)
                pe.wait_ge(copied, B)
                for c in range(KD):
                    for j in range(2):
                        for k in range(KD):
                            ins = pe.matmul(pt[4 + c * 2 + j][:, 0:2 * S], w[:, k, c * P:(c + 1) * P], cT[:, k, j * 2 * S:(j + 1) * 2 * S],
                                            start=k == 0, stop=k == KD - 1)
                    ins.then_inc(k_made, 1)
                for b in range(B):
                    if b >= 2:
                        pe.wait_ge(v_done, b - 1)
                    for k in range(KD):
                        pe.matmul(pt[b % 2][:, 0:D], cT[:, k, b * S:b * S + P], w[:, k, D:2 * D], start=k == 0, stop=k == KD - 1)
                    for hh in range(4):
                        for k in range(KD):
                            ins = pe.matmul(pt[2 + b % 2][32 * hh:32 * hh + S1, 0:D], cT[:, k, b * S + P:(b + 1) * S], w[:, k, D:2 * D],
                                            start=k == 0, stop=k == KD - 1)
                    ins.then_inc(v_made, 1)


def context_queries(nc, io, x_sb, xh, xl, q_hi, q_lo):
    NU = KD * (TOK // 512)
    R = 4
    with ExitStack() as ctx:
        sb = lambda n, s, d=F32: ctx.enter_context(nc.sbuf_tensor(n, s, d))
        sem = lambda n: ctx.enter_context(nc.semaphore(n))
        w32 = sb("q_w_sb", [P, KD, D])
        wh = sb("q_w_hi", [P, KD, D], F32R)
        wl = sb("q_w_lo", [P, KD, D], F32R)
        qb = sb("q_bias", [P, KD])
        qbs = sb("q_bias_scaled", [P, KD])
        pb = sb("proj_bias", [P, D])
        qf = sb("q_full", [P, 2, 512])
        qh = sb("q_hi_sb", [P, R, 512], F32R)
        ql = sb("q_lo_sb", [P, R, 512], F32R)
        pq = [ctx.enter_context(nc.psum_tensor(f"q_p{i}", [P, 512], F32)) for i in range(2)]
        w_loaded, b_loaded, pb_loaded = sem("q_w_loaded"), sem("q_b_loaded"), sem("proj_b_loaded")
        w_hi, w_lo, b_scaled = sem("q_w_hi_done"), sem("q_w_lo_done"), sem("q_b_scaled")
        q_made, q_full, h_done, l_done = sem("q_product"), sem("q_full_done"), sem("q_hi_cut"), sem("q_lo_cut")
        h_stored = [sem(f"q_hi_stored{i}") for i in range(R)]
        l_stored = [sem(f"q_lo_stored{i}") for i in range(R)]
        biased = sem("x_biased")
        with nc.Block() as block:
            @block.sync
            def _(sp):
                sp.dma_start(w32[:, :, :], io["L1_xattn_q_w"].rearrange("(k p) n -> p k n", p=P)).then_inc(w_loaded, 16)
                sp.dma_start(qb[:, :], io["L1_xattn_q_b"].rearrange("(k p) -> p k", p=P), allow_slow_non_contiguous=True).then_inc(b_loaded, 16)
                sp.dma_start(pb[:, :], io["L1_xattn_proj_b"].rearrange("(o e) -> o e", o=1).broadcast_to([P, D])).then_inc(pb_loaded, 16)
                for n in range(NU):
                    G, c = n // KD, n % KD
                    dst = (slice(c * P, (c + 1) * P), slice(G * 512, (G + 1) * 512))
                    sp.wait_ge(h_done, n + 1)
                    sp.dma_start(q_hi[dst], qh[:, n % R, :].bitcast(F32)).then_inc(h_stored[n % R], 16)
                    sp.wait_ge(l_done, n + 1)
                    sp.dma_start(q_lo[dst], ql[:, n % R, :].bitcast(F32)).then_inc(l_stored[n % R], 16)
                for i in range(R):
                    sp.wait_ge(h_stored[i], 16 * (NU // R))
                    sp.wait_ge(l_stored[i], 16 * (NU // R))

            @block.gpsimd
            def _(pool):
                pool.wait_ge(pb_loaded, 16)
                pool.tensor_tensor(x_sb[:, :, :], x_sb[:, :, :], pb[:, :].rearrange("p (o d) -> p o d", o=1).broadcast_to([P, TT, D]),
                                   ALU.add).then_inc(biased, 1)
                pool.wait_ge(biased, 1)

            @block.scalar
            def _(act):
                act.wait_ge(w_loaded, 16)
                act.activation(wh[:, :, :], w32[:, :, :], ACT.Copy).then_inc(w_hi, 1)
                act.wait_ge(b_loaded, 16)
                act.activation(qbs[:, :], qb[:, :], ACT.Copy, scale=HD1 ** -0.5).then_inc(b_scaled, 1)
                act.wait_ge(b_scaled, 1)
                for n in range(NU):
                    act.wait_ge(q_made, n + 1)
                    if n >= 2:
                        act.wait_ge(l_done, n - 1)
                    act.activation(qf[:, n % 2, :], pq[n % 2][:, :], ACT.Identity, bias=qbs[:, n % KD:n % KD + 1],
                                   scale=HD1 ** -0.5).then_inc(q_full, 1)
                    act.wait_ge(q_full, n + 1)
                    if n >= R:
                        act.wait_ge(h_stored[n % R], 16 * (n // R))
                    act.activation(qh[:, n % R, :], qf[:, n % 2, :], ACT.Copy).then_inc(h_done, 1)

            @block.vector
            def _(dve):
                dve.wait_ge(w_hi, 1)
                dve.tensor_tensor(wl[:, :, :], w32[:, :, :], wh[:, :, :].bitcast(F32), ALU.subtract).then_inc(w_lo, 1)
                for n in range(NU):
                    dve.wait_ge(h_done, n + 1)
                    if n >= R:
                        dve.wait_ge(l_stored[n % R], 16 * (n // R))
                    dve.tensor_tensor(ql[:, n % R, :], qf[:, n % 2, :], qh[:, n % R, :].bitcast(F32), ALU.subtract).then_inc(l_done, 1)

            @block.tensor
            def _(pe):
                pe.wait_ge(w_hi, 1)
                pe.wait_ge(w_lo, 1)
                for n in range(NU):
                    if n >= 2:
                        pe.wait_ge(q_full, n - 1)
                    G, c = n // KD, n % KD
                    x = slice(G * 512, (G + 1) * 512)
                    w = slice(c * P, (c + 1) * P)
                    for k in range(KD):
                        ins = matmul3(pe, pq[n % 2][:, :], wh[:, k, w], wl[:, k, w], xh[:, k, x], xl[:, k, x], k == 0, k == KD - 1)
                    ins.then_inc(q_made, 1)


def context_attention(nc, io, x_sb, ident, q_hi, q_lo, ks, vm, vt):
    NG = TOK // 512
    with ExitStack() as ctx:
        sb = lambda n, s, d=F32: ctx.enter_context(nc.sbuf_tensor(n, s, d))
        sem = lambda n: ctx.enter_context(nc.semaphore(n))
        pw = sb("proj_w_rows", [P, 2, D])
        vs = sb("c_values", [P, 2, 16, 32])
        vts = sb("c_rest_values", [P, 2, GRP, P])
        qs = sb("q_stack", [97, 2, 8, 512], F32R)
        exps_sb = sb("c_exps", [P, 4, 4, S])
        probs = sb("c_probs", [P, 2, 4, 4, P])
        rest = sb("c_rest_probs", [P, 2, 4, 4, 32])
        sums = sb("c_sums", [P, 2, 16])
        neg = sb("c_neg_max", [P, 2, 16])
        rec = sb("c_recip", [P, 2, 16])
        pT = sb("c_probsT", [P, 2, 512])
        oT = sb("c_outT", [P, 2, 512])
        st = [ctx.enter_context(nc.psum_tensor(f"c_s{i}", [P, 2, 512], F32)) for i in range(2)]
        tb = [ctx.enter_context(nc.psum_tensor(f"c_t{i}", [P, 512], F32)) for i in range(2)]
        ob = ctx.enter_context(nc.psum_tensor("c_o", [P, 512], F32))
        mb = ctx.enter_context(nc.psum_tensor("c_m", [P, 512], F32))
        loaded, zeroed = sem("c_loaded"), sem("c_zeroed")
        q_loaded = [sem(f"c_q_loaded{i}") for i in range(2)]
        v_placed = sem("c_v_placed")
        scores, maxed, exped = sem("c_scores"), sem("c_maxed"), sem("c_exped")
        recips, scaled = sem("c_recips"), sem("c_scaled")
        t_made = sem("c_turned")
        t_act, t_dve = sem("c_pT_act"), sem("c_pT_dve")
        o_made, o_done = sem("c_o_made"), sem("c_o_done")
        y_made, y_added = sem("c_y_made"), sem("c_y_added")
        BANKS = 5
        ON_ACT = {0: 0, 2: 1}
        ON_DVE = {1: 0, 3: 1, 4: 2}

        def wait_copied(eng, s, j):
            if j in ON_ACT:
                eng.wait_ge(t_act, s * 2 + (ON_ACT[j] + 1))
            else:
                eng.wait_ge(t_dve, s * 3 + (ON_DVE[j] + 1))

        with nc.Block() as block:
            @block.sync
            def _(sp):
                for j in range(4):
                    for u in range(2):
                        r = 32 * j + 16 * u
                        sp.dma_start(pw[r:r + HD1, :, :],
                                     io["L1_xattn_proj_w"].rearrange("(c u j d) n -> j u d c n", c=2, u=2, j=4)[j, u]).then_inc(loaded, 16)
                hi = q_hi.rearrange("(pr r) n -> r pr n", r=32)
                lo = q_lo.rearrange("(pr r) n -> r pr n", r=32)

                def load(i, par, first):
                    G = i * 2 + par
                    if not first:
                        sp.wait_ge(scores, G * 16 - 16)
                    for j, src in enumerate((hi, lo, hi)):
                        sp.dma_start(qs[j * 32:(j + 1) * 32, par, :, :].bitcast(F32), src[:, :, bass.ds(G * 512, 512)]).then_inc(q_loaded[par], 16)

                load(0, 0, True)
                load(0, 1, True)
                with sp.Fori(1, NG // 2) as i:
                    load(i, 0, False)
                    load(i, 1, False)

            @block.gpsimd
            def _(pool):
                pool.memset(qs[96:97, :, :, :].bitcast(F32), 1.0).then_inc(zeroed, 1)
                pool.wait_ge(zeroed, 1)
                pool.memset(rest[:, :, :, :, :], 0.0).then_inc(zeroed, 1)

                for G in range(NG):
                    if G >= 2:
                        pool.wait_ge(v_placed, 2 * G - 2)
                        pool.wait_ge(o_made, 2 * G - 2)
                    pool.tensor_copy(vs[:, G % 2], vm[:, G // 2]).then_inc(v_placed, 1)
                    pool.tensor_copy(vts[:, G % 2], vt[:, G // 2]).then_inc(v_placed, 1)

            @block.scalar
            def _(act):
                def exps(s, n, par):
                    act.wait_ge(maxed, s * 4 + (n + 1))
                    for h in range(4):
                        col = slice(n * 4 + h, n * 4 + h + 1)
                        ins = act.activation(exps_sb[:, n, h, :], st[n % 2][:, h // 2, (h % 2) * S:(h % 2 + 1) * S], ACT.Exp,
                                             bias=neg[:, par, col], accum_out=sums[:, par, col])
                    ins.then_inc(exped, 1)

                def copy_pT(s, j):
                    act.wait_ge(t_made, s * BANKS + (j + 1))
                    act.activation(pT[:, j % 2, :], tb[j % 2][:, :], ACT.Copy).then_inc(t_act, 1)

                def copy_out(G, c):
                    act.wait_ge(o_made, G * 2 + (c + 1))
                    act.activation(oT[:, c, :], ob[:, :], ACT.Copy).then_inc(o_done, 1)

                def round_(i, par, last):
                    G = i * 2 + par
                    for g in range(GRP):
                        s = G * GRP + g
                        more = not (last and g == GRP - 1)
                        copy_pT(s, 0)
                        if more:
                            exps(s + 1, 0, 1 - g % 2)
                            exps(s + 1, 1, 1 - g % 2)
                        copy_pT(s, 2)
                        if more:
                            exps(s + 1, 2, 1 - g % 2)
                            exps(s + 1, 3, 1 - g % 2)
                        if g % 2:
                            copy_out(G, g // 2)

                for n in range(4):
                    exps(0, n, 0)
                with act.Fori(0, NG // 2 - 1) as i:
                    round_(i, 0, False)
                    round_(i, 1, False)
                round_(NG // 2 - 1, 0, False)
                round_(NG // 2 - 1, 1, True)

            @block.vector
            def _(dve):
                def top(s, n, par):
                    dve.wait_ge(scores, s * 4 + (n + 1))
                    dve.tensor_reduce(neg[:, par, n * 4:n * 4 + 4], st[n % 2][:, :, 0:2 * S].rearrange("p q (h s) -> p q h s", h=2),
                                      AX.X, ALU.max, negate=True).then_inc(maxed, 1)

                def scale(s, n, par):
                    dve.wait_ge(exped, s * 4 + (n + 1))
                    c = slice(n * 4, n * 4 + 4)
                    dve.reciprocal(rec[:, par, c], sums[:, par, c]).then_inc(recips, 1)
                    dve.wait_ge(recips, s * 4 + (n + 1))
                    by = rec[:, par, c].rearrange("p (h s) -> p h s", s=1)
                    dve.tensor_tensor(probs[:, par, n], exps_sb[:, n, :, 0:P], by.broadcast_to([P, 4, P]), ALU.mult)
                    dve.tensor_tensor(rest[:, par, n, :, 0:S1], exps_sb[:, n, :, P:S], by.broadcast_to([P, 4, S1]), ALU.mult).then_inc(scaled, 1)

                def copy_pT(s, j):
                    dve.wait_ge(t_made, s * BANKS + (j + 1))
                    dve.tensor_copy(pT[:, j % 2, :], tb[j % 2][:, :]).then_inc(t_dve, 1)

                def add(G, j):
                    dve.wait_ge(y_made, G * 2 + (j + 1))
                    dst = x_sb[:, bass.ds(G * 4 + 2 * j, 2), :]
                    dve.tensor_tensor(dst, dst, mb[:, :].rearrange("p (t d) -> p t d", d=D), ALU.add).then_inc(y_added, 1)

                def round_(i, par, first, last):
                    G = i * 2 + par
                    for g in range(GRP):
                        s = G * GRP + g
                        more = not (last and g == GRP - 1)
                        late = g == 0 and not first
                        o = 1 - g % 2
                        if more:
                            top(s + 1, 0, o)
                            top(s + 1, 1, o)
                        copy_pT(s, 1)
                        if late:
                            add(G - 1, 0)
                        if more:
                            scale(s + 1, 0, o)
                            top(s + 1, 2, o)
                            scale(s + 1, 1, o)
                            top(s + 1, 3, o)
                        copy_pT(s, 3)
                        if late:
                            add(G - 1, 1)
                        if more:
                            scale(s + 1, 2, o)
                        copy_pT(s, 4)
                        if more:
                            scale(s + 1, 3, o)

                dve.wait_ge(zeroed, 2)
                top(0, 0, 0)
                for n in range(1, 4):
                    top(0, n, 0)
                    scale(0, n - 1, 0)
                scale(0, 3, 0)
                round_(0, 0, True, False)
                round_(0, 1, False, False)
                with dve.Fori(1, NG // 2 - 1) as i:
                    round_(i, 0, False, False)
                    round_(i, 1, False, False)
                round_(NG // 2 - 1, 0, False, False)
                round_(NG // 2 - 1, 1, False, True)
                add(NG - 1, 0)
                add(NG - 1, 1)

            @block.tensor
            def _(pe):
                def score(i, par, g, n, first=False):
                    s = (i * 2 + par) * GRP + g
                    if n == 0 and g == 0:
                        pe.wait_ge(q_loaded[par], i * 48 + 48)
                    if not first or n >= 2:
                        pe.wait_ge(exped, s * 4 + (n - 1))
                    for q in range(2):
                        pair = g * 2 + q
                        k = ks[:, bass.ds(i, 1), pair, :, :].rearrange("p b h s -> p (b h s)")
                        ins = pe.matmul(st[n % 2][:, q, 0:2 * S], qs[:, par, pair, n * P:(n + 1) * P], k, start=True, stop=True)
                    ins.then_inc(scores, 1)

                def turn(s, g, j, first=False):
                    if j == 0:
                        pe.wait_ge(scaled, s * 4 + 4)
                    if j >= 2:
                        wait_copied(pe, s, j - 2)
                    elif not first:
                        wait_copied(pe, s - 1, 4 - j)
                    for n in range(4):
                        if j < 4:
                            ins = pe.transpose(tb[j % 2][:, n * P:(n + 1) * P], probs[:, g % 2, n, j, :], ident[:, :])
                        else:
                            ins = pe.transpose(tb[0][:, n * P:(n + 1) * P], rest[:, g % 2, n].rearrange("p h s -> p (h s)"), ident[:, :])
                    ins.then_inc(t_made, 1)

                def weigh(G, par, g, j, first=False):
                    s = G * GRP + g
                    if j == 0 and g == 0:
                        pe.wait_ge(v_placed, G * 2 + 2)
                    if j == 0 and g % 2 == 0 and not first:
                        pe.wait_ge(o_done, G * 2 + g // 2)
                    wait_copied(pe, s, j)
                    even = g % 2 == 0
                    if j < 4:
                        pe.matmul(ob[32 * j:32 * (j + 1), :], vs[:, par, g * 4 + j, :], pT[:, j % 2, :], start=even, stop=False,
                                  skip_group_check=True)
                    else:
                        ins = pe.matmul(ob[:, :], vts[:, par, g, :], pT[:, 0, :], start=False, stop=not even, skip_group_check=True)
                        if not even:
                            ins.then_inc(o_made, 1)

                def project(G, j):
                    if j == 0:
                        pe.wait_ge(o_done, G * 2 + 2)
                    if j or not (isinstance(G, int) and G == 0):
                        pe.wait_ge(y_added, G * 2 + j)
                    for t in range(2):
                        rows = slice((2 * j + t) * P, (2 * j + t + 1) * P)
                        for c in range(2):
                            ins = pe.matmul(mb[:, t * D:(t + 1) * D], oT[:, c, rows], pw[:, c, :], start=c == 0, stop=c == 1)
                    ins.then_inc(y_made, 1)

                def round_(i, par, first, last):
                    G = i * 2 + par
                    for g in range(GRP):
                        s = G * GRP + g
                        start = first and g == 0
                        late = g == 0 and not first

                        def next_score(n):
                            if g < GRP - 1:
                                score(i, par, g + 1, n)
                            elif not last:
                                score(i + par, 1 - par, 0, n)

                        turn(s, g, 0, start)
                        next_score(0)
                        turn(s, g, 1, start)
                        if late:
                            project(G - 1, 0)
                        weigh(G, par, g, 0, start)
                        next_score(1)
                        turn(s, g, 2)
                        weigh(G, par, g, 1)
                        next_score(2)
                        turn(s, g, 3)
                        if late:
                            project(G - 1, 1)
                        weigh(G, par, g, 2)
                        next_score(3)
                        turn(s, g, 4)
                        weigh(G, par, g, 3)
                        weigh(G, par, g, 4)

                pe.wait_ge(zeroed, 2)
                for n in range(4):
                    score(0, 0, 0, n, True)
                pe.wait_ge(loaded, 16 * 8)
                round_(0, 0, True, False)
                round_(0, 1, False, False)
                with pe.Fori(1, NG // 2 - 1) as i:
                    round_(i, 0, False, False)
                    round_(i, 1, False, False)
                round_(NG // 2 - 1, 0, False, False)
                round_(NG // 2 - 1, 1, False, True)
                project(NG - 1, 0)
                project(NG - 1, 1)


E1, H1, CAP1 = 8, 512, TOK // 8
T1 = -(-(TOK + E1 * (P - 1)) // P)
T1 = -(-T1 // 4) * 4
SLOTS1 = T1 * P


def route1(nc, io, cst, logits, r, tile_expert, ws):
    with ExitStack() as c1:
        sb = lambda n, s, d=F32: c1.enter_context(nc.sbuf_tensor(n, s, d))
        sem = lambda n: c1.enter_context(nc.semaphore(n))
        pr = sb("r1_probs", [P, TT, E1])
        key = sb("r1_key", [P, E1, TT])
        chosen = sb("r1_chosen", [P, E1, TT])
        rank = sb("r1_rank", [P, E1, TT])
        over_e = lambda t: t.rearrange("p (t e) -> p t e", e=1).broadcast_to([P, TT, E1])
        flat = lambda t: t[:, :, :].rearrange("p a b -> p (a b)")
        te = lambda t: t[:, :, :].rearrange("p e t -> p t e")
        W = E1 * TT
        with ExitStack() as c2:
            m = c2.enter_context(nc.sbuf_tensor("r1_max", [P, TT], F32))
            step_s, exped = (c2.enter_context(nc.semaphore(n)) for n in ("r1_step", "r1_exp"))
            with nc.Block() as block:
                @block.vector
                def _(dve):
                    step = Steps(dve, step_s)
                    step.then(dve.tensor_reduce(m[:, :], logits[:, :, :], AX.X, ALU.max))
                    step.then(dve.tensor_tensor(pr[:, :, :], logits[:, :, :], over_e(m[:, :]), ALU.subtract))
                    dve.wait_ge(exped, 1)
                    step.then(dve.tensor_reduce(m[:, :], pr[:, :, :], AX.X, ALU.add))
                    step.then(dve.reciprocal(m[:, :], m[:, :]))
                    step.then(dve.tensor_tensor(pr[:, :, :], pr[:, :, :], over_e(m[:, :]), ALU.mult))
                    step.then(dve.tensor_copy(te(key), pr[:, :, :]))

                @block.scalar
                def _(act):
                    act.wait_ge(step_s, 2)
                    act.activation(pr[:, :, :], pr[:, :, :], ACT.Exp).then_inc(exped, 1)

        choose(nc, cst, key, E1, CAP1, chosen, rank, "r1_", ws)
        with ExitStack() as c2:
            sb2 = lambda n, s, d=F32: c2.enter_context(nc.sbuf_tensor(n, s, d))
            v = sb2("r1_value", [P, TT, E1])
            eq = sb2("r1_is_max", [P, TT, E1])
            pre = sb2("r1_prefix", [P, TT, E1])
            one = sb2("r1_one_hot", [P, E1, TT])
            m = sb2("r1_max2", [P, TT])
            count = sb2("r1_count", [P, E1])
            ci = sb2("r1_count_i", [P, E1], I32)
            upto = sb2("r1_tiles_upto", [P, E1])
            base = sb2("r1_base", [P, E1])
            past = sb2("r1_past", [P, T1, E1])
            tf = sb2("r1_tile_f", [P, T1])
            row = sb2("r1_slot_row", [P, TT], I32)
            pq = [c2.enter_context(nc.psum_tensor(f"r1_p{i}", [P, 512], F32)) for i in range(3)]
            step_s, summed = (c2.enter_context(nc.semaphore(n)) for n in ("r1_slots_step", "r1_summed"))
            with nc.Block() as block:
                @block.vector
                def _(dve):
                    step = Steps(dve, step_s)
                    step.then(dve.tensor_reduce(m[:, :], te(chosen), AX.X, ALU.max))
                    step.then(dve.tensor_tensor(v[:, :, :], over_e(m[:, :]), te(chosen), ALU.subtract))
                    step.then(dve.scalar_tensor_tensor(out=v[:, :, :], in0=v[:, :, :], scalar=-4.0, in1=pr[:, :, :], op0=ALU.mult, op1=ALU.add))
                    step.then(dve.tensor_reduce(m[:, :], v[:, :, :], AX.X, ALU.max))
                    step.then(dve.tensor_tensor(eq[:, :, :], v[:, :, :], over_e(m[:, :]), ALU.is_equal))
                    step.then(dve.tensor_tensor_scan(flat(pre), cst["keep_8"][:, 0:W], flat(eq), 0.0, ALU.mult, ALU.add))
                    step.then(dve.tensor_scalar(pre[:, :, :], pre[:, :, :], 1.0, None, ALU.is_equal))
                    step.then(dve.tensor_tensor(te(one), pre[:, :, :], eq[:, :, :], ALU.mult))
                    step.then(dve.tensor_reduce(count[:, :], one[:, :, :], AX.X, ALU.add))
                    step.then(dve.tensor_tensor(v[:, :, :], te(one), pr[:, :, :], ALU.mult))
                    step.then(dve.tensor_reduce(r["weight"][:, 0, :], v[:, :, :], AX.X, ALU.add))
                    dve.wait_ge(summed, 1)
                    step.then(dve.tensor_copy(ci[:, :], pq[0][:, 0:E1]))
                    step.then(dve.tensor_scalar(ci[:, :], ci[:, :], P - 1, None, ALU.add))
                    step.then(dve.tensor_scalar(ci[:, :], ci[:, :], P.bit_length() - 1, None, ALU.logical_shift_right))
                    step.then(dve.tensor_copy(count[:, :], ci[:, :]))
                    step.then(dve.tensor_tensor_scan(upto[:, :], cst["ones"][:, 0:E1], count[:, :], 0.0, ALU.mult, ALU.add))
                    step.then(dve.tensor_tensor(base[:, :], upto[:, :], count[:, :], ALU.subtract))
                    step.then(dve.tensor_scalar(base[:, :], base[:, :], float(P), None, ALU.mult))
                    step.then(dve.tensor_tensor(past[:, :, :], cst["tile_no"][:, 0:T1].rearrange("p (t e) -> p t e", e=1).broadcast_to([P, T1, E1]),
                                                upto[:, :].rearrange("p (t e) -> p t e", t=1).broadcast_to([P, T1, E1]), ALU.is_ge))
                    step.then(dve.tensor_reduce(tf[:, :], past[:, :, :], AX.X, ALU.add))
                    step.then(dve.tensor_scalar(tf[:, :], tf[:, :], float(E1 - 1), None, ALU.min))
                    step.then(dve.tensor_copy(tile_expert[:, :], tf[:, :]))
                    step.then(dve.tensor_copy(chosen[:, :, :], pq[2][:, 0:W].rearrange("p (e t) -> p e t", t=TT)))
                    step.then(dve.tensor_tensor_scan(flat(rank), cst["keep"][:, 0:W], flat(chosen), 0.0, ALU.mult, ALU.add))
                    step.then(dve.tensor_tensor(rank[:, :, :], rank[:, :, :], chosen[:, :, :], ALU.subtract))
                    step.then(dve.tensor_tensor(rank[:, :, :], rank[:, :, :], pq[1][:, 0:W].rearrange("p (e t) -> p e t", t=TT), ALU.add))
                    step.then(dve.tensor_tensor(rank[:, :, :], rank[:, :, :], base[:, :].rearrange("p (e t) -> p e t", t=1).broadcast_to([P, E1, TT]), ALU.add))
                    step.then(dve.tensor_tensor(rank[:, :, :], rank[:, :, :], one[:, :, :], ALU.mult))
                    step.then(dve.tensor_reduce(m[:, :], te(rank), AX.X, ALU.add))
                    slot, scatter = r["slot"][:, 0, :], r["scatter"][:, 0, :]
                    step.then(dve.tensor_copy(slot, m[:, :]))
                    step.then(dve.tensor_scalar(row[:, :], slot, P - 1, None, ALU.bitwise_and))
                    step.then(dve.tensor_scalar(row[:, :], row[:, :], T1, None, ALU.mult))
                    step.then(dve.tensor_scalar(scatter, slot, P.bit_length() - 1, None, ALU.logical_shift_right))
                    step.then(dve.tensor_tensor(scatter, scatter, row[:, :], ALU.add))

                @block.tensor
                def _(pe):
                    pe.wait_ge(step_s, 9)
                    pe.matmul(pq[0][:, 0:E1], cst["ones"][:, :], count[:, :], start=True, stop=True)
                    pe.matmul(pq[1][:, 0:W], cst["before"][:, :], flat(one), start=True, stop=True)
                    pe.matmul(pq[2][:, 0:W], cst["ones"][:, :], flat(one), start=True, stop=True).then_inc(summed, 1)


class ResidentWeights:

    def __init__(self, nc, ctx, io):
        sb = lambda n, s, d=F32: ctx.enter_context(nc.sbuf_tensor(n, s, d))
        sem = lambda n: ctx.enter_context(nc.semaphore(n))
        self.io = io
        self.hi = [sb(f"w{j + 1}_hi", [P, E1 * 1024], F32R) for j in range(2)]
        self.lo = [sb(f"w{j + 1}_lo", [P, E1 * 1024], F32R) for j in range(2)]
        self.stage = sb("w_stage", [P, 2, 1024])
        self.loaded = [sem(f"rw_loaded{j}") for j in range(2)]
        self.hi_done, self.lo_done = sem("rw_hi_done"), sem("rw_lo_done")

    def load(self, sp):
        for n in range(2 * E1):
            e, j = n // 2, n % 2
            src = self.io[("L1_ffn_W1", "L1_ffn_W2")[j]][e].rearrange("(c p) h -> p c h", p=P)
            if n >= 2:
                sp.wait_ge(self.lo_done, n - 1)
            sp.dma_start(self.stage[:, j, :].rearrange("p (c h) -> p c h", h=src.shape[2]), src).then_inc(self.loaded[j], 16)

    def high(self, act):
        for n in range(2 * E1):
            e, j = n // 2, n % 2
            act.wait_ge(self.loaded[j], 16 * e + 16)
            act.activation(self.hi[j][:, e * 1024:(e + 1) * 1024], self.stage[:, j, :], ACT.Copy).then_inc(self.hi_done, 1)

    def low(self, pool):
        for n in range(2 * E1):
            e, j = n // 2, n % 2
            c = slice(e * 1024, (e + 1) * 1024)
            pool.wait_ge(self.hi_done, n + 1)
            pool.tensor_tensor(self.lo[j][:, c], self.stage[:, j, :], self.hi[j][:, c].bitcast(F32), ALU.subtract).then_inc(self.lo_done, 1)


def sorted_experts(nc, io, ident, cst, xn_rows, table, y_rows, r, tile_expert, ws, sw):
    R = 4
    with ExitStack() as ctx:
        sb = lambda n, s, d=F32: ctx.enter_context(nc.sbuf_tensor(n, s, d))
        sem = lambda n: ctx.enter_context(nc.semaphore(n))
        ids = sb("s_ids", [P, T1], I32)
        xr = sb("s_rows", [P, R, D])
        xh = sb("s_x_hi", [P, 2, KD, P], F32R)
        xl = sb("s_x_lo", [P, 2, KD, P], F32R)
        ge = sb("s_gelu", [P, 2, H1])
        gh = sb("s_g_hi", [P, 2, H1], F32R)
        gl = sb("s_g_lo", [P, 2, H1], F32R)
        ys = sb("s_y", [P, R, D])
        xb, yb, hb, tb = ([ctx.enter_context(nc.psum_tensor(f"s_{n}{i}", [P, 512], F32)) for i in range(2)] for n in ("x", "y", "h", "t"))
        zeroed, scattered, read = sw[0:3]
        gathered = sw[3:3 + R]
        stored = [sem(f"s_stored{i}") for i in range(R)]
        x_turned, x_hi, x_lo = sem("s_x_turned"), sem("s_x_hi_done"), sem("s_x_lo_done")
        h_made, gelu = sem("s_h_made"), sem("s_gelu_done")
        g_turned, g_hi, g_lo = sem("s_g_turned"), sem("s_g_hi_done"), sem("s_g_lo_done")
        y_made, y_copied = sem("s_y_made"), sem("s_y_copied")

        def exists(j):
            return not isinstance(j, int) or 0 <= j < T1

        def all_steps(eng, step):
            for j in range(-2, 2 * R):
                step(j, j % R)
            with eng.Fori(2, T1 // R - 1) as i:
                for p in range(R):
                    step(i * R + p, p)
            for j in range(T1 - R, T1 + 1):
                step(j, j % R)

        with nc.Block() as block:
            @block.gpsimd
            def _(pool):
                pool.dma_start(table.rearrange("(p c) o -> p (c o)", p=P), cst["zero"][:, 0:T1]).then_inc(zeroed, 16)
                pool.wait_ge(zeroed, 16)
                for t in range(TT):
                    pool.indirect_dma_start(out=table, out_offset=bass.IndirectOffsetOnAxis(ap=r["scatter"][:, 0, t:t + 1].bitcast(U32), axis=0),
                                            in_=cst["token"][:, t:t + 1], in_offset=None).then_inc(scattered, 16)
                pool.wait_ge(scattered, 16 * TT)
                pool.dma_start(ids[:, :], table.rearrange("(p j) o -> p (j o)", p=P)).then_inc(read, 16)
                pool.wait_ge(read, 16)
                for j in range(T1):
                    if j >= R:
                        pool.wait_ge(x_turned, j - R + 1)
                    pool.indirect_dma_start(out=xr[:, j % R, :], out_offset=None, in_=xn_rows,
                                            in_offset=bass.IndirectOffsetOnAxis(ap=ids[:, j:j + 1].bitcast(U32), axis=0)).then_inc(gathered[j % R], 16)

            @block.sync
            def _(sp):
                y_t = y_rows.rearrange("(j p) d -> p j d", p=P)

                def put(i, p):
                    j = i * R + p
                    sp.wait_ge(y_copied, j + 1)
                    sp.dma_start(y_t[:, bass.ds(j, 1), :], ys[:, p:p + 1, :]).then_inc(stored[p], 16)

                with sp.Fori(0, T1 // R) as i:
                    for p in range(R):
                        put(i, p)
                for p in range(R):
                    sp.wait_ge(stored[p], 16 * (T1 // R))

            @block.scalar
            def _(act):
                def step(j, p):
                    if exists(j + 1):
                        act.wait_ge(h_made, j + 2)
                        if due(j):
                            act.wait_ge(g_turned, j)
                        act.activation(ge[:, (p + 1) % 2, :], hb[(p + 1) % 2][:, :], ACT.Gelu).then_inc(gelu, 1)
                    if exists(j):
                        act.wait_ge(g_turned, j + 1)
                        if due(j - 1):
                            act.wait_ge(y_made, j - 1)
                        act.activation(gh[:, p % 2, :], tb[p % 2][:, :], ACT.Copy).then_inc(g_hi, 1)
                    if exists(j + 2):
                        act.wait_ge(x_turned, j + 3)
                        if due(j + 1):
                            act.wait_ge(h_made, j + 1)
                        act.activation(xh[:, p % 2].rearrange("p k c -> p (k c)"), xb[p % 2][:, 0:D], ACT.Copy).then_inc(x_hi, 1)

                all_steps(act, step)

            @block.vector
            def _(dve):
                def step(j, p):
                    if exists(j):
                        dve.wait_ge(g_hi, j + 1)
                        dve.tensor_tensor(gl[:, p % 2, :], tb[p % 2][:, :], gh[:, p % 2, :].bitcast(F32), ALU.subtract).then_inc(g_lo, 1)
                    if exists(j + 2):
                        dve.wait_ge(x_hi, j + 3)
                        dve.tensor_tensor(xl[:, p % 2].rearrange("p k c -> p (k c)"), xb[p % 2][:, 0:D],
                                          xh[:, p % 2].rearrange("p k c -> p (k c)").bitcast(F32), ALU.subtract).then_inc(x_lo, 1)
                    if exists(j - 1):
                        q = (p - 1) % R
                        dve.wait_ge(y_made, j)
                        if not (isinstance(j, int) and j - 1 < R):
                            dve.wait_ge(stored[q], (j - 1 - q) * (16 // R))
                        dve.tensor_copy(ys[:, q, :], yb[q % 2][:, 0:D]).then_inc(y_copied, 1)

                all_steps(dve, step)

            @block.tensor
            def _(pe):
                def hidden(j, p):
                    e = pe.value_load(tile_expert[0:1, bass.ds(j, 1)], min_val=0, max_val=E1 - 1)
                    pe.wait_ge(x_hi, j + 1)
                    pe.wait_ge(x_lo, j + 1)
                    if due(j - 1):
                        pe.wait_ge(gelu, j - 1)
                    for k in range(KD):
                        w = bass.ds(e * 1024 + k * H1, H1)
                        x = (xh[:, p % 2, k, :], xl[:, p % 2, k, :])
                        pe.matmul(hb[p % 2][:, :], x[0], ws.hi[0][:, w], start=k == 0, stop=False)
                        pe.matmul(hb[p % 2][:, :], x[0], ws.lo[0][:, w], start=False, stop=False)
                        ins = pe.matmul(hb[p % 2][:, :], x[1], ws.hi[0][:, w], start=False, stop=k == KD - 1)
                    ins.then_inc(h_made, 1)

                def turn_hidden(j, p):
                    pe.wait_ge(gelu, j + 1)
                    if due(j - 1):
                        pe.wait_ge(g_hi, j - 1)
                        pe.wait_ge(g_lo, j - 1)
                    for m in range(HC):
                        c = slice(m * P, (m + 1) * P)
                        ins = pe.transpose(tb[p % 2][:, c], ge[:, p % 2, c], ident[:, :])
                    ins.then_inc(g_turned, 1)

                def turn_rows(j, p):
                    pe.wait_ge(gathered[p], (j - p) * (16 // R) + 16)
                    if due(j - 1):
                        pe.wait_ge(x_hi, j - 1)
                        pe.wait_ge(x_lo, j - 1)
                    for k in range(KD):
                        ins = pe.transpose(xb[p % 2][:, k * P:(k + 1) * P], xr[:, p, k * P:(k + 1) * P], ident[:, :])
                    ins.then_inc(x_turned, 1)

                def back(j, p):
                    e = pe.value_load(tile_expert[0:1, bass.ds(j, 1)], min_val=0, max_val=E1 - 1)
                    pe.wait_ge(g_hi, j + 1)
                    pe.wait_ge(g_lo, j + 1)
                    if due(j - 1):
                        pe.wait_ge(y_copied, j - 1)
                    out = yb[p % 2][:, 0:D]
                    for m in range(HC):
                        w = bass.ds(e * 1024 + m * D, D)
                        g = (gh[:, p % 2, m * P:(m + 1) * P], gl[:, p % 2, m * P:(m + 1) * P])
                        pe.matmul(out, g[0], ws.hi[1][:, w], start=m == 0, stop=False)
                        pe.matmul(out, g[0], ws.lo[1][:, w], start=False, stop=False)
                        ins = pe.matmul(out, g[1], ws.hi[1][:, w], start=False, stop=m == HC - 1)
                    ins.then_inc(y_made, 1)

                def step(j, p):
                    if exists(j + 1):
                        hidden(j + 1, (p + 1) % R)
                    if exists(j):
                        turn_hidden(j, p)
                    if exists(j + 2):
                        turn_rows(j + 2, (p + 2) % R)
                    if exists(j - 1):
                        back(j - 1, (p - 1) % R)

                all_steps(pe, step)


def store(nc, x_sb, out):
    with ExitStack() as ctx:
        stored = ctx.enter_context(nc.semaphore("x_stored"))
        with nc.Block() as block:
            @block.sync
            def _(sp):
                o = out.rearrange("b (t p) d -> b p t d", p=P)
                for b in range(B):
                    sp.dma_start(o[b], x_sb[:, b * TB:(b + 1) * TB, :]).then_inc(stored, 16)
                sp.wait_ge(stored, 16 * B)



def clear_semaphores(nc):
    free = sorted(nc.released_uncleared_semaphores)
    starts = [n for n in free if n - 1 not in free]
    ends = [n + 1 for n in free if n + 1 not in free]
    with nc.Block() as block:
        @block.gpsimd
        def _(pool):
            for a, b in zip(starts, ends):
                pool.sem_clear(range(a, b))


def build(nc, io, out):
    with ExitStack() as ctx:
        x_sb = ctx.enter_context(nc.sbuf_tensor("x_sb", [P, TT, D], F32))
        ident = ctx.enter_context(nc.sbuf_tensor("ident", [P, P], F32))
        dram = lambda n, s, d=F32: nc.dram_tensor(n, s, d, kind="Internal").ap()
        with ExitStack() as c2:
            kvT = c2.enter_context(nc.sbuf_tensor("kvT", [P, KD, B * KEYS], F32))
            embed(nc, io, x_sb, ident, kvT)
            latent_attention(nc, io, x_sb, ident, kvT)
        sw0, sw1 = ([ctx.enter_context(nc.semaphore(f"software_dma{layer}_{i}")) for i in range(15)] for layer in range(2))
        cst = constants(nc, ctx)
        xn_rows = dram("xn_rows", [TOK, D])
        y_rows = dram("y_rows", [SLOTS0, D])
        table = dram("slot_token", [SLOTS0, 1], I32)
        with ExitStack() as c2:
            logits = c2.enter_context(nc.sbuf_tensor("logits", [P, TT, E0], F32))
            ids = c2.enter_context(nc.sbuf_tensor("slot_ids", [P, E0, NT0], I32))
            r = slot_arrays(nc, c2, 2)
            with ExitStack() as c3:
                xh, xl = (c3.enter_context(nc.sbuf_tensor(n, [P, KD, TOK], F32R)) for n in ("xT_hi", "xT_lo"))
                normalise(nc, x_sb, ident, xh, xl, xn_rows, io["L0_ffn_gate_w"], E0, logits)
                route0(nc, io, cst, logits, r)
                shared_experts(nc, io, cst, x_sb, xh, xl, table, ids, r["scatter"], sw0)
            routed_experts(nc, io, ident, xn_rows, ids, y_rows, sw0)
            combine(nc, x_sb, y_rows, r["slot"], r["weight"], 2, "combine0", sw0)
        clear_semaphores(nc)
        q_hi, q_lo = dram("q_hi", [D, TOK]), dram("q_lo", [D, TOK])
        with ExitStack() as c2:
            xh, xl = (c2.enter_context(nc.sbuf_tensor(n, [P, KD, TOK], F32R)) for n in ("xT1_hi", "xT1_lo"))
            normalise(nc, x_sb, ident, xh, xl, None, None, 0, None, "c")
            context_queries(nc, io, x_sb, xh, xl, q_hi, q_lo)
        with ExitStack() as c2:
            sb = lambda n, s, d=F32: c2.enter_context(nc.sbuf_tensor(n, s, d))
            ks = sb("keys_stack", [97, B, 8, 2, S], F32R)
            vm = sb("values_main", [P, B, 16, 32])
            vt = sb("values_rest", [P, B, GRP, P])
            context_keys(nc, io, ident, ks, vm, vt)
            context_attention(nc, io, x_sb, ident, q_hi, q_lo, ks, vm, vt)
        xn_rows, y_rows = dram("xn1_rows", [TOK, D]), dram("y1_rows", [SLOTS1, D])
        table = dram("slot_token1", [SLOTS1, 1], I32)
        with ExitStack() as c2:
            r = slot_arrays(nc, c2, 1, "r1_")
            tile_expert = c2.enter_context(nc.sbuf_tensor("tile_expert", [P, T1], I32))
            with ExitStack() as c3:
                ws = ResidentWeights(nc, c3, io)
                with ExitStack() as c4:
                    logits = c4.enter_context(nc.sbuf_tensor("logits1", [P, TT, E1], F32))
                    with ExitStack() as c5:
                        xh, xl = (c5.enter_context(nc.sbuf_tensor(n, [P, KD, 1024], F32R)) for n in ("xT2_hi", "xT2_lo"))
                        normalise(nc, x_sb, ident, xh, xl, xn_rows, io["L1_ffn_Wg"], E1, logits, "d")
                    route1(nc, io, cst, logits, r, tile_expert, ws)
                sorted_experts(nc, io, ident, cst, xn_rows, table, y_rows, r, tile_expert, ws, sw1)
            combine(nc, x_sb, y_rows, r["slot"], r["weight"], 1, "combine1", sw1)
        store(nc, x_sb, out)

INPUTS = (
    "x", "ctx_1024", "mask_BxS2_bk0", "L0_xattn_ln_m_w", "L0_xattn_ln_m_b", "L0_xattn_ln_l_w",
    "L0_xattn_ln_l_b", "L0_xattn_Wq", "L0_xattn_Wkv", "L0_xattn_Wout", "L0_ffn_gate_w", "L0_ffn_gate_b",
    "L0_ffn_ew1", "L0_ffn_ew3", "L0_ffn_ew2", "L0_ffn_sw1", "L0_ffn_sw3", "L0_ffn_sw2", "L1_xattn_q_w",
    "L1_xattn_q_b", "L1_xattn_kv_w", "L1_xattn_kv_b", "L1_xattn_proj_w", "L1_xattn_proj_b", "L1_ffn_Wg",
    "L1_ffn_W1", "L1_ffn_W2")


def kernel(**inputs):
    import concourse.bacc as bacc
    from concourse.bass_utils import run_bass_kernel_spmd

    nc = bacc.Bacc("TRN2", target_bir_lowering=False, num_devices=1)
    arrays, io = {}, {}
    for name in INPUTS:
        a = np.ascontiguousarray(inputs[name])
        arrays[f"in_{name}"] = a
        io[name] = nc.dram_tensor(f"in_{name}", a.shape, mybir.dt.from_np(a.dtype), kind="ExternalInput").ap()
    out = nc.dram_tensor("out_x", (B, N, D), F32, kind="ExternalOutput").ap()
    build(nc, io, out)
    got = run_bass_kernel_spmd(nc, [arrays], core_ids=[0])
    return got.results[0]["out_x"]
```

```python
from contextlib import ExitStack

import numpy as np

import concourse.bass as bass
from concourse import mybir

F32 = mybir.dt.float32
F32R = mybir.dt.float32r
I32 = mybir.dt.int32
U32 = mybir.dt.uint32
ALU = mybir.AluOpType
ACT = mybir.ActivationFunctionType
AX = mybir.AxisListType

P = 128
B, N, S, D = 4, 1024, 154, 256
TOK = B * N
TT = TOK // P
TB = N // P
KD = D // P
S1 = S - P
EPS = 1e-5

KEYS = N + S
PAIRS = 4
DH = 64
KC = -(-KEYS // P)
KREST = KEYS - (KC - 1) * P


class Steps:

    def __init__(self, eng, sem, it=0, per=0, base=0):
        self.eng, self.sem, self.it, self.per, self.base, self.n = eng, sem, it, per, base, 0

    def done(self, instruction):
        instruction.then_inc(self.sem, 1)
        self.n += 1

    def wait(self):
        self.eng.wait_ge(self.sem, self.it * self.per + (self.base + self.n))

    def then(self, instruction):
        self.done(instruction)
        self.wait()


def due(count):
    return not isinstance(count, int) or count > 0


def spans(n, width=512):
    return [(a, min(width, n - a)) for a in range(0, n, width)]


def inverse_root(act, dve, steps, root_done, ve, root, y, tmp, count):
    if act is not None:
        act.activation(root, ve, ACT.Sqrt).then_inc(root_done, 1)
        return
    dve.wait_ge(root_done, count)
    steps.then(dve.reciprocal(y, root))
    steps.then(dve.tensor_tensor(tmp, y, y, ALU.mult))
    steps.then(dve.tensor_tensor(tmp, tmp, ve, ALU.mult))
    steps.then(dve.tensor_scalar(tmp, tmp, -0.5, 1.5, ALU.mult, ALU.add))
    steps.then(dve.tensor_tensor(y, y, tmp, ALU.mult))


def embed(nc, io, x_sb, ident, kvT):
    with ExitStack() as ctx:
        sb = lambda n, s, d=F32: ctx.enter_context(nc.sbuf_tensor(n, s, d))
        sem = lambda n: ctx.enter_context(nc.semaphore(n))
        ctx0 = sb("ctx_rows0", [P, B, D])
        ctx1 = sb("ctx_rows1", [S1, B, D])
        NS = TT + 2 * B
        stats = sb("ln0_stats", [P, NS, 6])
        mv = sb("ln0_mean_var", [P, NS, 2])
        ve = sb("ln0_var_eps", [P, NS])
        root = sb("ln0_root", [P, NS])
        inv = sb("ln0_inv", [P, NS])
        tmp = sb("ln0_tmp", [P, NS])
        ve2 = sb("ln0_var_eps2", [P, TT])
        root2 = sb("ln0_root2", [P, TT])
        inv2 = sb("ln0_inv2", [P, TT])
        tmp2 = sb("ln0_tmp2", [P, TT])
        lw = sb("ln_l_affine", [P, 2, KD])
        mw = sb("ln_m_affine", [P, 2, KD])
        xn = sb("ln0_rows", [P, 2, 4, D])
        cn = sb("ln0_ctx_rows", [P, 2, D])
        pt = [ctx.enter_context(nc.psum_tensor(f"ln0_T{i}", [P, 512], F32)) for i in range(6)]
        x_loaded = [sem(f"x_loaded{b}") for b in range(B)]
        c_loaded = sem("ctx_loaded")
        w_loaded = sem("ln_affine_loaded")
        identity_made = sem("identity_made")
        dve_step = sem("ln0_dve_step")
        var_ready = sem("ln0_var_ready")
        root_done = sem("ln0_root_done")
        rows_ready = sem("ln0_rows_ready")
        turned = sem("ln0_turned")
        copied = sem("ln0_copied")

        with nc.Block() as block:
            @block.sync
            def _(sp):
                x_t = io["x"].rearrange("b (t p) d -> b p t d", p=P)
                for b in range(B):
                    sp.dma_start(x_sb[:, b * TB:(b + 1) * TB, :], x_t[b]).then_inc(x_loaded[b], 16)

            @block.gpsimd
            def _(pool):
                pool.memset(ident[:, :], 0.0).then_inc(identity_made, 1)
                pool.wait_ge(identity_made, 1)
                pool.affine_select(out=ident[:, :], in_=ident[:, :], compare_op=ALU.not_equal, fill=1.0,
                                   base=0, pattern=[[-1, P]], channel_multiplier=1).then_inc(identity_made, 1)

            @block.scalar
            def _(act):
                act.dma_start(ctx0[:, :, :], io["ctx_1024"][:, 0:P, :].rearrange("b p d -> p b d")).then_inc(c_loaded, 16)
                act.dma_start(ctx1[:, :, :], io["ctx_1024"][:, P:S, :].rearrange("b p d -> p b d")).then_inc(c_loaded, 16)
                for t, names in ((lw, ("L0_xattn_ln_l_w", "L0_xattn_ln_l_b")), (mw, ("L0_xattn_ln_m_w", "L0_xattn_ln_m_b"))):
                    for j, name in enumerate(names):
                        act.dma_start(t[:, j, :], io[name].rearrange("(k p) -> p k", p=P), allow_slow_non_contiguous=True).then_inc(w_loaded, 16)
                act.wait_ge(var_ready, 1)
                inverse_root(act, None, None, root_done, ve[:, :], root[:, :], None, None, 0)
                act.wait_ge(var_ready, 2)
                inverse_root(act, None, None, root_done, ve2[:, :], root2[:, :], None, None, 0)
                act.wait_ge(w_loaded, 64)
                with act.Fori(0, B) as b:
                    for u in range(3):
                        act.wait_ge(turned, b * 3 + (u + 1))
                        for k in range(KD):
                            w = lw if u < 2 else mw
                            cols, n = (u * 512, 512) if u < 2 else (N, S)
                            out = kvT[:, k, bass.ds(b * KEYS + cols, n)]
                            ins = act.activation(out, pt[2 * u + k][:, 0:n], ACT.Identity,
                                                 bias=w[:, 1, k:k + 1], scale=w[:, 0, k:k + 1])
                        ins.then_inc(copied, 1)

            @block.vector
            def _(dve):
                step = Steps(dve, dve_step)
                step.then(dve.memset(mv[:, :, :], 1.0))
                for b in range(B):
                    dve.wait_ge(x_loaded[b], 16)
                    for j in range(TB):
                        t = b * TB + j
                        step.done(dve.bn_stats(stats[:, t, :], x_sb[:, t, :]))
                dve.wait_ge(c_loaded, 32)
                for b in range(B):
                    step.done(dve.bn_stats(stats[:, TT + b, :], ctx0[:, b, :]))
                    step.done(dve.bn_stats(stats[0:S1, TT + B + b, :], ctx1[:, b, :]))
                step.wait()
                for t in range(NS):
                    r = P if t < TT + B else S1
                    step.done(dve.bn_aggr(mv[0:r, t, :], stats[0:r, t, :]))
                step.wait()
                dve.tensor_scalar(ve[:, :], mv[:, :, 1], EPS, None, ALU.add).then_inc(var_ready, 1)
                inverse_root(None, dve, step, root_done, ve[:, :], root[:, :], inv[:, :], tmp[:, :], 1)
                lat = slice(0, TT)
                step.then(dve.tensor_tensor(tmp[:, lat], inv[:, lat], inv[:, lat], ALU.mult))
                step.then(dve.tensor_tensor(tmp[:, lat], tmp[:, lat], mv[:, lat, 1], ALU.mult))
                dve.tensor_scalar(ve2[:, :], tmp[:, lat], EPS, None, ALU.add).then_inc(var_ready, 1)
                dve.wait_ge(var_ready, 2)
                inverse_root(None, dve, step, root_done, ve2[:, :], root2[:, :], inv2[:, :], tmp2[:, :], 2)
                step.then(dve.tensor_tensor(inv[:, lat], inv[:, lat], inv2[:, :], ALU.mult))
                def batch(b):
                    for u in range(2):
                        if due(b * 3):
                            dve.wait_ge(turned, b * 3)
                        for j in range(4):
                            t = b * TB + (u * 4 + j)
                            ins = dve.tensor_scalar(xn[:, u, j, :], x_sb[:, bass.ds(t, 1), :].rearrange("p a d -> p (a d)"),
                                                    mv[:, bass.ds(t, 1), 0], inv[:, bass.ds(t, 1)], ALU.subtract, ALU.mult)
                        ins.then_inc(rows_ready, 1)
                    t0, t1 = b + TT, b + (TT + B)
                    dve.tensor_scalar(cn[:, 0, :], ctx0[:, bass.ds(b, 1), :].rearrange("p a d -> p (a d)"),
                                      mv[:, bass.ds(t0, 1), 0], inv[:, bass.ds(t0, 1)], ALU.subtract, ALU.mult)
                    dve.tensor_scalar(cn[0:S1, 1, :], ctx1[:, bass.ds(b, 1), :].rearrange("p a d -> p (a d)"),
                                      mv[0:S1, bass.ds(t1, 1), 0], inv[0:S1, bass.ds(t1, 1)],
                                      ALU.subtract, ALU.mult).then_inc(rows_ready, 1)

                batch(0)
                with dve.Fori(1, B) as b:
                    batch(b)

            @block.tensor
            def _(pe):
                def batch(b):
                    for u in range(3):
                        pe.wait_ge(rows_ready, b * 3 + (u + 1))
                        if due(b * 3):
                            pe.wait_ge(copied, b * 3)
                        for k in range(KD):
                            cols = slice(k * P, (k + 1) * P)
                            if u < 2:
                                for j in range(4):
                                    ins = pe.transpose(pt[2 * u + k][:, j * P:(j + 1) * P], xn[:, u, j, cols], ident[:, :])
                            else:
                                pe.transpose(pt[4 + k][:, 0:P], cn[:, 0, cols], ident[:, :])
                                ins = pe.transpose(pt[4 + k][:, P:S], cn[0:S1, 1, cols], ident[0:S1, 0:S1])
                        ins.then_inc(turned, 1)

                pe.wait_ge(identity_made, 2)
                batch(0)
                with pe.Fori(1, B) as b:
                    batch(b)


def latent_attention(nc, io, x_sb, ident, kvT):
    ROUNDS = B * PAIRS
    G, GQ = 4, 256
    SC = KEYS
    with ExitStack() as ctx:
        sb = lambda n, s, d=F32: ctx.enter_context(nc.sbuf_tensor(n, s, d))
        sem = lambda n: ctx.enter_context(nc.semaphore(n))
        w_pair = sb("w_pair", [P, 3, KD, P])
        w_out = sb("w_out", [P, PAIRS, D])
        q2 = sb("q_halves", [P, 2, 2, N], F32R)
        own_hi = sb("k_own_high", [P, SC], F32R)
        own_lo = sb("k_own_low", [P, SC], F32R)
        k_hi = sb("k_high", [P, 2, 2, SC], F32R)
        k_lo = sb("k_low", [P, 2, 2, SC], F32R)
        vT = sb("vT", [P, SC])
        v = sb("v_pair", [P, 2, KC, P])
        probs = sb("probs", [P, 8, SC])
        sums = sb("prob_sums", [P, 8])
        neg_max = sb("neg_max", [P, 8])
        recip = sb("prob_recip", [P, 8])
        pT = sb("probsT", [P, 2, 512])
        oT = sb("outT", [P, GQ])
        tile = [ctx.enter_context(nc.psum_tensor(f"tile{j}", [P, 1536], F32)) for j in range(2)]
        turn = ctx.enter_context(nc.psum_tensor("turn", [P, 512], F32))
        outp = ctx.enter_context(nc.psum_tensor("out_acc", [P, 512], F32))

        wout_loaded = sem("wout_loaded")
        w_loaded = sem("w_pair_loaded")
        q_made = sem("q_made")
        k_made = sem("k_made")
        v_made = sem("v_made")
        v_turned = sem("v_turned")
        q_hi_done = sem("q_hi_done")
        q_lo_done = sem("q_lo_done")
        k_hi_done = sem("k_hi_done")
        k_lo_done = sem("k_lo_done")
        k_placed = [sem(f"k_placed{j}") for j in range(2)]
        vT_done = sem("vT_done")
        v_done = sem("v_done")
        scores = sem("scores_made")
        maxed = sem("max_done")
        exped = sem("exp_done")
        recips = sem("recip_done")
        scaled = sem("probs_scaled")
        p_turned = sem("probs_turned")
        pT_act = sem("pT_act_done")
        pT_dve = sem("pT_dve_done")
        o_made = sem("out_made")
        o_done = sem("out_done")
        y_made = sem("y_made")
        y_added = sem("y_added")
        ACT_CHUNKS = (0, 1, 2, 4, 6, 8)
        DVE_CHUNKS = (3, 5, 7, 9)
        assert len(ACT_CHUNKS) + len(DVE_CHUNKS) == KC and KC % 2 == 0
        PARTS = 3

        def share(n, part):
            return slice(-(-n * part // PARTS), -(-n * (part + 1) // PARTS))

        def wait_copied(eng, W, c):
            if c in ACT_CHUNKS:
                eng.wait_ge(pT_act, W * len(ACT_CHUNKS) + (ACT_CHUNKS.index(c) + 1))
            else:
                eng.wait_ge(pT_dve, W * len(DVE_CHUNKS) + (DVE_CHUNKS.index(c) + 1))

        def chunk(c):
            return P if c < KC - 1 else KREST

        def tile_of(w, u):
            return tile[(w * 5 + u) % 2]

        with nc.Block() as block:
            @block.sync
            def _(sp):
                wq = io["L0_xattn_Wq"].rearrange("(k p) n -> p k n", p=P)
                wkv = io["L0_xattn_Wkv"].rearrange("(k p) n -> p k n", p=P)

                def load(i):
                    if due(i):
                        sp.wait_ge(v_made, i)
                    c = (i % PAIRS) * P
                    sp.dma_start(w_pair[:, 0], wq[:, :, bass.ds(c, P)]).then_inc(w_loaded, 16)
                    sp.dma_start(w_pair[:, 1], wkv[:, :, bass.ds(c, P)]).then_inc(w_loaded, 16)
                    sp.dma_start(w_pair[:, 2], wkv[:, :, bass.ds(c + PAIRS * P, P)]).then_inc(w_loaded, 16)

                def place(i, par):
                    sp.wait_ge(k_hi_done, i + 1)
                    sp.wait_ge(k_lo_done, i + 1)
                    for own, twice in ((own_hi, k_hi), (own_lo, k_lo)):
                        for h in range(2):
                            for r in range(2):
                                sp.dma_start(twice[r * DH:(r + 1) * DH, par, h, :].bitcast(F32),
                                             own[h * DH:(h + 1) * DH, :].bitcast(F32)).then_inc(k_placed[par], 16)

                load(0)
                sp.dma_start(w_out[:, :, :], io["L0_xattn_Wout"].rearrange("(q p) n -> p q n", p=P)).then_inc(wout_loaded, 16)
                place(0, 0)
                load(1)
                with sp.Fori(0, ROUNDS // 2 - 1) as m:
                    place(m * 2 + 1, 1)
                    load(m * 2 + 2)
                    place(m * 2 + 2, 0)
                    load(m * 2 + 3)
                place(ROUNDS - 1, 1)

            @block.tensor
            def _(pe):
                def project(j, which, dst, part):
                    if which == 0 and part == 0:
                        pe.wait_ge(w_loaded, j * 48 + 48)
                    todo = [(a, n, k) for a, n in spans(N if which == 0 else SC) for k in range(KD)]
                    for a, n, k in todo[share(len(todo), part)]:
                        ins = pe.matmul(dst[:, a:a + n], w_pair[:, which, k, :], kvT[:, k, bass.ds((j // PAIRS) * KEYS + a, n)],
                                        start=k == 0, stop=k == KD - 1)
                    if part == PARTS - 1:
                        ins.then_inc((q_made, k_made, v_made)[which], 1)

                def turn_v(j, dst, part):
                    if part == 0:
                        pe.wait_ge(vT_done, j + 1)
                    for c in range(KC)[share(KC, part)]:
                        ins = pe.transpose(dst[0:chunk(c), c * P:(c + 1) * P], vT[:, c * P:c * P + chunk(c)], ident[:, :])
                    if part == PARTS - 1:
                        ins.then_inc(v_turned, 1)

                def wait_unit(i, w):
                    if w == 0:
                        pe.wait_ge(q_hi_done, i * 2 + 4)
                        pe.wait_ge(q_lo_done, i * 2 + 4)
                    elif w == 1:
                        pe.wait_ge(k_hi_done, i + 2)
                        pe.wait_ge(k_lo_done, i + 2)
                    elif w == 2:
                        pe.wait_ge(vT_done, i + 2)
                    else:
                        pe.wait_ge(v_done, i + 2)

                def score(par, g, j, dst, part):
                    h = j // 2
                    q = q2[:, par, h, g * GQ + (j % 2) * P:g * GQ + (j % 2 + 1) * P]
                    cut = spans(SC)
                    for a, n in {0: cut[:1], 1: cut[1:], None: cut}[part]:
                        pe.matmul(dst[:, a:a + n], q, k_hi[:, par, h, a:a + n], start=True, stop=False)
                        ins = pe.matmul(dst[:, a:a + n], q, k_lo[:, par, h, a:a + n], start=False, stop=True)
                    if part != 0:
                        ins.then_inc(scores, 1)

                def turn_probs(W, w, c):
                    if c == 0:
                        pe.wait_ge(scaled, W * 4 + 4)
                        if due(W):
                            wait_copied(pe, W - 1, KC - 1)
                    else:
                        wait_copied(pe, W, c - 1)
                        if c == 2 and due(W):
                            pe.wait_ge(y_added, W)
                    for j in range(4):
                        ins = pe.transpose(turn[0:chunk(c), j * P:(j + 1) * P],
                                           probs[:, 4 * (w % 2) + j, c * P:c * P + chunk(c)], ident[:, :])
                    ins.then_inc(p_turned, 1)

                def weigh(W, par, c):
                    if c == 0 and due(W):
                        pe.wait_ge(o_done, W)
                    wait_copied(pe, W, c)
                    for h in range(2):
                        ins = pe.matmul(outp[h * DH:(h + 1) * DH, 0:GQ], v[0:chunk(c), par, c, h * DH:(h + 1) * DH],
                                        pT[0:chunk(c), c % 2, h * GQ:(h + 1) * GQ], start=c == 0, stop=c == KC - 1)
                    if c == KC - 1:
                        ins.then_inc(o_made, 1)

                def to_width(i, W):
                    pe.wait_ge(o_done, W + 1)
                    for t in range(2):
                        ins = pe.matmul(turn[:, t * D:(t + 1) * D], oT[:, t * P:(t + 1) * P],
                                        w_out[:, bass.ds(i % PAIRS, 1), :].rearrange("p a n -> p (a n)"), start=True, stop=True)
                    ins.then_inc(y_made, 1)

                def window(i, par, w, last):
                    W = i * G + w
                    before = (i, par) if w else (i - 1, 1 - par)
                    more = not (last and w == G - 1)
                    npar, ng = (par, w + 1) if w < G - 1 else (1 - par, 0)
                    t = W * 4 + 4

                    def tile_score(j, part=None):
                        if not more:
                            return
                        if part != 1:
                            if j == 0:
                                pe.wait_ge(exped, t)
                                if w == G - 1:
                                    pe.wait_ge(k_placed[npar], ((i + 1 - npar) // 2) * 128 + 128)
                                    pe.wait_ge(q_hi_done, i * 2 + 4)
                                    pe.wait_ge(q_lo_done, i * 2 + 4)
                            elif j == 1 and w:
                                if not last:
                                    wait_unit(i, w - 1)
                            elif j == 1:
                                pe.wait_ge(v_done, i + 1)
                            else:
                                pe.wait_ge(exped, t + (j - 1))
                        score(npar, ng, j, tile_of(w, j), part)

                    def extra(part):
                        if last:
                            return
                        if part == 0:
                            pe.wait_ge(exped, t + 3)
                        if w < 3:
                            project(i + 1, w, tile_of(w, 4), part)
                        else:
                            turn_v(i + 1, tile_of(w, 4), part)

                    for c in range(KC):
                        turn_probs(W, w, c)
                        if c:
                            weigh(W, par, c - 1)
                        elif due(W):
                            weigh(W - 1, before[1], KC - 1)
                        if c == 0:
                            tile_score(0)
                        if c == 1:
                            tile_score(1, 0)
                            if due(W):
                                wait_copied(pe, W, 1)
                                to_width(before[0], W - 1)
                            tile_score(1, 1)
                        if c in (2, 3):
                            tile_score(2, c - 2)
                        if c in (4, 5):
                            tile_score(3, c - 4)
                        if 6 <= c < 6 + PARTS:
                            extra(c - 6)

                def round_(i, par, last=False):
                    for w in range(G):
                        window(i, par, w, last)

                for part in range(PARTS):
                    project(0, 0, tile[0], part)
                for part in range(PARTS):
                    project(0, 1, tile[1], part)
                pe.wait_ge(q_lo_done, 2)
                pe.wait_ge(q_hi_done, 2)
                for part in range(PARTS):
                    project(0, 2, tile[0], part)
                pe.wait_ge(k_hi_done, 1)
                pe.wait_ge(k_lo_done, 1)
                for part in range(PARTS):
                    turn_v(0, tile[1], part)
                pe.wait_ge(k_placed[0], 128)
                for j in range(4):
                    if j == 0:
                        pe.wait_ge(v_done, 1)
                    if j >= 2:
                        pe.wait_ge(exped, j - 1)
                    score(0, 0, j, tile_of(-1, j), None)
                pe.wait_ge(wout_loaded, 16)
                round_(0, 0)
                round_(1, 1)
                with pe.Fori(1, ROUNDS // 2 - 1) as m:
                    round_(m * 2, 0)
                    round_(m * 2 + 1, 1)
                round_(ROUNDS - 2, 0)
                round_(ROUNDS - 1, 1, last=True)
                weigh(ROUNDS * G - 1, 1, KC - 1)
                wait_copied(pe, ROUNDS * G - 1, KC - 1)
                to_width(ROUNDS - 1, ROUNDS * G - 1)

            @block.scalar
            def _(act):
                def q_high(j, par, src):
                    act.wait_ge(q_made, j + 1)
                    for h in range(2):
                        r = slice(h * DH, (h + 1) * DH)
                        act.activation(q2[r, par, h, :], src[r, 0:N], ACT.Copy, scale=DH ** -0.5).then_inc(q_hi_done, 1)

                def k_high(j, src):
                    act.wait_ge(k_made, j + 1)
                    act.activation(own_hi[:, :], src[:, 0:SC], ACT.Copy).then_inc(k_hi_done, 1)

                def copy_vT(j, src):
                    act.wait_ge(v_made, j + 1)
                    act.activation(vT[:, :], src[:, 0:SC], ACT.Copy).then_inc(vT_done, 1)

                def copy_v(j, par, src):
                    act.wait_ge(v_turned, j + 1)
                    act.activation(v[:, par, 0:KC - 1, :], src[:, 0:(KC - 1) * P].rearrange("p (c n) -> p c n", n=P), ACT.Copy)
                    act.activation(v[0:KREST, par, KC - 1, :], src[0:KREST, (KC - 1) * P:KC * P], ACT.Copy).then_inc(v_done, 1)

                def exp(t, s, src):
                    act.wait_ge(maxed, t + 1)
                    act.activation(probs[:, s, :], src[:, 0:SC], ACT.Exp, bias=neg_max[:, s:s + 1], accum_out=sums[:, s:s + 1]).then_inc(exped, 1)

                def copy_pT(W, c):
                    act.wait_ge(p_turned, W * KC + (c + 1))
                    act.activation(pT[0:chunk(c), c % 2, :], turn[0:chunk(c), :], ACT.Copy).then_inc(pT_act, 1)

                def copy_out(W):
                    act.wait_ge(o_made, W + 1)
                    act.activation(oT[:, :], outp[:, 0:GQ], ACT.Copy).then_inc(o_done, 1)

                def window(i, par, w, last):
                    W = i * G + w
                    for n in range(5):
                        copy_pT(W, 2 * n)
                        if n == 0 and due(W):
                            copy_out(W - 1)
                        if n == 0:
                            copy_pT(W, 1)
                        if n < 4 and not (last and w == G - 1):
                            exp(W * 4 + (4 + n), (w + 1) % 2 * 4 + n, tile_of(w, n))
                    if not last:
                        src = tile_of(w, 4)
                        if w == 0:
                            q_high(i + 1, 1 - par, src)
                        elif w == 1:
                            k_high(i + 1, src)
                        elif w == 2:
                            copy_vT(i + 1, src)
                        else:
                            copy_v(i + 1, 1 - par, src)

                def round_(i, par, last=False):
                    for w in range(G):
                        window(i, par, w, last)

                q_high(0, 0, tile[0])
                k_high(0, tile[1])
                copy_vT(0, tile[0])
                copy_v(0, 0, tile[1])
                for j in range(4):
                    exp(j, j, tile_of(-1, j))
                round_(0, 0)
                round_(1, 1)
                with act.Fori(1, ROUNDS // 2 - 1) as m:
                    round_(m * 2, 0)
                    round_(m * 2 + 1, 1)
                round_(ROUNDS - 2, 0)
                round_(ROUNDS - 1, 1, last=True)
                copy_out(ROUNDS * G - 1)

            @block.vector
            def _(dve):
                def q_low(j, par, src):
                    for h in range(2):
                        dve.wait_ge(q_hi_done, j * 2 + (h + 1))
                        r, o = slice(h * DH, (h + 1) * DH), slice((1 - h) * DH, (2 - h) * DH)
                        dve.scalar_tensor_tensor(out=q2[o, par, h, :], in0=src[r, 0:N], scalar=DH ** -0.5,
                                                 in1=q2[r, par, h, :].bitcast(F32), op0=ALU.mult,
                                                 op1=ALU.subtract).then_inc(q_lo_done, 1)

                def k_low(j, src):
                    dve.wait_ge(k_hi_done, j + 1)
                    dve.tensor_tensor(own_lo[:, :], src[:, 0:SC], own_hi[:, :].bitcast(F32), ALU.subtract).then_inc(k_lo_done, 1)

                def top(t, s, src):
                    dve.wait_ge(scores, t + 1)
                    dve.tensor_reduce(neg_max[:, s:s + 1], src[:, 0:SC], AX.X, ALU.max, negate=True).then_inc(maxed, 1)

                def invert(t, s):
                    dve.wait_ge(exped, t + 1)
                    dve.reciprocal(recip[:, s:s + 1], sums[:, s:s + 1]).then_inc(recips, 1)

                def scale(t, s):
                    dve.wait_ge(recips, t + 1)
                    dve.tensor_scalar(probs[:, s, :], probs[:, s, :], recip[:, s:s + 1], None, ALU.mult).then_inc(scaled, 1)

                def copy_pT(W, c):
                    dve.wait_ge(p_turned, W * KC + (c + 1))
                    dve.tensor_copy(pT[0:chunk(c), c % 2, :], turn[0:chunk(c), :]).then_inc(pT_dve, 1)

                def add(i, w, W):
                    dve.wait_ge(y_made, W + 1)
                    if due(W):
                        dve.wait_ge(y_added, W)
                    dst = x_sb[:, bass.ds((i // PAIRS) * TB + 2 * w, 2), :]
                    dve.tensor_tensor(dst, dst, turn[:, :].rearrange("p (t d) -> p t d", d=D), ALU.add).then_inc(y_added, 1)

                def window(i, par, w, last):
                    W = i * G + w
                    more = not (last and w == G - 1)
                    t, s = W * 4 + 4, (w + 1) % 2 * 4
                    if more:
                        top(t, s, tile_of(w, 0))
                    if due(W):
                        if w:
                            add(i, w - 1, W - 1)
                        else:
                            add(i - 1, G - 1, W - 1)
                    for n in range(4):
                        if more:
                            if n < 3:
                                top(t + (n + 1), s + n + 1, tile_of(w, n + 1))
                                copy_pT(W, 2 * n + 3)
                            invert(t + n, s + n)
                            scale(t + n, s + n)
                        if n == 3 or not more:
                            copy_pT(W, 2 * n + 3)
                    if not last and w < 2:
                        (q_low if w == 0 else k_low)(*((i + 1, 1 - par) if w == 0 else (i + 1,)), tile_of(w, 4))

                def round_(i, par, last=False):
                    for w in range(G):
                        window(i, par, w, last)

                q_low(0, 0, tile[0])
                k_low(0, tile[1])
                top(0, 0, tile_of(-1, 0))
                for j in range(1, 4):
                    top(j, j, tile_of(-1, j))
                    invert(j - 1, j - 1)
                    scale(j - 1, j - 1)
                invert(3, 3)
                scale(3, 3)
                round_(0, 0)
                round_(1, 1)
                with dve.Fori(1, ROUNDS // 2 - 1) as m:
                    round_(m * 2, 0)
                    round_(m * 2 + 1, 1)
                round_(ROUNDS - 2, 0)
                round_(ROUNDS - 1, 1, last=True)
                add(ROUNDS - 1, G - 1, ROUNDS * G - 1)


E0, H0, CAP0 = 16, 512, 640
SLOTS0 = E0 * CAP0
NEG = -3.0e38
HC = H0 // P
NT0 = CAP0 // P


def normalise(nc, x_sb, ident, xh, xl, rows, gate, E, logits, tag="", given=None):
    GT = 4
    NG = TT // GT
    places = xh.shape[2] // (GT * P)
    with ExitStack() as ctx:
        sb = lambda n, s, d=F32: ctx.enter_context(nc.sbuf_tensor(tag + n, s, d))
        sem = lambda n: ctx.enter_context(nc.semaphore(tag + n))
        stats = sb("ln_stats", [P, TT, 6]) if given is None else given
        mv = sb("ln_mean_var", [P, TT, 2])
        ve, root, inv, tmp = (sb(f"ln_{n}", [P, TT]) for n in ("ve", "root", "inv", "tmp"))
        xn = sb("ln_rows", [P, 2, GT, D])
        pt = [ctx.enter_context(nc.psum_tensor(f"{tag}ln_T{i}", [P, 512], F32)) for i in range(4)]
        pl = [ctx.enter_context(nc.psum_tensor(f"{tag}ln_L{i}", [P, 512], F32)) for i in range(2)]
        pr = [ctx.enter_context(nc.psum_tensor(f"{tag}ln_R{i}", [P, 512], F32)) for i in range(2)]
        dve_step, var_ready, root_done = sem("ln_dve_step"), sem("ln_var_ready"), sem("ln_root_done")
        rows_ready = sem("ln_rows_ready")
        turned = sem("ln_turned")
        hi_done = sem("ln_hi_done")
        lo_done = sem("ln_lo_done")
        stored = [sem(f"ln_rows_stored{i}") for i in range(2)]
        gate_loaded, gate_hi, gate_lo = sem("gate_loaded"), sem("gate_hi"), sem("gate_lo")
        multiplied = sem("logits_multiplied")
        summed = sem("logits_summed")
        if gate is not None:
            g32 = sb("gate32", [P, KD, E])
            g2 = sb("gate_halves", [P, KD, P], F32R)
            lt = sb("logits_T", [2 * E, 2, 512])
            zeroed = sem("gate_zeroed")
            copied, back = sem("logits_copied"), sem("logits_turned")

        with nc.Block() as block:
            @block.sync
            def _(sp):
                if gate is not None:
                    sp.dma_start(g32[:, :, :], gate.rearrange("(k p) e -> p k e", p=P)).then_inc(gate_loaded, 16)
                if rows is not None:
                    r = rows.rearrange("(g t p) d -> g p t d", p=P, t=GT)
                    for g in range(NG):
                        sp.wait_ge(rows_ready, g + 1)
                        sp.dma_start(r[g], xn[:, g % 2]).then_inc(stored[g % 2], 16)
                    for i in range(2):
                        sp.wait_ge(stored[i], 16 * (NG // 2))

            if gate is not None:
                @block.gpsimd
                def _(pool):
                    pool.memset(g2[:, :, :].bitcast(F32), 0.0).then_inc(zeroed, 1)

            @block.vector
            def _(dve):
                step = Steps(dve, dve_step)
                if given is None:
                    for t in range(TT):
                        step.done(dve.bn_stats(stats[:, t, :], x_sb[:, t, :]))
                    step.wait()
                for t in range(TT):
                    step.done(dve.bn_aggr(mv[:, t, :], stats[:, t, :]))
                step.wait()
                dve.tensor_scalar(ve[:, :], mv[:, :, 1], EPS, None, ALU.add).then_inc(var_ready, 1)
                inverse_root(None, dve, step, root_done, ve[:, :], root[:, :], inv[:, :], tmp[:, :], 1)
                if gate is not None:
                    dve.wait_ge(gate_loaded, 16)
                    dve.wait_ge(gate_hi, 1)
                    dve.tensor_tensor(g2[:, :, E:2 * E], g32[:, :, :], g2[:, :, 0:E].bitcast(F32), ALU.subtract).then_inc(gate_lo, 1)
                for g in range(NG + 4):
                    if g < NG:
                        if g >= 2:
                            dve.wait_ge(turned, g - 1)
                            if rows is not None:
                                dve.wait_ge(stored[g % 2], 16 * (g // 2))
                        for j in range(GT):
                            t = g * GT + j
                            ins = dve.tensor_scalar(xn[:, g % 2, j, :], x_sb[:, t, :], mv[:, t, 0:1], inv[:, t:t + 1],
                                                    ALU.subtract, ALU.mult)
                        ins.then_inc(rows_ready, 1)
                    if 1 <= g <= NG:
                        dve.wait_ge(hi_done, g)
                        for k in range(KD):
                            c = slice((g - 1) % places * 512, ((g - 1) % places + 1) * 512)
                            ins = dve.tensor_tensor(xl[:, k, c], pt[(g - 1) % 2 * 2 + k][:, :], xh[:, k, c].bitcast(F32), ALU.subtract)
                        ins.then_inc(lo_done, 1)
                    if gate is not None and g >= 4:
                        dve.wait_ge(back, g - 3)
                        dve.tensor_reduce(logits[:, (g - 4) * GT:(g - 3) * GT, :],
                                          pr[g % 2][:, 0:GT * 2 * E].rearrange("p (t h e) -> p t e h", t=GT, h=2),
                                          AX.X, ALU.add).then_inc(summed, 1)

            @block.scalar
            def _(act):
                if gate is not None:
                    act.wait_ge(gate_loaded, 16)
                    act.wait_ge(zeroed, 1)
                    act.activation(g2[:, :, 0:E], g32[:, :, :], ACT.Copy).then_inc(gate_hi, 1)
                act.wait_ge(var_ready, 1)
                inverse_root(act, None, None, root_done, ve[:, :], root[:, :], None, None, 0)
                for g in range(NG + 2):
                    if gate is not None and g >= 2:
                        act.wait_ge(multiplied, g - 1)
                        if g >= 4:
                            act.wait_ge(back, g - 3)
                        act.activation(lt[:, g % 2, :], pl[g % 2][0:2 * E, :], ACT.Copy).then_inc(copied, 1)
                    if g >= NG:
                        continue
                    act.wait_ge(turned, g + 1)
                    for k in range(KD):
                        ins = act.activation(xh[:, k, g % places * 512:(g % places + 1) * 512], pt[g % 2 * 2 + k][:, :], ACT.Copy)
                    ins.then_inc(hi_done, 1)

            @block.tensor
            def _(pe):
                def multiply(g):
                    pe.wait_ge(lo_done, g + 1)
                    pe.wait_ge(hi_done, g + 1)
                    if g == 0:
                        pe.wait_ge(gate_lo, 1)
                        pe.wait_ge(gate_hi, 1)
                    if g >= 2:
                        pe.wait_ge(copied, g - 1)
                    c = slice(g % places * GT * P, (g % places + 1) * GT * P)
                    n = 0
                    for half in (xh, xl):
                        for k in range(KD):
                            ins = pe.matmul(pl[g % 2][:, :], g2[:, k, :], half[:, k, c], start=n == 0, stop=n == 3)
                            n += 1
                    ins.then_inc(multiplied, 1)

                def turn_logits(g):
                    pe.wait_ge(copied, g + 1)
                    if g >= 2:
                        pe.wait_ge(summed, g - 1)
                    for j in range(GT):
                        ins = pe.transpose(pr[g % 2][:, j * 2 * E:(j + 1) * 2 * E], lt[:, g % 2, j * P:(j + 1) * P], ident[0:2 * E, 0:2 * E])
                    ins.then_inc(back, 1)

                for g in range(NG):
                    if gate is not None and g >= 2:
                        multiply(g - 2)
                        if g >= 3:
                            turn_logits(g - 3)
                    pe.wait_ge(rows_ready, g + 1)
                    if g >= 2:
                        pe.wait_ge(hi_done, g - 1)
                        pe.wait_ge(lo_done, g - 1)
                    for k in range(KD):
                        for j in range(GT):
                            ins = pe.transpose(pt[g % 2 * 2 + k][:, j * P:(j + 1) * P], xn[:, g % 2, j, k * P:(k + 1) * P], ident[:, :])
                    ins.then_inc(turned, 1)
                if gate is not None:
                    multiply(NG - 2)
                    turn_logits(NG - 3)
                    multiply(NG - 1)
                    turn_logits(NG - 2)
                    turn_logits(NG - 1)


class Threshold:
    PER = 5

    def __init__(self, nc, ctx, cst, key, E, cap, tag, probabilities=False):
        self.skipped = 2 if probabilities else 0
        self.steps = 32 - self.skipped
        sb = lambda n, s, d=F32: ctx.enter_context(nc.sbuf_tensor(tag + n, s, d))
        sem = lambda n: ctx.enter_context(nc.semaphore(tag + n))
        self.cst, self.key, self.E, self.cap = cst, key, E, cap
        self.thr = sb("threshold", [P, E], I32)
        self.cand = sb("candidate", [P, E], I32)
        self.change = sb("kept_bit", [P, E], I32)
        self.part = sb("count_part", [P, E])
        self.hit = sb("at_least", [P, E, TT])
        self.step = sem("search_step")
        self.totalled = sem("search_totalled")

    def spread(self, t):
        return t.rearrange("p (e t) -> p e t", t=1).broadcast_to([P, self.E, TT])

    def start(self, dve):
        dve.memset(self.thr[:, :], 0 if self.skipped else -1).then_inc(self.step, 1)

    def count(self, dve, i):
        dve.wait_ge(self.step, i * self.PER + 1)
        s = Steps(dve, self.step, i, self.PER, 1)
        s.then(dve.tensor_tensor(self.cand[:, :], self.thr[:, :], self.bit(i), ALU.bitwise_xor))
        s.then(dve.tensor_tensor(self.hit[:, :, :], self.key[:, :, :], self.spread(self.cand[:, :].bitcast(F32)), ALU.is_ge))
        s.done(dve.tensor_reduce(self.part[:, :], self.hit[:, :, :], AX.X, ALU.add))

    def total(self, pe, i, out):
        pe.wait_ge(self.step, i * self.PER + 4)
        pe.matmul(out, self.cst["ones"][:, :], self.part[:, :], start=True, stop=True).then_inc(self.totalled, 1)

    def keep(self, dve, i, total):
        dve.wait_ge(self.totalled, i + 1)
        s = Steps(dve, self.step, i, self.PER, 4)
        s.then(dve.scalar_tensor_tensor(out=self.change[:, :], in0=total, scalar=self.cap - 0.5, in1=self.bit(i),
                                        op0=ALU.is_ge, op1=ALU.mult))
        s.done(dve.tensor_tensor(self.thr[:, :], self.thr[:, :], self.change[:, :], ALU.bitwise_xor))

    def bit(self, i):
        return self.cst["bits"][:, bass.ds(i + self.skipped, 1)].broadcast_to([P, self.E])


def search(nc, th, tag, weights=None):
    with ExitStack() as ctx:
        tot = ctx.enter_context(nc.psum_tensor(tag + "search_total", [P, 512], F32))
        with nc.Block() as block:
            if weights is not None:
                @block.sync
                def _(sp):
                    weights.load(sp)

                @block.scalar
                def _(act):
                    weights.high(act)

                @block.gpsimd
                def _(pool):
                    weights.low(pool)

            @block.vector
            def _(dve):
                th.start(dve)
                with dve.Fori(0, th.steps) as i:
                    th.count(dve, i)
                    th.keep(dve, i, tot[:, 0:th.E])

            @block.tensor
            def _(pe):
                with pe.Fori(0, th.steps) as i:
                    th.total(pe, i, tot[:, 0:th.E])


def take(nc, cst, th, key, E, cap, chosen, rank, tag=""):
    W = E * TT
    with ExitStack() as ctx:
        sb = lambda n, s, d=F32: ctx.enter_context(nc.sbuf_tensor(tag + n, s, d))
        sem = lambda n: ctx.enter_context(nc.semaphore(tag + n))
        above = sb("count_above", [P, E])
        a = sb("prefix_sum", [P, E, TT])
        thr, part, hit = th.thr, th.part, th.hit
        tot = ctx.enter_context(nc.psum_tensor(tag + "total", [P, 512], F32))
        within = ctx.enter_context(nc.psum_tensor(tag + "within", [P, 512], F32))
        tiles = ctx.enter_context(nc.psum_tensor(tag + "tile_totals", [P, 512], F32))
        dve_step = sem("take_step")
        counted = sem("take_counted")
        totalled = sem("take_totalled")
        flat = lambda t: t.rearrange("p e t -> p (e t)")

        with nc.Block() as block:
            @block.vector
            def _(dve):
                step = Steps(dve, dve_step)
                thr_f = th.spread(thr[:, :].bitcast(F32))
                step.then(dve.tensor_tensor(chosen[:, :, :], key[:, :, :], thr_f, ALU.is_gt))
                step.then(dve.tensor_reduce(part[:, :], chosen[:, :, :], AX.X, ALU.add))
                step.then(dve.tensor_tensor(hit[:, :, :], key[:, :, :], thr_f, ALU.is_equal))
                step.then(dve.tensor_scalar(rank[:, :, :], key[:, :, :], NEG, None, ALU.is_gt))
                step.then(dve.tensor_tensor(hit[:, :, :], hit[:, :, :], rank[:, :, :], ALU.mult))
                dve.tensor_copy(rank[:, :, :], hit[:, :, :]).then_inc(counted, 1)

                def prefix(n):
                    dve.wait_ge(totalled, n)
                    step.then(dve.tensor_copy(a[:, :, :], tiles[:, 0:W].rearrange("p (e t) -> p e t", t=TT)))
                    step.then(dve.tensor_tensor_scan(flat(rank[:, :, :]), cst["keep"][:, 0:W], flat(a[:, :, :]), 0.0, ALU.mult, ALU.add))
                    step.then(dve.tensor_tensor(rank[:, :, :], rank[:, :, :], a[:, :, :], ALU.subtract))
                    step.then(dve.tensor_tensor(rank[:, :, :], rank[:, :, :], within[:, 0:W].rearrange("p (e t) -> p e t", t=TT), ALU.add))

                prefix(1)
                step.then(dve.tensor_scalar(above[:, :], tot[:, 0:E], -1.0, float(cap), ALU.mult, ALU.add))
                step.then(dve.tensor_tensor(rank[:, :, :], rank[:, :, :], th.spread(above[:, :]), ALU.is_lt))
                step.then(dve.tensor_tensor(rank[:, :, :], rank[:, :, :], hit[:, :, :], ALU.mult))
                dve.tensor_tensor(chosen[:, :, :], chosen[:, :, :], rank[:, :, :], ALU.add).then_inc(counted, 1)
                prefix(2)

            @block.tensor
            def _(pe):
                pe.wait_ge(counted, 1)
                pe.matmul(tot[:, 0:E], cst["ones"][:, :], part[:, :], start=True, stop=True)
                pe.matmul(within[:, 0:W], cst["before"][:, :], flat(rank[:, :, :]), start=True, stop=True)
                pe.matmul(tiles[:, 0:W], cst["ones"][:, :], flat(rank[:, :, :]), start=True, stop=True).then_inc(totalled, 1)
                pe.wait_ge(counted, 2)
                pe.matmul(within[:, 0:W], cst["before"][:, :], flat(chosen[:, :, :]), start=True, stop=True)
                pe.matmul(tiles[:, 0:W], cst["ones"][:, :], flat(chosen[:, :, :]), start=True, stop=True).then_inc(totalled, 1)


def constants(nc, ctx):
    sb = lambda n, s, d=F32: ctx.enter_context(nc.sbuf_tensor(n, s, d))
    cst = {"ones": sb("ones", [P, P]), "before": sb("before", [P, P]), "bits": sb("bits", [P, 32], I32),
           "keep": sb("keep", [P, 512]), "keep_e": sb("keep_e", [P, 512]), "token": sb("token", [P, TT], I32),
           "zero": sb("zero_ids", [P, 80], I32),
           "keep_8": sb("keep_8", [P, 256]), "tile_no": sb("tile_no", [P, 64])}
    made = ctx.enter_context(nc.semaphore("constants_made"))
    with nc.Block() as block:
        @block.gpsimd
        def _(pool):
            for name in ("ones", "before", "keep", "keep_e", "keep_8"):
                pool.memset(cst[name][:, :], 1.0).then_inc(made, 1)
            pool.wait_ge(made, 5)
            pool.affine_select(out=cst["before"][:, :], in_=cst["before"][:, :], compare_op=ALU.is_gt, fill=0.0, base=0,
                               pattern=[[1, P]], channel_multiplier=-1)
            pool.memset(cst["keep"][:, :].rearrange("p (e t) -> p e t", t=TT)[:, :, 0:1], 0.0)
            pool.memset(cst["keep_e"][:, :].rearrange("p (t e) -> p t e", e=E0)[:, :, 0:1], 0.0)
            for i in range(32):
                pool.memset(cst["bits"][:, i:i + 1], -1 if i == 0 else 1 << (31 - i))
            pool.memset(cst["keep_8"][:, :].rearrange("p (t e) -> p t e", e=8)[:, :, 0:1], 0.0)
            pool.iota(cst["tile_no"][:, :], pattern=[[1, 64]], base=0, channel_multiplier=0, allow_small_or_imprecise_dtypes=True)
            pool.memset(cst["zero"][:, :], 0)
            pool.iota(cst["token"][:, :], pattern=[[P, TT]], base=0, channel_multiplier=1).then_inc(made, 1)
            pool.wait_ge(made, 6)
    return cst


def slot_arrays(nc, ctx, J, tag=""):
    sb = lambda n, d: ctx.enter_context(nc.sbuf_tensor(tag + n, [P, J, TT], d))
    return {"scatter": sb("slot_or_beyond", I32), "slot": sb("slot_or_zero", I32), "weight": sb("slot_weight", F32)}


def route0(nc, io, cst, logits, first, second, key, ws):
    with ExitStack() as c2:
        sem = lambda n: c2.enter_context(nc.semaphore(n))
        sb2 = lambda n, s, d=F32: c2.enter_context(nc.sbuf_tensor(n, s, d))
        sc = sb2("scores", [P, TT, E0])
        eq = sb2("score_is_max", [P, TT, E0])
        pre = sb2("score_prefix", [P, TT, E0])
        m = sb2("score_max", [P, TT])
        gb = sb2("gate_b_sb", [P, E0])
        step_s, exped, loaded = sem("route_step"), sem("route_exp"), sem("gate_b_loaded")
        over_e = lambda t: t.rearrange("p (t e) -> p t e", e=1).broadcast_to([P, TT, E0])
        flat = lambda t: t.rearrange("p t e -> p (t e)")
        with nc.Block() as block:
            @block.sync
            def _(sp):
                sp.dma_start(gb[:, :], io["L0_ffn_gate_b"].rearrange("(o e) -> o e", o=1).broadcast_to([P, E0])).then_inc(loaded, 16)
                ws.load(sp)

            @block.vector
            def _(dve):
                step = Steps(dve, step_s)
                step.then(dve.tensor_reduce(m[:, :], logits[:, :, :], AX.X, ALU.max))
                step.then(dve.tensor_tensor(sc[:, :, :], logits[:, :, :], over_e(m[:, :]), ALU.subtract))
                dve.wait_ge(exped, 1)
                step.then(dve.tensor_reduce(m[:, :], sc[:, :, :], AX.X, ALU.add))
                step.then(dve.reciprocal(m[:, :], m[:, :]))
                step.then(dve.tensor_tensor(sc[:, :, :], sc[:, :, :], over_e(m[:, :]), ALU.mult))
                dve.wait_ge(loaded, 16)
                step.then(dve.tensor_tensor(sc[:, :, :], sc[:, :, :],
                                            gb[:, :].rearrange("p (t e) -> p t e", t=1).broadcast_to([P, TT, E0]), ALU.add))
                for pick in (first, second):
                    step.then(dve.tensor_reduce(m[:, :], sc[:, :, :], AX.X, ALU.max))
                    step.then(dve.tensor_tensor(eq[:, :, :], sc[:, :, :], over_e(m[:, :]), ALU.is_equal))
                    step.then(dve.tensor_tensor_scan(flat(pre[:, :, :]), cst["keep_e"][:, :], flat(eq[:, :, :]), 0.0, ALU.mult, ALU.add))
                    step.then(dve.tensor_scalar(pre[:, :, :], pre[:, :, :], 1.0, None, ALU.is_equal))
                    step.then(dve.tensor_tensor(pick[:, :, :], pre[:, :, :], eq[:, :, :], ALU.mult))
                    if pick is first:
                        step.then(dve.tensor_scalar(eq[:, :, :], first[:, :, :], NEG, None, ALU.mult))
                        step.then(dve.tensor_tensor(sc[:, :, :], sc[:, :, :], eq[:, :, :], ALU.add))
                step.then(dve.tensor_tensor(eq[:, :, :], first[:, :, :], second[:, :, :], ALU.add))
                step.then(dve.tensor_tensor(sc[:, :, :], eq[:, :, :], logits[:, :, :], ALU.mult))
                step.then(dve.tensor_scalar(eq[:, :, :], eq[:, :, :], 1.0, -NEG, ALU.subtract, ALU.mult))
                step.then(dve.tensor_tensor(key[:, :, :].rearrange("p e t -> p t e"), sc[:, :, :], eq[:, :, :], ALU.add))

            @block.scalar
            def _(act):
                act.wait_ge(step_s, 2)
                act.activation(sc[:, :, :], sc[:, :, :], ACT.Exp).then_inc(exped, 1)
                ws.high(act)

            @block.gpsimd
            def _(pool):
                ws.low(pool)


def slots0(nc, logits, first, second, chosen, rank, r):
    with ExitStack() as c2:
        sb2 = lambda n, s, d=F32: c2.enter_context(nc.sbuf_tensor(n, s, d))
        t1 = sb2("pick_chosen", [P, TT, E0])
        t2 = sb2("pick_value", [P, TT, E0])
        kept = sb2("kept", [P, 2, TT])
        slot = sb2("slot_f32", [P, 2, TT])
        step_s = c2.enter_context(nc.semaphore("slots_step"))
        te = lambda t: t[:, :, :].rearrange("p e t -> p t e")
        with nc.Block() as block:
            @block.vector
            def _(dve):
                step = Steps(dve, step_s)
                for e in range(E0):
                    ins = dve.tensor_scalar(rank[:, e, :], rank[:, e, :], float(e * CAP0), None, ALU.add)
                    step.done(ins)
                step.wait()
                for j, pick in enumerate((first, second)):
                    step.then(dve.tensor_tensor(t1[:, :, :], pick[:, :, :], te(chosen), ALU.mult))
                    step.then(dve.tensor_reduce(kept[:, j, :], t1[:, :, :], AX.X, ALU.add))
                    step.then(dve.tensor_tensor(t2[:, :, :], t1[:, :, :], logits[:, :, :], ALU.mult))
                    step.then(dve.tensor_reduce(r["weight"][:, j, :], t2[:, :, :], AX.X, ALU.add))
                    step.then(dve.tensor_tensor(t2[:, :, :], t1[:, :, :], te(rank), ALU.mult))
                    step.then(dve.tensor_reduce(slot[:, j, :], t2[:, :, :], AX.X, ALU.add))
                step.then(dve.tensor_copy(r["slot"][:, :, :], slot[:, :, :]))
                step.then(dve.tensor_scalar(kept[:, :, :], kept[:, :, :], -1.0, -2.0 * SLOTS0, ALU.add, ALU.mult))
                step.then(dve.tensor_tensor(kept[:, :, :], kept[:, :, :], slot[:, :, :], ALU.add))
                step.then(dve.tensor_copy(r["scatter"][:, :, :], kept[:, :, :]))


def matmul3(pe, out, w_hi, w_lo, x_hi, x_lo, first, last):
    pe.matmul(out, w_hi, x_hi, start=first, stop=False)
    pe.matmul(out, w_hi, x_lo, start=False, stop=False)
    return pe.matmul(out, w_lo, x_hi, start=False, stop=last)


def expert_weights(io, names, e):
    return [io[n][e].rearrange("(c p) h -> p c h", p=P) for n in names]


class SharedWeights:

    def __init__(self, nc, ctx, io):
        sb = lambda n, s, d=F32: ctx.enter_context(nc.sbuf_tensor(n, s, d))
        sem = lambda n: ctx.enter_context(nc.semaphore(n))
        self.io = io
        self.hi = sb("sh_w_hi", [P, 2, 3, 1024], F32R)
        self.lo = sb("sh_w_lo", [P, 2, 3, 1024], F32R)
        self.stage = sb("sh_stage", [P, 2, 1024])
        self.loaded = [sem(f"sh_loaded{i}") for i in range(2)]
        self.hi_done, self.lo_done = sem("sh_w_hi_done"), sem("sh_w_lo_done")

    def load(self, sp):
        for n in range(6):
            src = expert_weights(self.io, ("L0_ffn_sw1", "L0_ffn_sw3", "L0_ffn_sw2"), n // 3)[n % 3]
            if n >= 2:
                sp.wait_ge(self.lo_done, n - 1)
            sp.dma_start(self.stage[:, n % 2, :].rearrange("p (c h) -> p c h", h=src.shape[2]), src).then_inc(self.loaded[n % 2], 16)

    def high(self, act):
        for n in range(6):
            act.wait_ge(self.loaded[n % 2], 16 * (n // 2 + 1))
            act.activation(self.hi[:, n // 3, n % 3, :], self.stage[:, n % 2, :], ACT.Copy).then_inc(self.hi_done, 1)

    def low(self, pool):
        for n in range(6):
            pool.wait_ge(self.hi_done, n + 1)
            pool.tensor_tensor(self.lo[:, n // 3, n % 3, :], self.stage[:, n % 2, :], self.hi[:, n // 3, n % 3, :].bitcast(F32),
                               ALU.subtract).then_inc(self.lo_done, 1)


def shared_expert(nc, io, cst, x_sb, xh, xl, ws, e, th, table, ids, scatter, sw):
    NB = TOK // 512
    NE = 2
    with ExitStack() as ctx:
        sb = lambda n, s, d=F32: ctx.enter_context(nc.sbuf_tensor(f"sh{e}_{n}", s, d))
        sem = lambda n: ctx.enter_context(nc.semaphore(f"sh{e}_{n}"))
        sg = sb("gated", [P, HC, 512])
        gh = sb("g_hi", [P, HC, 512], F32R)
        gl = sb("g_lo", [P, HC, 512], F32R)
        hb = [ctx.enter_context(nc.psum_tensor(f"sh{e}_h{i}", [P, 2, 512], F32)) for i in range(2)]
        yb = [ctx.enter_context(nc.psum_tensor(f"sh{e}_y{i}", [P, 512], F32)) for i in range(4)]
        h_made = sem("h_made")
        silu = sem("silu")
        gated = sem("gated_done")
        g_hi, g_lo = sem("g_hi_done"), sem("g_lo_done")
        y_made = sem("y_made")
        y_added = sem("y_added")
        zeroed, scattered, read = sw[0:3]
        searching = e == 0

        def total(m):
            return hb[m % 2][:, 0, 0:E0]

        with nc.Block() as block:
            if e == 1:
                @block.gpsimd
                def _(pool):
                    pool.dma_start(table.rearrange("(p c) o -> p (c o)", p=P), cst["zero"][:, 0:SLOTS0 // P]).then_inc(zeroed, 16)
                    pool.wait_ge(zeroed, 16)
                    for t in range(TT):
                        for j in range(2):
                            pool.indirect_dma_start(out=table, out_offset=bass.IndirectOffsetOnAxis(ap=scatter[:, j, t:t + 1].bitcast(U32), axis=0),
                                                    in_=cst["token"][:, t:t + 1], in_offset=None, bounds_check=SLOTS0 - 1,
                                                    oob_is_err=False).then_inc(scattered, 16)
                    pool.wait_ge(scattered, 16 * 2 * TT)
                    pool.dma_start(ids[:, :, :], table.rearrange("(e p j) o -> p e (j o)", p=P, j=NT0)).then_inc(read, 16)
                    pool.wait_ge(read, 16)

            @block.scalar
            def _(act):
                def g_high(u, m):
                    act.wait_ge(gated, u + 1)
                    act.activation(gh[:, m, :], sg[:, m, :], ACT.Copy).then_inc(g_hi, 1)

                def block_(q):
                    for m in range(HC):
                        u = q * HC + m
                        act.wait_ge(h_made, u + 1)
                        if due(u - 3):
                            act.wait_ge(g_lo, u - 3)
                        act.activation(sg[:, m, :], hb[m % 2][:, 0, :], ACT.Silu).then_inc(silu, 1)
                        if due(u):
                            g_high(u - 1, (m - 1) % HC)

                block_(0)
                with act.Fori(1, NB) as q:
                    block_(q)
                g_high(NB * HC - 1, HC - 1)

            @block.vector
            def _(dve):
                def g_low(u, m):
                    dve.wait_ge(g_hi, u + 1)
                    dve.tensor_tensor(gl[:, m, :], sg[:, m, :], gh[:, m, :].bitcast(F32), ALU.subtract).then_inc(g_lo, 1)

                def add(q):
                    dve.wait_ge(y_made, q + 1)
                    for j in range(4):
                        dst = x_sb[:, bass.ds(q * 4 + j, 1), :].rearrange("p a d -> p (a d)")
                        ins = dve.scalar_tensor_tensor(out=dst, in0=yb[j][:, 0:D], scalar=1.0 / NE, in1=dst, op0=ALU.mult, op1=ALU.add)
                    ins.then_inc(y_added, 1)

                def block_(q, last=False):
                    for m in range(HC):
                        u = q * HC + m
                        if m == 2 and due(q):
                            add(q - 1)
                        dve.wait_ge(silu, u + 1)
                        dve.tensor_tensor(sg[:, m, :], sg[:, m, :], hb[m % 2][:, 1, :], ALU.mult).then_inc(gated, 1)
                        if due(u):
                            g_low(u - 1, (m - 1) % HC)
                        if searching:
                            th.keep(dve, u, total(m))
                            if not (last and m == HC - 1):
                                th.count(dve, u + 1)

                if searching:
                    th.start(dve)
                    th.count(dve, 0)
                block_(0)
                with dve.Fori(1, NB - 1) as q:
                    block_(q)
                block_(NB - 1, last=True)
                g_low(NB * HC - 1, HC - 1)
                add(NB - 1)

            @block.tensor
            def _(pe):
                def hidden(u, q, m):
                    if due(u - 1):
                        pe.wait_ge(gated, u - 1)
                        if searching:
                            pe.wait_ge(th.step, (u - 1) * th.PER)
                    x = bass.ds(q * 512, 512)
                    for w in range(2):
                        for k in range(KD):
                            c = slice(k * H0 + m * P, k * H0 + (m + 1) * P)
                            ins = matmul3(pe, hb[m % 2][:, w, :], ws.hi[:, e, w, c], ws.lo[:, e, w, c], xh[:, k, x], xl[:, k, x],
                                          k == 0, k == KD - 1)
                    ins.then_inc(h_made, 1)

                def back(u, q, m):
                    pe.wait_ge(g_hi, u + 1)
                    pe.wait_ge(g_lo, u + 1)
                    if m == 0 and due(q):
                        pe.wait_ge(y_added, q)
                    w = slice(m * D, (m + 1) * D)
                    for j in range(4):
                        c = slice(j * P, (j + 1) * P)
                        pe.matmul(yb[j][:, 0:D], gh[:, m, c], ws.hi[:, e, 2, w], start=m == 0, stop=False)
                        pe.matmul(yb[j][:, 0:D], gh[:, m, c], ws.lo[:, e, 2, w], start=False, stop=False)
                        ins = pe.matmul(yb[j][:, 0:D], gl[:, m, c], ws.hi[:, e, 2, w], start=False, stop=m == HC - 1)
                    if m == HC - 1:
                        ins.then_inc(y_made, 1)

                def block_(q, last=False):
                    for m in range(HC):
                        u = q * HC + m
                        if m < HC - 1:
                            hidden(u + 1, q, m + 1)
                        elif not last:
                            hidden(u + 1, q + 1, 0)
                        if searching:
                            pe.wait_ge(gated, u + 1)
                            th.total(pe, u, total(m))
                        if m:
                            back(u - 1, q, m - 1)
                        elif due(q):
                            back(u - 1, q - 1, HC - 1)

                hidden(0, 0, 0)
                block_(0)
                with pe.Fori(1, NB - 1) as q:
                    block_(q)
                block_(NB - 1, last=True)
                back(NB * HC - 1, NB - 1, HC - 1)


def routed_experts(nc, io, ident, xn_rows, ids, y_rows, sw):
    BL = [(0, 2), (2, 3)]
    U = 2 * HC
    TG = [(0, 2), (2, 2), (4, 1)]
    names = ("L0_ffn_ew1", "L0_ffn_ew3", "L0_ffn_ew2")
    with ExitStack() as ctx:
        sb = lambda n, s, d=F32: ctx.enter_context(nc.sbuf_tensor(n, s, d))
        sem = lambda n: ctx.enter_context(nc.semaphore(n))
        stage = sb("ex_stage", [P, 3, 1024])
        wh = sb("ex_w_hi", [P, 2, 3, 1024], F32R)
        wl = sb("ex_w_lo", [P, 2, 3, 1024], F32R)
        xr = sb("ex_rows", [P, 2, NT0, D])
        xh = sb("ex_x_hi", [P, 2, KD, CAP0], F32R)
        xl = sb("ex_x_lo", [P, 2, KD, CAP0], F32R)
        sg = sb("ex_gated", [P, HC, 384])
        gh = sb("ex_g_hi", [P, HC, 384], F32R)
        gl = sb("ex_g_lo", [P, HC, 384], F32R)
        ys = sb("ex_y", [P, 2, NT0, D])
        hb = [ctx.enter_context(nc.psum_tensor(f"ex_h{i}", [P, 2, 512], F32)) for i in range(2)]
        yb = [ctx.enter_context(nc.psum_tensor(f"ex_yb{i}", [P, 512], F32)) for i in range(3)]
        tb = ctx.enter_context(nc.psum_tensor("ex_tb", [P, 512], F32))
        loaded = [sem(f"ex_loaded{j}") for j in range(3)]
        w_hi, w_lo = sem("ex_w_hi_done"), sem("ex_w_lo_done")
        gathered = sw[3:5]
        turned = sem("ex_turned")
        x_hi, x_lo = sem("ex_x_hi_done"), sem("ex_x_lo_done")
        h_made, silu, gated = sem("ex_h_made"), sem("ex_silu"), sem("ex_gated_done")
        g_hi, g_lo = sem("ex_g_hi_done"), sem("ex_g_lo_done")
        y_made, y_copied = sem("ex_y_made"), sem("ex_y_copied")
        stored = sw[5:7]

        def width(v):
            return BL[v // HC][1] * P

        with nc.Block() as block:
            @block.sync
            def _(sp):
                def load(e, first):
                    for j, src in enumerate(expert_weights(io, names, 0)):
                        if not first:
                            sp.wait_ge(w_lo, (e - 1) * 3 + (j + 1))
                        full = io[names[j]].rearrange("e (c p) h -> p e c h", p=P)
                        s = full[:, 0] if first else full[:, bass.ds(e, 1)].rearrange("p a c h -> p (a c) h")
                        sp.dma_start(stage[:, j, :].rearrange("p (c h) -> p c h", h=src.shape[2]), s).then_inc(loaded[j], 16)

                load(0, True)
                with sp.Fori(1, E0) as e:
                    load(e, False)

            @block.gpsimd
            def _(pool):
                def gather(e):
                    for j in range(NT0):
                        pool.indirect_dma_start(out=xr[:, e % 2, j, :], out_offset=None, in_=xn_rows,
                                                in_offset=bass.IndirectOffsetOnAxis(ap=ids[:, e, j:j + 1].bitcast(U32), axis=0)
                                                ).then_inc(gathered[e % 2], 16)

                y_t = y_rows.rearrange("(e p j) d -> e p j d", p=P, j=NT0)
                gather(0)
                gather(1)
                pool.wait_ge(turned, 3)
                gather(2)
                for e in range(E0):
                    if e + 3 < E0:
                        pool.wait_ge(turned, 3 * (e + 2))
                        gather(e + 3)
                    pool.wait_ge(y_copied, 2 * (e + 1))
                    pool.dma_start(y_t[e], ys[:, e % 2]).then_inc(stored[e % 2], 16)
                for j in range(2):
                    pool.wait_ge(stored[j], 16 * (E0 // 2))

            def tile_view(t, par, g):
                a, n = TG[g]
                return t[:, par, :, a * P:(a + n) * P]

            def turned_view(g):
                n = TG[g][1] * P
                return tb[:, 0:KD * n].rearrange("p (k c) -> p k c", k=KD)

            @block.scalar
            def _(act):
                def w_high(e, par, j):
                    act.wait_ge(loaded[j], e * 16 + 16)
                    act.activation(wh[:, par, j, :], stage[:, j, :], ACT.Copy).then_inc(w_hi, 1)

                def x_high(e, par, g):
                    act.wait_ge(turned, e * 3 + (g + 1))
                    act.activation(tile_view(xh, par, g), turned_view(g), ACT.Copy).then_inc(x_hi, 1)

                def g_high(u, v):
                    act.wait_ge(gated, u + 1)
                    act.activation(gh[:, v % HC, 0:width(v)], sg[:, v % HC, 0:width(v)], ACT.Copy).then_inc(g_hi, 1)

                def copy_y(e, par, b):
                    act.wait_ge(y_made, e * 2 + (b + 1))
                    if b == 0:
                        act.wait_ge(stored[par], (e // 2) * 16)
                    for j in range(BL[b][1]):
                        ins = act.activation(ys[:, par, BL[b][0] + j, :], yb[j][:, 0:D], ACT.Copy)
                    ins.then_inc(y_copied, 1)

                def expert(e, par, first, last):
                    for v in range(U):
                        u = e * U + v
                        if v == 2 and not first:
                            copy_y(e - 1, 1 - par, 1)
                        if v == HC + 2:
                            copy_y(e, par, 0)
                        act.wait_ge(h_made, u + 1)
                        if not (first and v < HC):
                            act.wait_ge(g_lo, u - 3)
                        act.activation(sg[:, v % HC, 0:width(v)], hb[v % 2][:, 0, 0:width(v)], ACT.Silu).then_inc(silu, 1)
                        if v or not first:
                            g_high(u - 1, (v - 1) % U)
                        if not last and v in (2, 4, 6):
                            w_high(e + 1, 1 - par, v // 2 - 1)
                        if not last and v in (1, 3, 5):
                            x_high(e + 1, 1 - par, v // 2)

                for g in range(3):
                    w_high(0, 0, g)
                for g in range(3):
                    x_high(0, 0, g)
                expert(0, 0, True, False)
                expert(1, 1, False, False)
                with act.Fori(1, E0 // 2 - 1) as i:
                    for par in range(2):
                        expert(i * 2 + par, par, False, False)
                expert(E0 - 2, 0, False, False)
                expert(E0 - 1, 1, False, True)
                g_high(E0 * U - 1, U - 1)
                copy_y(E0 - 1, 1, 1)

            @block.vector
            def _(dve):
                def w_low(e, par, j):
                    dve.wait_ge(w_hi, e * 3 + (j + 1))
                    dve.tensor_tensor(wl[:, par, j, :], stage[:, j, :], wh[:, par, j, :].bitcast(F32), ALU.subtract).then_inc(w_lo, 1)

                def x_low(e, par, g):
                    dve.wait_ge(x_hi, e * 3 + (g + 1))
                    dve.tensor_tensor(tile_view(xl, par, g), turned_view(g), tile_view(xh, par, g).bitcast(F32),
                                      ALU.subtract).then_inc(x_lo, 1)

                def g_low(u, v):
                    dve.wait_ge(g_hi, u + 1)
                    w = slice(0, width(v))
                    dve.tensor_tensor(gl[:, v % HC, w], sg[:, v % HC, w], gh[:, v % HC, w].bitcast(F32), ALU.subtract).then_inc(g_lo, 1)

                def expert(e, par, first, last):
                    for v in range(U):
                        u = e * U + v
                        w = slice(0, width(v))
                        dve.wait_ge(silu, u + 1)
                        dve.tensor_tensor(sg[:, v % HC, w], sg[:, v % HC, w], hb[v % 2][:, 1, w], ALU.mult).then_inc(gated, 1)
                        if v or not first:
                            g_low(u - 1, (v - 1) % U)
                        if not last and v in (2, 4, 6):
                            w_low(e + 1, 1 - par, v // 2 - 1)
                        if not last and v in (1, 3, 5):
                            x_low(e + 1, 1 - par, v // 2)

                for g in range(3):
                    w_low(0, 0, g)
                for g in range(3):
                    x_low(0, 0, g)
                expert(0, 0, True, False)
                expert(1, 1, False, False)
                with dve.Fori(1, E0 // 2 - 1) as i:
                    for par in range(2):
                        expert(i * 2 + par, par, False, False)
                expert(E0 - 2, 0, False, False)
                expert(E0 - 1, 1, False, True)
                g_low(E0 * U - 1, U - 1)

            @block.tensor
            def _(pe):
                def turn(e, par, g, first=False):
                    if g == 0:
                        pe.wait_ge(gathered[par], (e // 2) * (16 * NT0) + 16 * NT0)
                    if not (first and g == 0):
                        pe.wait_ge(x_lo, e * 3 + g)
                        pe.wait_ge(x_hi, e * 3 + g)
                    a, n = TG[g]
                    for k in range(KD):
                        for j in range(n):
                            ins = pe.transpose(tb[:, (k * n + j) * P:(k * n + j + 1) * P], xr[:, par, a + j, k * P:(k + 1) * P], ident[:, :])
                    ins.then_inc(turned, 1)

                def hidden(e, par, v, wait=True):
                    u = e * U + v
                    if v == 0:
                        for s in (w_hi, w_lo, x_hi, x_lo):
                            pe.wait_ge(s, e * 3 + 3)
                    if wait:
                        pe.wait_ge(gated, u - 1)
                    a, n = BL[v // HC]
                    x = slice(a * P, (a + n) * P)
                    m = v % HC
                    for w in range(2):
                        for k in range(KD):
                            c = slice(k * H0 + m * P, k * H0 + (m + 1) * P)
                            ins = matmul3(pe, hb[v % 2][:, w, 0:n * P], wh[:, par, w, c], wl[:, par, w, c],
                                          xh[:, par, k, x], xl[:, par, k, x], k == 0, k == KD - 1)
                    ins.then_inc(h_made, 1)

                def back(e, par, v):
                    u = e * U + v
                    pe.wait_ge(g_hi, u + 1)
                    pe.wait_ge(g_lo, u + 1)
                    m = v % HC
                    if m == 0:
                        pe.wait_ge(y_copied, e * 2 + v // HC)
                    w = slice(m * D, (m + 1) * D)
                    for j in range(BL[v // HC][1]):
                        c = slice(j * P, (j + 1) * P)
                        pe.matmul(yb[j][:, 0:D], gh[:, m, c], wh[:, par, 2, w], start=m == 0, stop=False)
                        pe.matmul(yb[j][:, 0:D], gh[:, m, c], wl[:, par, 2, w], start=False, stop=False)
                        ins = pe.matmul(yb[j][:, 0:D], gl[:, m, c], wh[:, par, 2, w], start=False, stop=m == HC - 1)
                    if m == HC - 1:
                        ins.then_inc(y_made, 1)

                def expert(e, par, first, last):
                    for v in range(U):
                        if v < U - 1:
                            hidden(e, par, v + 1, wait=not (first and v == 0))
                        elif not last:
                            hidden(e + 1, 1 - par, 0)
                        if not last and v in (0, 2, 4):
                            turn(e + 1, 1 - par, v // 2)
                        if v:
                            back(e, par, v - 1)
                        elif not first:
                            back(e - 1, 1 - par, U - 1)

                for g in range(3):
                    turn(0, 0, g, True)
                hidden(0, 0, 0, wait=False)
                expert(0, 0, True, False)
                expert(1, 1, False, False)
                with pe.Fori(1, E0 // 2 - 1) as i:
                    for par in range(2):
                        expert(i * 2 + par, par, False, False)
                expert(E0 - 2, 0, False, False)
                expert(E0 - 1, 1, False, True)
                back(E0 - 1, 1, U - 1)


def combine(nc, x_sb, y_rows, slot, weight, J, tag, sw, aside=None, stats=None, out=None):
    R = 8
    with ExitStack() as ctx:
        g = ctx.enter_context(nc.sbuf_tensor(f"{tag}_rows", [P, R, D], F32))
        arrived = sw[7:7 + R]
        added = ctx.enter_context(nc.semaphore(f"{tag}_added"))
        stored = ctx.enter_context(nc.semaphore(f"{tag}_stored"))
        with nc.Block() as block:
            @block.gpsimd
            def _(pool):
                for n in range(TT * J):
                    if n >= R:
                        pool.wait_ge(added, n - R + 1)
                    pool.indirect_dma_start(out=g[:, n % R, :], out_offset=None, in_=y_rows,
                                            in_offset=bass.IndirectOffsetOnAxis(ap=slot[:, n % J, n // J:n // J + 1].bitcast(U32), axis=0)
                                            ).then_inc(arrived[n % R], 16)

            if out is not None:
                @block.sync
                def _(sp):
                    o = out.rearrange("b (t p) d -> b p t d", p=P)
                    for b in range(B):
                        sp.wait_ge(added, (b + 1) * TB * J)
                        sp.dma_start(o[b], x_sb[:, b * TB:(b + 1) * TB, :]).then_inc(stored, 16)
                    sp.wait_ge(stored, 16 * B)

            if aside is not None:
                @block.sync
                def _(sp):
                    aside.sync(sp)

                @block.scalar
                def _(act):
                    aside.scalar(act)

                @block.tensor
                def _(pe):
                    aside.tensor(pe)

            @block.vector
            def _(dve):
                if aside is not None:
                    aside.vector_first(dve)
                for n in range(TT * J):
                    t, j = n // J, n % J
                    if aside is not None and n == 2 * R:
                        aside.vector_rest(dve)
                    dve.wait_ge(arrived[n % R], 16 * (n // R + 1))
                    if j:
                        dve.wait_ge(added, n)
                    dve.scalar_tensor_tensor(out=x_sb[:, t, :], in0=g[:, n % R, :], scalar=weight[:, j, t:t + 1],
                                             in1=x_sb[:, t, :], op0=ALU.mult, op1=ALU.add).then_inc(added, 1)
                    if stats is not None and t and j == 0:
                        dve.wait_ge(added, n)
                        dve.bn_stats(stats[:, t - 1, :], x_sb[:, t - 1, :])
                if stats is not None:
                    dve.wait_ge(added, TT * J)
                    dve.bn_stats(stats[:, TT - 1, :], x_sb[:, TT - 1, :])


HD1, GRP = 16, 4
BIG = 1.0e30


class ContextKeys:

    def __init__(self, nc, ctx, io, ident, ks, vm, vt):
        self.io, self.ident, self.ks, self.vm, self.vt = io, ident, ks, vm, vt
        sb = lambda n, s, d=F32: ctx.enter_context(nc.sbuf_tensor(n, s, d))
        sem = lambda n: ctx.enter_context(nc.semaphore(n))
        self.c0 = sb("c1_rows0", [P, B, D])
        self.c1 = sb("c1_rows1", [S1, B, D])
        self.cT = sb("c1_T", [P, KD, B * S])
        self.w = sb("kv_w_sb", [P, KD, 2 * D])
        self.kb = sb("k_bias", [P, KD])
        self.vb = sb("v_bias", [P, D])
        self.kf = sb("k_full", [P, KD, B * S])
        self.kh = sb("k_hi", [P, KD, B * S], F32R)
        self.kl = sb("k_lo", [P, KD, B * S], F32R)
        self.m8 = sb("mask_u8", [97, B * S], mybir.dt.uint8)
        self.pt = [ctx.enter_context(nc.psum_tensor(f"c1_p{i}", [P, 512], F32)) for i in range(8)]
        self.loaded = sem("c1_loaded")
        self.turned, self.copied = sem("c1_turned"), sem("c1_copied")
        self.k_made, self.k_done, self.kh_done, self.kl_done = sem("c1_k_made"), sem("c1_k_done"), sem("c1_kh_done"), sem("c1_kl_done")
        self.v_made, self.v_done, self.placed, self.zeroed = sem("c1_v_made"), sem("c1_v_done"), sem("c1_placed"), sem("c1_zeroed")

    def sync(self, sp):
        sp.dma_start(self.c0[:, :, :], self.io["ctx_1024"][:, 0:P, :].rearrange("b p d -> p b d")).then_inc(self.loaded, 16)
        sp.dma_start(self.c1[:, :, :], self.io["ctx_1024"][:, P:S, :].rearrange("b p d -> p b d")).then_inc(self.loaded, 16)
        sp.dma_start(self.w[:, :, :], self.io["L1_xattn_kv_w"].rearrange("(k p) n -> p k n", p=P)).then_inc(self.loaded, 16)
        sp.dma_start(self.kb[:, :], self.io["L1_xattn_kv_b"][0:D].rearrange("(k p) -> p k", p=P), allow_slow_non_contiguous=True).then_inc(self.loaded, 16)
        sp.dma_start(self.vb[:, :], self.io["L1_xattn_kv_b"][D:2 * D].rearrange("(o e) -> o e", o=1).broadcast_to([P, D])).then_inc(self.loaded, 16)
        sp.dma_start(self.m8[96:97, :], self.io["mask_BxS2_bk0"].rearrange("(o b) s -> o (b s)", o=1)).then_inc(self.loaded, 16)
        sp.wait_ge(self.kl_done, KD)
        sp.wait_ge(self.kh_done, KD)
        sp.wait_ge(self.zeroed, 3)
        for c in range(KD):
            for q in range(4):
                for h in range(2):
                    src = slice(q * 32 + h * HD1, q * 32 + (h + 1) * HD1)
                    for j, half in enumerate((self.kh, self.kh, self.kl)):
                        dst = slice(j * 32 + h * HD1, j * 32 + (h + 1) * HD1)
                        sp.dma_start(self.ks[dst, :, c * 4 + q, h, :].bitcast(F32), half[src, c, :].bitcast(F32).rearrange("p (b s) -> p b s", b=B)).then_inc(self.placed, 16)
        sp.wait_ge(self.placed, 16 * KD * 4 * 2 * 3)

    def scalar(self, act):
        for b in range(B):
            act.wait_ge(self.turned, b + 1)
            for k in range(KD):
                ins = act.activation(self.cT[:, k, b * S:(b + 1) * S], self.pt[(b % 2) * 2 + k][:, 0:S], ACT.Copy)
            ins.then_inc(self.copied, 1)
        for c in range(KD):
            act.wait_ge(self.k_made, c + 1)
            act.wait_ge(self.loaded, 96)
            for j in range(2):
                n = slice(j * 2 * S, (j + 1) * 2 * S)
                ins = act.activation(self.kf[:, c, n], self.pt[4 + c * 2 + j][:, 0:2 * S], ACT.Identity, bias=self.kb[:, c:c + 1])
            ins.then_inc(self.k_done, 1)
            act.wait_ge(self.k_done, c + 1)
            act.activation(self.kh[:, c, :], self.kf[:, c, :], ACT.Copy).then_inc(self.kh_done, 1)

    def vector_first(self, dve):
        dve.memset(self.ks[:, :, :, :, :].bitcast(F32), 0.0).then_inc(self.zeroed, 1)
        dve.memset(self.vt[:, :, :, :], 0.0).then_inc(self.zeroed, 1)
        dve.memset(self.vm[:, :, :, :], 0.0).then_inc(self.zeroed, 1)
        dve.wait_ge(self.zeroed, 3)
        dve.wait_ge(self.loaded, 96)
        for b in range(B):
            dve.tensor_scalar(self.ks[96:97, b, :, :, :].rearrange("p q h s -> p (q h) s"),
                              self.m8[96:97, b * S:(b + 1) * S].rearrange("p (o s) -> p o s", o=1).broadcast_to([1, 16, S]),
                              -BIG, None, ALU.mult)

    def vector_rest(self, dve):
        for c in range(KD):
            dve.wait_ge(self.kh_done, c + 1)
            dve.tensor_tensor(self.kl[:, c, :], self.kf[:, c, :], self.kh[:, c, :].bitcast(F32), ALU.subtract).then_inc(self.kl_done, 1)
        for b in range(B):
            dve.wait_ge(self.v_made, b + 1)
            split = dict(c=2, u=2, h=4)
            for u in range(2):
                ins = dve.tensor_tensor(self.vm[:, b].rearrange("p (c u h) d -> p u c h d", **split)[:, u, :, :, u * HD1:(u + 1) * HD1],
                                        self.pt[b % 2][:, 0:D].rearrange("p (c u h d) -> p u c h d", **split)[:, u],
                                        self.vb[:, :].rearrange("p (c u h d) -> p u c h d", **split)[:, u], ALU.add)
            for hh in range(4):
                r = slice(32 * hh, 32 * hh + S1)
                for u in range(2):
                    ins = dve.tensor_tensor(self.vt[r, b].rearrange("p (c u) w -> p u c w", u=2)[:, u, :, 32 * hh + u * HD1:32 * hh + (u + 1) * HD1],
                                            self.pt[2 + b % 2][r, 0:D].rearrange("p (c u h d) -> p u h c d", **split)[:, u, hh],
                                            self.vb[r, :].rearrange("p (c u h d) -> p u h c d", **split)[:, u, hh], ALU.add)
            ins.then_inc(self.v_done, 1)

    def tensor(self, pe):
        pe.wait_ge(self.loaded, 96)
        for b in range(B):
            if b >= 2:
                pe.wait_ge(self.copied, b - 1)
            for k in range(KD):
                cols = slice(k * P, (k + 1) * P)
                pe.transpose(self.pt[(b % 2) * 2 + k][:, 0:P], self.c0[:, b, cols], self.ident[:, :])
                ins = pe.transpose(self.pt[(b % 2) * 2 + k][:, P:S], self.c1[:, b, cols], self.ident[0:S1, 0:S1])
            ins.then_inc(self.turned, 1)
        pe.wait_ge(self.copied, B)
        for c in range(KD):
            for j in range(2):
                for k in range(KD):
                    ins = pe.matmul(self.pt[4 + c * 2 + j][:, 0:2 * S], self.w[:, k, c * P:(c + 1) * P], self.cT[:, k, j * 2 * S:(j + 1) * 2 * S],
                                    start=k == 0, stop=k == KD - 1)
            ins.then_inc(self.k_made, 1)
        for b in range(B):
            if b >= 2:
                pe.wait_ge(self.v_done, b - 1)
            for k in range(KD):
                pe.matmul(self.pt[b % 2][:, 0:D], self.cT[:, k, b * S:b * S + P], self.w[:, k, D:2 * D], start=k == 0, stop=k == KD - 1)
            for hh in range(4):
                for k in range(KD):
                    ins = pe.matmul(self.pt[2 + b % 2][32 * hh:32 * hh + S1, 0:D], self.cT[:, k, b * S + P:(b + 1) * S], self.w[:, k, D:2 * D],
                                    start=k == 0, stop=k == KD - 1)
            ins.then_inc(self.v_made, 1)


def context_queries(nc, io, x_sb, xh, xl, q_hi, q_lo):
    NU = KD * (TOK // 512)
    R = 4
    with ExitStack() as ctx:
        sb = lambda n, s, d=F32: ctx.enter_context(nc.sbuf_tensor(n, s, d))
        sem = lambda n: ctx.enter_context(nc.semaphore(n))
        w32 = sb("q_w_sb", [P, KD, D])
        wh = sb("q_w_hi", [P, KD, D], F32R)
        wl = sb("q_w_lo", [P, KD, D], F32R)
        qb = sb("q_bias", [P, KD])
        qbs = sb("q_bias_scaled", [P, KD])
        pb = sb("proj_bias", [P, D])
        qf = sb("q_full", [P, 2, 512])
        qh = sb("q_hi_sb", [P, R, 512], F32R)
        ql = sb("q_lo_sb", [P, R, 512], F32R)
        pq = [ctx.enter_context(nc.psum_tensor(f"q_p{i}", [P, 512], F32)) for i in range(2)]
        w_loaded, b_loaded, pb_loaded = sem("q_w_loaded"), sem("q_b_loaded"), sem("proj_b_loaded")
        w_hi, w_lo, b_scaled = sem("q_w_hi_done"), sem("q_w_lo_done"), sem("q_b_scaled")
        q_made, q_full, h_done, l_done = sem("q_product"), sem("q_full_done"), sem("q_hi_cut"), sem("q_lo_cut")
        h_stored = [sem(f"q_hi_stored{i}") for i in range(R)]
        l_stored = [sem(f"q_lo_stored{i}") for i in range(R)]
        biased = sem("x_biased")
        with nc.Block() as block:
            @block.sync
            def _(sp):
                sp.dma_start(w32[:, :, :], io["L1_xattn_q_w"].rearrange("(k p) n -> p k n", p=P)).then_inc(w_loaded, 16)
                sp.dma_start(qb[:, :], io["L1_xattn_q_b"].rearrange("(k p) -> p k", p=P), allow_slow_non_contiguous=True).then_inc(b_loaded, 16)
                sp.dma_start(pb[:, :], io["L1_xattn_proj_b"].rearrange("(o e) -> o e", o=1).broadcast_to([P, D])).then_inc(pb_loaded, 16)
                for n in range(NU):
                    G, c = n // KD, n % KD
                    dst = (slice(c * P, (c + 1) * P), slice(G * 512, (G + 1) * 512))
                    sp.wait_ge(h_done, n + 1)
                    sp.dma_start(q_hi[dst], qh[:, n % R, :].bitcast(F32)).then_inc(h_stored[n % R], 16)
                    sp.wait_ge(l_done, n + 1)
                    sp.dma_start(q_lo[dst], ql[:, n % R, :].bitcast(F32)).then_inc(l_stored[n % R], 16)
                for i in range(R):
                    sp.wait_ge(h_stored[i], 16 * (NU // R))
                    sp.wait_ge(l_stored[i], 16 * (NU // R))

            @block.gpsimd
            def _(pool):
                pool.wait_ge(pb_loaded, 16)
                pool.tensor_tensor(x_sb[:, :, :], x_sb[:, :, :], pb[:, :].rearrange("p (o d) -> p o d", o=1).broadcast_to([P, TT, D]),
                                   ALU.add).then_inc(biased, 1)
                pool.wait_ge(biased, 1)

            @block.scalar
            def _(act):
                act.wait_ge(w_loaded, 16)
                act.activation(wh[:, :, :], w32[:, :, :], ACT.Copy).then_inc(w_hi, 1)
                act.wait_ge(b_loaded, 16)
                act.activation(qbs[:, :], qb[:, :], ACT.Copy, scale=HD1 ** -0.5).then_inc(b_scaled, 1)
                act.wait_ge(b_scaled, 1)
                for n in range(NU):
                    act.wait_ge(q_made, n + 1)
                    if n >= 2:
                        act.wait_ge(l_done, n - 1)
                    act.activation(qf[:, n % 2, :], pq[n % 2][:, :], ACT.Identity, bias=qbs[:, n % KD:n % KD + 1],
                                   scale=HD1 ** -0.5).then_inc(q_full, 1)
                    act.wait_ge(q_full, n + 1)
                    if n >= R:
                        act.wait_ge(h_stored[n % R], 16 * (n // R))
                    act.activation(qh[:, n % R, :], qf[:, n % 2, :], ACT.Copy).then_inc(h_done, 1)

            @block.vector
            def _(dve):
                dve.wait_ge(w_hi, 1)
                dve.tensor_tensor(wl[:, :, :], w32[:, :, :], wh[:, :, :].bitcast(F32), ALU.subtract).then_inc(w_lo, 1)
                for n in range(NU):
                    dve.wait_ge(h_done, n + 1)
                    if n >= R:
                        dve.wait_ge(l_stored[n % R], 16 * (n // R))
                    dve.tensor_tensor(ql[:, n % R, :], qf[:, n % 2, :], qh[:, n % R, :].bitcast(F32), ALU.subtract).then_inc(l_done, 1)

            @block.tensor
            def _(pe):
                pe.wait_ge(w_hi, 1)
                pe.wait_ge(w_lo, 1)
                for n in range(NU):
                    if n >= 2:
                        pe.wait_ge(q_full, n - 1)
                    G, c = n // KD, n % KD
                    x = slice(G * 512, (G + 1) * 512)
                    w = slice(c * P, (c + 1) * P)
                    for k in range(KD):
                        ins = matmul3(pe, pq[n % 2][:, :], wh[:, k, w], wl[:, k, w], xh[:, k, x], xl[:, k, x], k == 0, k == KD - 1)
                    ins.then_inc(q_made, 1)


def context_attention(nc, io, x_sb, ident, q_hi, q_lo, ks, vm, vt):
    NG = TOK // 512
    with ExitStack() as ctx:
        sb = lambda n, s, d=F32: ctx.enter_context(nc.sbuf_tensor(n, s, d))
        sem = lambda n: ctx.enter_context(nc.semaphore(n))
        pw = sb("proj_w_rows", [P, 2, D])
        vs = sb("c_values", [P, 2, 16, 32])
        vts = sb("c_rest_values", [P, 2, GRP, P])
        qs = sb("q_stack", [97, 2, 8, 512], F32R)
        exps_sb = sb("c_exps", [P, 4, 4, S])
        probs = sb("c_probs", [P, 2, 4, 4, P])
        rest = sb("c_rest_probs", [P, 2, 4, 4, 32])
        sums = sb("c_sums", [P, 2, 16])
        neg = sb("c_neg_max", [P, 2, 16])
        rec = sb("c_recip", [P, 2, 16])
        pT = sb("c_probsT", [P, 5, 512])
        oT = sb("c_outT", [P, 2, 512])
        st = [ctx.enter_context(nc.psum_tensor(f"c_s{i}", [P, 2, 512], F32)) for i in range(2)]
        tb = [ctx.enter_context(nc.psum_tensor(f"c_t{i}", [P, 512], F32)) for i in range(2)]
        ob = ctx.enter_context(nc.psum_tensor("c_o", [P, 512], F32))
        mb = ctx.enter_context(nc.psum_tensor("c_m", [P, 512], F32))
        loaded, zeroed = sem("c_loaded"), sem("c_zeroed")
        q_loaded = [sem(f"c_q_loaded{i}") for i in range(2)]
        v_placed = sem("c_v_placed")
        scores, maxed, exped = sem("c_scores"), sem("c_maxed"), sem("c_exped")
        recips, scaled = sem("c_recips"), sem("c_scaled")
        t_made = sem("c_turned")
        t_act, t_dve = sem("c_pT_act"), sem("c_pT_dve")
        o_made, o_done = sem("c_o_made"), sem("c_o_done")
        y_made, y_added = sem("c_y_made"), sem("c_y_added")
        BANKS = 5
        ON_ACT = {0: 0, 2: 1, 4: 2}
        ON_DVE = {1: 0, 3: 1}

        def bank(g, j):
            return tb[(g * BANKS + j) % 2]

        def wait_copied(eng, s, j):
            if j in ON_ACT:
                eng.wait_ge(t_act, s * 3 + (ON_ACT[j] + 1))
            else:
                eng.wait_ge(t_dve, s * 2 + (ON_DVE[j] + 1))

        with nc.Block() as block:
            @block.sync
            def _(sp):
                for j in range(4):
                    for u in range(2):
                        r = 32 * j + 16 * u
                        sp.dma_start(pw[r:r + HD1, :, :],
                                     io["L1_xattn_proj_w"].rearrange("(c u j d) n -> j u d c n", c=2, u=2, j=4)[j, u]).then_inc(loaded, 16)
                hi = q_hi.rearrange("(pr r) n -> r pr n", r=32)
                lo = q_lo.rearrange("(pr r) n -> r pr n", r=32)

                def load(i, par, first):
                    G = i * 2 + par
                    if not first:
                        sp.wait_ge(scores, G * 16 - 16)
                    for j, src in enumerate((hi, lo, hi)):
                        sp.dma_start(qs[j * 32:(j + 1) * 32, par, :, :].bitcast(F32), src[:, :, bass.ds(G * 512, 512)]).then_inc(q_loaded[par], 16)

                load(0, 0, True)
                load(0, 1, True)
                with sp.Fori(1, NG // 2) as i:
                    load(i, 0, False)
                    load(i, 1, False)

            @block.gpsimd
            def _(pool):
                pool.memset(qs[96:97, :, :, :].bitcast(F32), 1.0).then_inc(zeroed, 1)
                pool.wait_ge(zeroed, 1)
                pool.memset(rest[:, :, :, :, :], 0.0).then_inc(zeroed, 1)

                for G in range(NG):
                    if G >= 2:
                        pool.wait_ge(v_placed, 2 * G - 2)
                        pool.wait_ge(o_made, 2 * G - 2)
                    pool.tensor_copy(vs[:, G % 2], vm[:, G // 2]).then_inc(v_placed, 1)
                    pool.tensor_copy(vts[:, G % 2], vt[:, G // 2]).then_inc(v_placed, 1)

            @block.scalar
            def _(act):
                def exps(s, n, par):
                    act.wait_ge(maxed, s * 4 + (n + 1))
                    for h in range(4):
                        col = slice(n * 4 + h, n * 4 + h + 1)
                        ins = act.activation(exps_sb[:, n, h, :], st[n % 2][:, h // 2, (h % 2) * S:(h % 2 + 1) * S], ACT.Exp,
                                             bias=neg[:, par, col], accum_out=sums[:, par, col])
                    ins.then_inc(exped, 1)

                def copy_pT(s, g, j):
                    act.wait_ge(t_made, s * BANKS + (j + 1))
                    act.activation(pT[:, j, :], bank(g, j)[:, :], ACT.Copy).then_inc(t_act, 1)

                def copy_out(G, c):
                    act.wait_ge(o_made, G * 2 + (c + 1))
                    act.activation(oT[:, c, :], ob[:, :], ACT.Copy).then_inc(o_done, 1)

                def round_(i, par, first, last):
                    G = i * 2 + par
                    for g in range(GRP):
                        s = G * GRP + g
                        more = not (last and g == GRP - 1)
                        copy_pT(s, g, 0)
                        if more:
                            exps(s + 1, 0, 1 - g % 2)
                        if g == 2:
                            copy_out(G, 0)
                        if g == 0 and not first:
                            copy_out(G - 1, 1)
                        if more:
                            exps(s + 1, 1, 1 - g % 2)
                        copy_pT(s, g, 2)
                        if more:
                            exps(s + 1, 2, 1 - g % 2)
                            exps(s + 1, 3, 1 - g % 2)
                        copy_pT(s, g, 4)

                for n in range(4):
                    exps(0, n, 0)
                round_(0, 0, True, False)
                round_(0, 1, False, False)
                with act.Fori(1, NG // 2 - 1) as i:
                    round_(i, 0, False, False)
                    round_(i, 1, False, False)
                round_(NG // 2 - 1, 0, False, False)
                round_(NG // 2 - 1, 1, False, True)
                copy_out(NG - 1, 1)

            @block.vector
            def _(dve):
                def top(s, n, par):
                    dve.wait_ge(scores, s * 4 + (n + 1))
                    dve.tensor_reduce(neg[:, par, n * 4:n * 4 + 4], st[n % 2][:, :, 0:2 * S].rearrange("p q (h s) -> p q h s", h=2),
                                      AX.X, ALU.max, negate=True).then_inc(maxed, 1)

                def scale(s, n, par):
                    dve.wait_ge(exped, s * 4 + (n + 1))
                    c = slice(n * 4, n * 4 + 4)
                    dve.reciprocal(rec[:, par, c], sums[:, par, c]).then_inc(recips, 1)
                    dve.wait_ge(recips, s * 4 + (n + 1))
                    by = rec[:, par, c].rearrange("p (h s) -> p h s", s=1)
                    dve.tensor_tensor(probs[:, par, n], exps_sb[:, n, :, 0:P], by.broadcast_to([P, 4, P]), ALU.mult)
                    dve.tensor_tensor(rest[:, par, n, :, 0:S1], exps_sb[:, n, :, P:S], by.broadcast_to([P, 4, S1]), ALU.mult).then_inc(scaled, 1)

                def copy_pT(s, g, j):
                    dve.wait_ge(t_made, s * BANKS + (j + 1))
                    dve.tensor_copy(pT[:, j, :], bank(g, j)[:, :]).then_inc(t_dve, 1)

                def add(G, j):
                    dve.wait_ge(y_made, G * 2 + (j + 1))
                    dst = x_sb[:, bass.ds(G * 4 + 2 * j, 2), :]
                    dve.tensor_tensor(dst, dst, mb[:, :].rearrange("p (t d) -> p t d", d=D), ALU.add).then_inc(y_added, 1)

                def round_(i, par, first, last):
                    G = i * 2 + par
                    for g in range(GRP):
                        s = G * GRP + g
                        more = not (last and g == GRP - 1)
                        late = g == 0 and not first
                        o = 1 - g % 2
                        if more:
                            top(s + 1, 1, o)
                        copy_pT(s, g, 1)
                        if more:
                            scale(s + 1, 0, o)
                            top(s + 1, 2, o)
                            scale(s + 1, 1, o)
                            top(s + 1, 3, o)
                        copy_pT(s, g, 3)
                        if more:
                            scale(s + 1, 2, o)
                        if late:
                            add(G - 1, 0)
                        if more:
                            scale(s + 1, 3, o)
                        if late:
                            add(G - 1, 1)
                        if not (last and g >= GRP - 2):
                            top(s + 2, 0, g % 2)

                dve.wait_ge(zeroed, 2)
                top(0, 0, 0)
                for n in range(1, 4):
                    top(0, n, 0)
                    scale(0, n - 1, 0)
                scale(0, 3, 0)
                top(1, 0, 1)
                round_(0, 0, True, False)
                round_(0, 1, False, False)
                with dve.Fori(1, NG // 2 - 1) as i:
                    round_(i, 0, False, False)
                    round_(i, 1, False, False)
                round_(NG // 2 - 1, 0, False, False)
                round_(NG // 2 - 1, 1, False, True)
                add(NG - 1, 0)
                add(NG - 1, 1)

            @block.tensor
            def _(pe):
                def score(i, par, g, n, first=False):
                    s = (i * 2 + par) * GRP + g
                    if n == 0 and g == 0:
                        pe.wait_ge(q_loaded[par], i * 48 + 48)
                    if not first or n >= 2:
                        pe.wait_ge(exped, s * 4 + (n - 1))
                    for q in range(2):
                        pair = g * 2 + q
                        k = ks[:, bass.ds(i, 1), pair, :, :].rearrange("p b h s -> p (b h s)")
                        ins = pe.matmul(st[n % 2][:, q, 0:2 * S], qs[:, par, pair, n * P:(n + 1) * P], k, start=True, stop=True)
                    ins.then_inc(scores, 1)

                def turn(s, g, j, first=False):
                    if j == 0:
                        pe.wait_ge(scaled, s * 4 + 4)
                    if j >= 2:
                        wait_copied(pe, s, j - 2)
                    elif not first:
                        wait_copied(pe, s - 1, 3 + j)
                    for n in range(4):
                        if j < 4:
                            ins = pe.transpose(bank(g, j)[:, n * P:(n + 1) * P], probs[:, g % 2, n, j, :], ident[:, :])
                        else:
                            ins = pe.transpose(bank(g, j)[:, n * P:(n + 1) * P], rest[:, g % 2, n].rearrange("p h s -> p (h s)"), ident[:, :])
                    ins.then_inc(t_made, 1)

                def weigh(G, par, g, j, first=False):
                    s = G * GRP + g
                    if j == 0 and g == 0:
                        pe.wait_ge(v_placed, G * 2 + 2)
                    if j == 0 and g % 2 == 0 and not first:
                        pe.wait_ge(o_done, G * 2 + g // 2)
                    wait_copied(pe, s, j)
                    even = g % 2 == 0
                    if j < 4:
                        pe.matmul(ob[32 * j:32 * (j + 1), :], vs[:, par, g * 4 + j, :], pT[:, j, :], start=even, stop=False,
                                  skip_group_check=True)
                    else:
                        ins = pe.matmul(ob[:, :], vts[:, par, g, :], pT[:, 4, :], start=False, stop=not even, skip_group_check=True)
                        if not even:
                            ins.then_inc(o_made, 1)

                def project(G, j):
                    if j == 0:
                        pe.wait_ge(o_done, G * 2 + 2)
                    if j or not (isinstance(G, int) and G == 0):
                        pe.wait_ge(y_added, G * 2 + j)
                    for t in range(2):
                        rows = slice((2 * j + t) * P, (2 * j + t + 1) * P)
                        for c in range(2):
                            ins = pe.matmul(mb[:, t * D:(t + 1) * D], oT[:, c, rows], pw[:, c, :], start=c == 0, stop=c == 1)
                    ins.then_inc(y_made, 1)

                def round_(i, par, first, last):
                    G = i * 2 + par
                    for g in range(GRP):
                        s = G * GRP + g
                        start = first and g == 0
                        late = g == 0 and not first

                        def coming_score(ahead, n):
                            if g + ahead < GRP:
                                score(i, par, g + ahead, n)
                            elif not last:
                                score(i + par, 1 - par, g + ahead - GRP, n)

                        turn(s, g, 0, start)
                        coming_score(1, 1)
                        turn(s, g, 1, start)
                        if g:
                            weigh(G, par, g - 1, 4)
                        elif not first:
                            weigh(G - 1, 1 - par, GRP - 1, 4)
                        coming_score(1, 2)
                        turn(s, g, 2)
                        coming_score(1, 3)
                        turn(s, g, 3)
                        weigh(G, par, g, 0, start)
                        weigh(G, par, g, 1)
                        if late:
                            project(G - 1, 0)
                        coming_score(2, 0)
                        turn(s, g, 4)
                        weigh(G, par, g, 2)
                        weigh(G, par, g, 3)
                        if late:
                            project(G - 1, 1)

                pe.wait_ge(zeroed, 2)
                for n in range(4):
                    score(0, 0, 0, n, True)
                score(0, 0, 1, 0)
                pe.wait_ge(loaded, 16 * 8)
                round_(0, 0, True, False)
                round_(0, 1, False, False)
                with pe.Fori(1, NG // 2 - 1) as i:
                    round_(i, 0, False, False)
                    round_(i, 1, False, False)
                round_(NG // 2 - 1, 0, False, False)
                round_(NG // 2 - 1, 1, False, True)
                weigh(NG - 1, 1, GRP - 1, 4)
                project(NG - 1, 0)
                project(NG - 1, 1)


E1, H1, CAP1 = 8, 512, TOK // 8
T1 = -(-(TOK + E1 * (P - 1)) // P)
T1 = -(-T1 // 4) * 4
SLOTS1 = T1 * P


def route1(nc, io, cst, logits, r, tile_expert, ws):
    with ExitStack() as c1:
        sb = lambda n, s, d=F32: c1.enter_context(nc.sbuf_tensor(n, s, d))
        sem = lambda n: c1.enter_context(nc.semaphore(n))
        pr = sb("r1_probs", [P, TT, E1])
        key = sb("r1_key", [P, E1, TT])
        chosen = sb("r1_chosen", [P, E1, TT])
        rank = sb("r1_rank", [P, E1, TT])
        over_e = lambda t: t.rearrange("p (t e) -> p t e", e=1).broadcast_to([P, TT, E1])
        flat = lambda t: t[:, :, :].rearrange("p a b -> p (a b)")
        te = lambda t: t[:, :, :].rearrange("p e t -> p t e")
        W = E1 * TT
        with ExitStack() as c2:
            m = c2.enter_context(nc.sbuf_tensor("r1_max", [P, TT], F32))
            step_s, exped = (c2.enter_context(nc.semaphore(n)) for n in ("r1_step", "r1_exp"))
            with nc.Block() as block:
                @block.vector
                def _(dve):
                    step = Steps(dve, step_s)
                    step.then(dve.tensor_reduce(m[:, :], logits[:, :, :], AX.X, ALU.max))
                    step.then(dve.tensor_tensor(pr[:, :, :], logits[:, :, :], over_e(m[:, :]), ALU.subtract))
                    dve.wait_ge(exped, 1)
                    step.then(dve.tensor_reduce(m[:, :], pr[:, :, :], AX.X, ALU.add))
                    step.then(dve.reciprocal(m[:, :], m[:, :]))
                    step.then(dve.tensor_tensor(pr[:, :, :], pr[:, :, :], over_e(m[:, :]), ALU.mult))
                    step.then(dve.tensor_copy(te(key), pr[:, :, :]))

                @block.scalar
                def _(act):
                    act.wait_ge(step_s, 2)
                    act.activation(pr[:, :, :], pr[:, :, :], ACT.Exp).then_inc(exped, 1)

        th = Threshold(nc, c1, cst, key, E1, CAP1, "r1_", probabilities=True)
        search(nc, th, "r1_", ws)
        take(nc, cst, th, key, E1, CAP1, chosen, rank, "r1_")
        with ExitStack() as c2:
            sb2 = lambda n, s, d=F32: c2.enter_context(nc.sbuf_tensor(n, s, d))
            v = sb2("r1_value", [P, TT, E1])
            eq = sb2("r1_is_max", [P, TT, E1])
            pre = sb2("r1_prefix", [P, TT, E1])
            one = sb2("r1_one_hot", [P, E1, TT])
            m = sb2("r1_max2", [P, TT])
            count = sb2("r1_count", [P, E1])
            ci = sb2("r1_count_i", [P, E1], I32)
            upto = sb2("r1_tiles_upto", [P, E1])
            base = sb2("r1_base", [P, E1])
            past = sb2("r1_past", [P, T1, E1])
            tf = sb2("r1_tile_f", [P, T1])
            row = sb2("r1_slot_row", [P, TT], I32)
            pq = [c2.enter_context(nc.psum_tensor(f"r1_p{i}", [P, 512], F32)) for i in range(3)]
            step_s, summed = (c2.enter_context(nc.semaphore(n)) for n in ("r1_slots_step", "r1_summed"))
            with nc.Block() as block:
                @block.vector
                def _(dve):
                    step = Steps(dve, step_s)
                    step.then(dve.tensor_reduce(m[:, :], te(chosen), AX.X, ALU.max))
                    step.then(dve.tensor_tensor(v[:, :, :], over_e(m[:, :]), te(chosen), ALU.subtract))
                    step.then(dve.scalar_tensor_tensor(out=v[:, :, :], in0=v[:, :, :], scalar=-4.0, in1=pr[:, :, :], op0=ALU.mult, op1=ALU.add))
                    step.then(dve.tensor_reduce(m[:, :], v[:, :, :], AX.X, ALU.max))
                    step.then(dve.tensor_tensor(eq[:, :, :], v[:, :, :], over_e(m[:, :]), ALU.is_equal))
                    step.then(dve.tensor_tensor_scan(flat(pre), cst["keep_8"][:, 0:W], flat(eq), 0.0, ALU.mult, ALU.add))
                    step.then(dve.tensor_scalar(pre[:, :, :], pre[:, :, :], 1.0, None, ALU.is_equal))
                    step.then(dve.tensor_tensor(te(one), pre[:, :, :], eq[:, :, :], ALU.mult))
                    step.then(dve.tensor_reduce(count[:, :], one[:, :, :], AX.X, ALU.add))
                    step.then(dve.tensor_tensor(v[:, :, :], te(one), pr[:, :, :], ALU.mult))
                    step.then(dve.tensor_reduce(r["weight"][:, 0, :], v[:, :, :], AX.X, ALU.add))
                    dve.wait_ge(summed, 1)
                    step.then(dve.tensor_copy(ci[:, :], pq[0][:, 0:E1]))
                    step.then(dve.tensor_scalar(ci[:, :], ci[:, :], P - 1, None, ALU.add))
                    step.then(dve.tensor_scalar(ci[:, :], ci[:, :], P.bit_length() - 1, None, ALU.logical_shift_right))
                    step.then(dve.tensor_copy(count[:, :], ci[:, :]))
                    step.then(dve.tensor_tensor_scan(upto[:, :], cst["ones"][:, 0:E1], count[:, :], 0.0, ALU.mult, ALU.add))
                    step.then(dve.tensor_tensor(base[:, :], upto[:, :], count[:, :], ALU.subtract))
                    step.then(dve.tensor_scalar(base[:, :], base[:, :], float(P), None, ALU.mult))
                    step.then(dve.tensor_tensor(past[:, :, :], cst["tile_no"][:, 0:T1].rearrange("p (t e) -> p t e", e=1).broadcast_to([P, T1, E1]),
                                                upto[:, :].rearrange("p (t e) -> p t e", t=1).broadcast_to([P, T1, E1]), ALU.is_ge))
                    step.then(dve.tensor_reduce(tf[:, :], past[:, :, :], AX.X, ALU.add))
                    step.then(dve.tensor_scalar(tf[:, :], tf[:, :], float(E1 - 1), None, ALU.min))
                    step.then(dve.tensor_copy(tile_expert[:, :], tf[:, :]))
                    step.then(dve.tensor_copy(chosen[:, :, :], pq[2][:, 0:W].rearrange("p (e t) -> p e t", t=TT)))
                    step.then(dve.tensor_tensor_scan(flat(rank), cst["keep"][:, 0:W], flat(chosen), 0.0, ALU.mult, ALU.add))
                    step.then(dve.tensor_tensor(rank[:, :, :], rank[:, :, :], chosen[:, :, :], ALU.subtract))
                    step.then(dve.tensor_tensor(rank[:, :, :], rank[:, :, :], pq[1][:, 0:W].rearrange("p (e t) -> p e t", t=TT), ALU.add))
                    step.then(dve.tensor_tensor(rank[:, :, :], rank[:, :, :], base[:, :].rearrange("p (e t) -> p e t", t=1).broadcast_to([P, E1, TT]), ALU.add))
                    step.then(dve.tensor_tensor(rank[:, :, :], rank[:, :, :], one[:, :, :], ALU.mult))
                    step.then(dve.tensor_reduce(m[:, :], te(rank), AX.X, ALU.add))
                    slot, scatter = r["slot"][:, 0, :], r["scatter"][:, 0, :]
                    step.then(dve.tensor_copy(slot, m[:, :]))
                    step.then(dve.tensor_scalar(row[:, :], slot, P - 1, None, ALU.bitwise_and))
                    step.then(dve.tensor_scalar(row[:, :], row[:, :], T1, None, ALU.mult))
                    step.then(dve.tensor_scalar(scatter, slot, P.bit_length() - 1, None, ALU.logical_shift_right))
                    step.then(dve.tensor_tensor(scatter, scatter, row[:, :], ALU.add))

                @block.tensor
                def _(pe):
                    pe.wait_ge(step_s, 9)
                    pe.matmul(pq[0][:, 0:E1], cst["ones"][:, :], count[:, :], start=True, stop=True)
                    pe.matmul(pq[1][:, 0:W], cst["before"][:, :], flat(one), start=True, stop=True)
                    pe.matmul(pq[2][:, 0:W], cst["ones"][:, :], flat(one), start=True, stop=True).then_inc(summed, 1)


class ResidentWeights:

    def __init__(self, nc, ctx, io):
        sb = lambda n, s, d=F32: ctx.enter_context(nc.sbuf_tensor(n, s, d))
        sem = lambda n: ctx.enter_context(nc.semaphore(n))
        self.io = io
        self.hi = [sb(f"w{j + 1}_hi", [P, E1 * 1024], F32R) for j in range(2)]
        self.lo = [sb(f"w{j + 1}_lo", [P, E1 * 1024], F32R) for j in range(2)]
        self.stage = sb("w_stage", [P, 2, 1024])
        self.loaded = [sem(f"rw_loaded{j}") for j in range(2)]
        self.hi_done, self.lo_done = sem("rw_hi_done"), sem("rw_lo_done")

    def load(self, sp):
        for n in range(2 * E1):
            e, j = n // 2, n % 2
            src = self.io[("L1_ffn_W1", "L1_ffn_W2")[j]][e].rearrange("(c p) h -> p c h", p=P)
            if n >= 2:
                sp.wait_ge(self.lo_done, n - 1)
            sp.dma_start(self.stage[:, j, :].rearrange("p (c h) -> p c h", h=src.shape[2]), src).then_inc(self.loaded[j], 16)

    def high(self, act):
        for n in range(2 * E1):
            e, j = n // 2, n % 2
            act.wait_ge(self.loaded[j], 16 * e + 16)
            act.activation(self.hi[j][:, e * 1024:(e + 1) * 1024], self.stage[:, j, :], ACT.Copy).then_inc(self.hi_done, 1)

    def low(self, pool):
        for n in range(2 * E1):
            e, j = n // 2, n % 2
            c = slice(e * 1024, (e + 1) * 1024)
            pool.wait_ge(self.hi_done, n + 1)
            pool.tensor_tensor(self.lo[j][:, c], self.stage[:, j, :], self.hi[j][:, c].bitcast(F32), ALU.subtract).then_inc(self.lo_done, 1)


def sorted_experts(nc, io, ident, cst, xn_rows, table, y_rows, r, tile_expert, ws, sw):
    R = 4
    with ExitStack() as ctx:
        sb = lambda n, s, d=F32: ctx.enter_context(nc.sbuf_tensor(n, s, d))
        sem = lambda n: ctx.enter_context(nc.semaphore(n))
        ids = sb("s_ids", [P, T1], I32)
        xr = sb("s_rows", [P, R, D])
        xh = sb("s_x_hi", [P, 2, KD, P], F32R)
        xl = sb("s_x_lo", [P, 2, KD, P], F32R)
        ge = sb("s_gelu", [P, 2, H1])
        gh = sb("s_g_hi", [P, 2, H1], F32R)
        gl = sb("s_g_lo", [P, 2, H1], F32R)
        ys = sb("s_y", [P, R, D])
        xb, yb, hb, tb = ([ctx.enter_context(nc.psum_tensor(f"s_{n}{i}", [P, 512], F32)) for i in range(2)] for n in ("x", "y", "h", "t"))
        zeroed, scattered, read = sw[0:3]
        gathered = sw[3:3 + R]
        stored = [sem(f"s_stored{i}") for i in range(R)]
        x_turned, x_hi, x_lo = sem("s_x_turned"), sem("s_x_hi_done"), sem("s_x_lo_done")
        h_made, gelu = sem("s_h_made"), sem("s_gelu_done")
        g_turned, g_hi, g_lo = sem("s_g_turned"), sem("s_g_hi_done"), sem("s_g_lo_done")
        y_made, y_copied = sem("s_y_made"), sem("s_y_copied")

        def exists(j):
            return not isinstance(j, int) or 0 <= j < T1

        def all_steps(eng, step):
            for j in range(-2, 2 * R):
                step(j, j % R)
            with eng.Fori(2, T1 // R - 1) as i:
                for p in range(R):
                    step(i * R + p, p)
            for j in range(T1 - R, T1 + 1):
                step(j, j % R)

        with nc.Block() as block:
            @block.gpsimd
            def _(pool):
                pool.dma_start(table.rearrange("(p c) o -> p (c o)", p=P), cst["zero"][:, 0:T1]).then_inc(zeroed, 16)
                pool.wait_ge(zeroed, 16)
                for t in range(TT):
                    pool.indirect_dma_start(out=table, out_offset=bass.IndirectOffsetOnAxis(ap=r["scatter"][:, 0, t:t + 1].bitcast(U32), axis=0),
                                            in_=cst["token"][:, t:t + 1], in_offset=None).then_inc(scattered, 16)
                pool.wait_ge(scattered, 16 * TT)
                pool.dma_start(ids[:, :], table.rearrange("(p j) o -> p (j o)", p=P)).then_inc(read, 16)
                pool.wait_ge(read, 16)
                for j in range(T1):
                    if j >= R:
                        pool.wait_ge(x_turned, j - R + 1)
                    pool.indirect_dma_start(out=xr[:, j % R, :], out_offset=None, in_=xn_rows,
                                            in_offset=bass.IndirectOffsetOnAxis(ap=ids[:, j:j + 1].bitcast(U32), axis=0)).then_inc(gathered[j % R], 16)

            @block.sync
            def _(sp):
                y_t = y_rows.rearrange("(j p) d -> p j d", p=P)

                def put(i, p):
                    j = i * R + p
                    sp.wait_ge(y_copied, j + 1)
                    sp.dma_start(y_t[:, bass.ds(j, 1), :], ys[:, p:p + 1, :]).then_inc(stored[p], 16)

                with sp.Fori(0, T1 // R) as i:
                    for p in range(R):
                        put(i, p)
                for p in range(R):
                    sp.wait_ge(stored[p], 16 * (T1 // R))

            @block.scalar
            def _(act):
                def step(j, p):
                    if exists(j + 1):
                        act.wait_ge(h_made, j + 2)
                        if due(j):
                            act.wait_ge(g_turned, j)
                        act.activation(ge[:, (p + 1) % 2, :], hb[(p + 1) % 2][:, :], ACT.Gelu).then_inc(gelu, 1)
                    if exists(j):
                        act.wait_ge(g_turned, j + 1)
                        if due(j - 1):
                            act.wait_ge(y_made, j - 1)
                        act.activation(gh[:, p % 2, :], tb[p % 2][:, :], ACT.Copy).then_inc(g_hi, 1)
                    if exists(j + 2):
                        act.wait_ge(x_turned, j + 3)
                        if due(j + 1):
                            act.wait_ge(h_made, j + 1)
                        act.activation(xh[:, p % 2].rearrange("p k c -> p (k c)"), xb[p % 2][:, 0:D], ACT.Copy).then_inc(x_hi, 1)

                all_steps(act, step)

            @block.vector
            def _(dve):
                def step(j, p):
                    if exists(j):
                        dve.wait_ge(g_hi, j + 1)
                        dve.tensor_tensor(gl[:, p % 2, :], tb[p % 2][:, :], gh[:, p % 2, :].bitcast(F32), ALU.subtract).then_inc(g_lo, 1)
                    if exists(j + 2):
                        dve.wait_ge(x_hi, j + 3)
                        dve.tensor_tensor(xl[:, p % 2].rearrange("p k c -> p (k c)"), xb[p % 2][:, 0:D],
                                          xh[:, p % 2].rearrange("p k c -> p (k c)").bitcast(F32), ALU.subtract).then_inc(x_lo, 1)
                    if exists(j - 1):
                        q = (p - 1) % R
                        dve.wait_ge(y_made, j)
                        if not (isinstance(j, int) and j - 1 < R):
                            dve.wait_ge(stored[q], (j - 1 - q) * (16 // R))
                        dve.tensor_copy(ys[:, q, :], yb[q % 2][:, 0:D]).then_inc(y_copied, 1)

                all_steps(dve, step)

            @block.tensor
            def _(pe):
                def hidden(j, p):
                    e = pe.value_load(tile_expert[0:1, bass.ds(j, 1)], min_val=0, max_val=E1 - 1)
                    pe.wait_ge(x_hi, j + 1)
                    pe.wait_ge(x_lo, j + 1)
                    if due(j - 1):
                        pe.wait_ge(gelu, j - 1)
                    for k in range(KD):
                        w = bass.ds(e * 1024 + k * H1, H1)
                        x = (xh[:, p % 2, k, :], xl[:, p % 2, k, :])
                        pe.matmul(hb[p % 2][:, :], x[0], ws.hi[0][:, w], start=k == 0, stop=False)
                        pe.matmul(hb[p % 2][:, :], x[0], ws.lo[0][:, w], start=False, stop=False)
                        ins = pe.matmul(hb[p % 2][:, :], x[1], ws.hi[0][:, w], start=False, stop=k == KD - 1)
                    ins.then_inc(h_made, 1)

                def turn_hidden(j, p):
                    pe.wait_ge(gelu, j + 1)
                    if due(j - 1):
                        pe.wait_ge(g_hi, j - 1)
                        pe.wait_ge(g_lo, j - 1)
                    for m in range(HC):
                        c = slice(m * P, (m + 1) * P)
                        ins = pe.transpose(tb[p % 2][:, c], ge[:, p % 2, c], ident[:, :])
                    ins.then_inc(g_turned, 1)

                def turn_rows(j, p):
                    pe.wait_ge(gathered[p], (j - p) * (16 // R) + 16)
                    if due(j - 1):
                        pe.wait_ge(x_hi, j - 1)
                        pe.wait_ge(x_lo, j - 1)
                    for k in range(KD):
                        ins = pe.transpose(xb[p % 2][:, k * P:(k + 1) * P], xr[:, p, k * P:(k + 1) * P], ident[:, :])
                    ins.then_inc(x_turned, 1)

                def back(j, p):
                    e = pe.value_load(tile_expert[0:1, bass.ds(j, 1)], min_val=0, max_val=E1 - 1)
                    pe.wait_ge(g_hi, j + 1)
                    pe.wait_ge(g_lo, j + 1)
                    if due(j - 1):
                        pe.wait_ge(y_copied, j - 1)
                    out = yb[p % 2][:, 0:D]
                    for m in range(HC):
                        w = bass.ds(e * 1024 + m * D, D)
                        g = (gh[:, p % 2, m * P:(m + 1) * P], gl[:, p % 2, m * P:(m + 1) * P])
                        pe.matmul(out, g[0], ws.hi[1][:, w], start=m == 0, stop=False)
                        pe.matmul(out, g[0], ws.lo[1][:, w], start=False, stop=False)
                        ins = pe.matmul(out, g[1], ws.hi[1][:, w], start=False, stop=m == HC - 1)
                    ins.then_inc(y_made, 1)

                def step(j, p):
                    if exists(j + 1):
                        hidden(j + 1, (p + 1) % R)
                    if exists(j):
                        turn_hidden(j, p)
                    if exists(j + 2):
                        turn_rows(j + 2, (p + 2) % R)
                    if exists(j - 1):
                        back(j - 1, (p - 1) % R)

                all_steps(pe, step)



def clear_semaphores(nc):
    free = sorted(nc.released_uncleared_semaphores)
    starts = [n for n in free if n - 1 not in free]
    ends = [n + 1 for n in free if n + 1 not in free]
    with nc.Block() as block:
        @block.gpsimd
        def _(pool):
            for a, b in zip(starts, ends):
                pool.sem_clear(range(a, b))


def build(nc, io, out):
    with ExitStack() as ctx:
        x_sb = ctx.enter_context(nc.sbuf_tensor("x_sb", [P, TT, D], F32))
        ident = ctx.enter_context(nc.sbuf_tensor("ident", [P, P], F32))
        dram = lambda n, s, d=F32: nc.dram_tensor(n, s, d, kind="Internal").ap()
        with ExitStack() as c2:
            kvT = c2.enter_context(nc.sbuf_tensor("kvT", [P, KD, B * KEYS], F32))
            embed(nc, io, x_sb, ident, kvT)
            latent_attention(nc, io, x_sb, ident, kvT)
        sw0, sw1 = ([ctx.enter_context(nc.semaphore(f"software_dma{layer}_{i}")) for i in range(15)] for layer in range(2))
        cst = constants(nc, ctx)
        xn_rows = dram("xn_rows", [TOK, D])
        y_rows = dram("y_rows", [SLOTS0, D])
        table = dram("slot_token", [SLOTS0, 1], I32)
        q_hi, q_lo = dram("q_hi", [D, TOK]), dram("q_lo", [D, TOK])
        with ExitStack() as c2:
            r = slot_arrays(nc, c2, 2)
            with ExitStack() as c3:
                logits = c3.enter_context(nc.sbuf_tensor("logits", [P, TT, E0], F32))
                ids = c3.enter_context(nc.sbuf_tensor("slot_ids", [P, E0, NT0], I32))
                with ExitStack() as c4:
                    xh, xl = (c4.enter_context(nc.sbuf_tensor(n, [P, KD, TOK], F32R)) for n in ("xT_hi", "xT_lo"))
                    normalise(nc, x_sb, ident, xh, xl, xn_rows, io["L0_ffn_gate_w"], E0, logits)
                    sb = lambda n, s, d=F32: c4.enter_context(nc.sbuf_tensor(n, s, d))
                    ws = SharedWeights(nc, c4, io)
                    first, second = sb("first_expert", [P, TT, E0]), sb("second_expert", [P, TT, E0])
                    key, chosen, rank = (sb(n, [P, E0, TT]) for n in ("router_key", "chosen", "slot_rank"))
                    th = Threshold(nc, c4, cst, key, E0, CAP0, "")
                    route0(nc, io, cst, logits, first, second, key, ws)
                    shared_expert(nc, io, cst, x_sb, xh, xl, ws, 0, th, table, ids, r["scatter"], sw0)
                    take(nc, cst, th, key, E0, CAP0, chosen, rank)
                    slots0(nc, logits, first, second, chosen, rank, r)
                    shared_expert(nc, io, cst, x_sb, xh, xl, ws, 1, th, table, ids, r["scatter"], sw0)
                routed_experts(nc, io, ident, xn_rows, ids, y_rows, sw0)
            clear_semaphores(nc)
            sb = lambda n, s, d=F32: c2.enter_context(nc.sbuf_tensor(n, s, d))
            ks = sb("keys_stack", [97, B, 8, 2, S], F32R)
            vm = sb("values_main", [P, B, 16, 32])
            vt = sb("values_rest", [P, B, GRP, P])
            stats = sb("row_stats", [P, TT, 6])
            with ExitStack() as c3:
                keys = ContextKeys(nc, c3, io, ident, ks, vm, vt)
                combine(nc, x_sb, y_rows, r["slot"], r["weight"], 2, "combine0", sw0, keys, stats)
            with ExitStack() as c3:
                xh, xl = (c3.enter_context(nc.sbuf_tensor(n, [P, KD, TOK], F32R)) for n in ("xT1_hi", "xT1_lo"))
                normalise(nc, x_sb, ident, xh, xl, None, None, 0, None, "c", stats)
                context_queries(nc, io, x_sb, xh, xl, q_hi, q_lo)
            context_attention(nc, io, x_sb, ident, q_hi, q_lo, ks, vm, vt)
        xn_rows, y_rows = dram("xn1_rows", [TOK, D]), dram("y1_rows", [SLOTS1, D])
        table = dram("slot_token1", [SLOTS1, 1], I32)
        with ExitStack() as c2:
            r = slot_arrays(nc, c2, 1, "r1_")
            tile_expert = c2.enter_context(nc.sbuf_tensor("tile_expert", [P, T1], I32))
            with ExitStack() as c3:
                ws = ResidentWeights(nc, c3, io)
                with ExitStack() as c4:
                    logits = c4.enter_context(nc.sbuf_tensor("logits1", [P, TT, E1], F32))
                    with ExitStack() as c5:
                        xh, xl = (c5.enter_context(nc.sbuf_tensor(n, [P, KD, 1024], F32R)) for n in ("xT2_hi", "xT2_lo"))
                        normalise(nc, x_sb, ident, xh, xl, xn_rows, io["L1_ffn_Wg"], E1, logits, "d")
                    route1(nc, io, cst, logits, r, tile_expert, ws)
                sorted_experts(nc, io, ident, cst, xn_rows, table, y_rows, r, tile_expert, ws, sw1)
            combine(nc, x_sb, y_rows, r["slot"], r["weight"], 1, "combine1", sw1, out=out)

INPUTS = (
    "x", "ctx_1024", "mask_BxS2_bk0", "L0_xattn_ln_m_w", "L0_xattn_ln_m_b", "L0_xattn_ln_l_w",
    "L0_xattn_ln_l_b", "L0_xattn_Wq", "L0_xattn_Wkv", "L0_xattn_Wout", "L0_ffn_gate_w", "L0_ffn_gate_b",
    "L0_ffn_ew1", "L0_ffn_ew3", "L0_ffn_ew2", "L0_ffn_sw1", "L0_ffn_sw3", "L0_ffn_sw2", "L1_xattn_q_w",
    "L1_xattn_q_b", "L1_xattn_kv_w", "L1_xattn_kv_b", "L1_xattn_proj_w", "L1_xattn_proj_b", "L1_ffn_Wg",
    "L1_ffn_W1", "L1_ffn_W2")


def kernel(**inputs):
    import concourse.bacc as bacc
    from concourse.bass_utils import run_bass_kernel_spmd

    nc = bacc.Bacc("TRN2", target_bir_lowering=False, num_devices=1)
    arrays, io = {}, {}
    for name in INPUTS:
        a = np.ascontiguousarray(inputs[name])
        arrays[f"in_{name}"] = a
        io[name] = nc.dram_tensor(f"in_{name}", a.shape, mybir.dt.from_np(a.dtype), kind="ExternalInput").ap()
    out = nc.dram_tensor("out_x", (B, N, D), F32, kind="ExternalOutput").ap()
    build(nc, io, out)
    got = run_bass_kernel_spmd(nc, [arrays], core_ids=[0])
    return got.results[0]["out_x"]
```
